# Optimizing a Trainium2 kernel written in Bass

```python
import numpy as np
import jax
import jax.numpy as jnp

def _softmax(x, axis=-1):
    return jax.nn.softmax(x, axis=axis)

def _gelu(x):
    return jax.nn.gelu(x, approximate=True)

def _silu(x):
    return jax.nn.silu(x)

def _sigmoid(x):
    return jax.nn.sigmoid(x)

def _layernorm(x, axis=-1, eps=1e-05):
    m = jnp.mean(x, axis=axis, keepdims=True)
    v = jnp.var(x, axis=axis, keepdims=True)
    return (x - m) / jnp.sqrt(v + eps)

def _scatter_add(tgt, idx, src, axis=0):
    return tgt.at[idx].add(src)

def _segment_sum(src, seg, n):
    return jax.ops.segment_sum(src, seg, n)
kernel_name = 'mk_seq_preln_d1_jaxref_r4_056434'

def setup_inputs(seed: int=0):
    np.random.seed(seed)
    _w = jnp.asarray

    def _L0_attn_setup():
        import jax, jax.numpy as jnp
        import numpy as np
        D = 256
        H = 16
        DK = D // H
        HI = 4
        DI = 64
        K = 128
        B, S = (2, 512)

        def _rope(x):
            d = x.shape[-1]
            s = x.shape[1]
            inv = 1.0 / 10000.0 ** (jnp.arange(0, d, 2, dtype=jnp.float32) / d)
            ang = jnp.arange(s, dtype=jnp.float32)[:, None] * inv
            cos = jnp.cos(ang)[None, :, None, :]
            sin = jnp.sin(ang)[None, :, None, :]
            x1, x2 = (x[..., ::2], x[..., 1::2])
            return jnp.stack([x1 * cos - x2 * sin, x1 * sin + x2 * cos], axis=-1).reshape(x.shape)
        key = jax.random.key(seed)
        ks = jax.random.split(key, 6)
        sc = 0.02
        return {'x': jax.random.normal(ks[0], (B, S, D), jnp.float32), 'w_qkv': jax.random.normal(ks[1], (3 * D, D), jnp.float32) * sc, 'w_o': jax.random.normal(ks[2], (D, D), jnp.float32) * sc, 'w_qi': jax.random.normal(ks[3], (HI * DI, D), jnp.float32) * sc, 'w_ki': jax.random.normal(ks[4], (DI, D), jnp.float32) * sc, 'w_wi': jax.random.normal(ks[5], (HI, D), jnp.float32) * sc}
    _L0_attn_in = _L0_attn_setup()

    def _L0_ffn_setup():
        import jax, jax.numpy as jnp
        import numpy as np
        B, S, DIM = (4, 1024, 256)
        BASE_COUPLING = 0.1
        NUM_CYCLES = 3

        def _gelu(x):
            return jax.nn.gelu(x, approximate=False)

        def _coupling_net(h, w1, b1, w2, b2, w3, b3, w4, b4):
            h = _gelu(h @ w1 + b1)
            h = _gelu(h @ w2 + b2)
            h = _gelu(h @ w3 + b3)
            return jax.nn.sigmoid(h @ w4 + b4)

        def _global_net(h, w1, b1, w2, b2, w3, b3):
            h = _gelu(h @ w1 + b1)
            h = _gelu(h @ w2 + b2)
            return jax.nn.sigmoid(h @ w3 + b3)

        def _twist(x):
            o_r, o_i, p_r, p_i = jnp.split(x, 4, axis=-1)
            return jnp.concatenate([p_r, -p_i, -o_r, o_i], axis=-1)
        key = jax.random.key(seed)
        ks = jax.random.split(key, 9)
        d = DIM

        def w(k, fan_in, fan_out):
            return jax.random.normal(k, (fan_in, fan_out), dtype=jnp.float32) / np.sqrt(fan_in).astype(np.float32)
        inp = {'x': jax.random.normal(ks[0], (B, S, d), dtype=jnp.float32)}
        cn_dims = [(d, d), (d, d // 2), (d // 2, d // 4), (d // 4, 1)]
        for i, (a, b) in enumerate(cn_dims):
            inp[f'cn_w{i + 1}'] = w(ks[1 + i], a, b)
            inp[f'cn_b{i + 1}'] = jnp.zeros((b,), dtype=jnp.float32)
        gc_dims = [(d, d // 2), (d // 2, d // 4), (d // 4, 1)]
        for i, (a, b) in enumerate(gc_dims):
            inp[f'gc_w{i + 1}'] = w(ks[5 + i], a, b)
            inp[f'gc_b{i + 1}'] = jnp.zeros((b,), dtype=jnp.float32)
        inp['adaptive_range'] = jnp.full((1,), 0.2, dtype=jnp.float32)
        return inp
    _L0_ffn_in = _L0_ffn_setup()
    _d = {'L0_attn_x': _L0_attn_in['x'], 'L0_attn_w_qkv': _L0_attn_in['w_qkv'], 'L0_attn_w_o': _L0_attn_in['w_o'], 'L0_attn_w_qi': _L0_attn_in['w_qi'], 'L0_attn_w_ki': _L0_attn_in['w_ki'], 'L0_attn_w_wi': _L0_attn_in['w_wi'], 'L0_ffn_cn_w1': _L0_ffn_in['cn_w1'], 'L0_ffn_cn_b1': _L0_ffn_in['cn_b1'], 'L0_ffn_cn_w2': _L0_ffn_in['cn_w2'], 'L0_ffn_cn_b2': _L0_ffn_in['cn_b2'], 'L0_ffn_cn_w3': _L0_ffn_in['cn_w3'], 'L0_ffn_cn_b3': _L0_ffn_in['cn_b3'], 'L0_ffn_cn_w4': _L0_ffn_in['cn_w4'], 'L0_ffn_cn_b4': _L0_ffn_in['cn_b4'], 'L0_ffn_gc_w1': _L0_ffn_in['gc_w1'], 'L0_ffn_gc_b1': _L0_ffn_in['gc_b1'], 'L0_ffn_gc_w2': _L0_ffn_in['gc_w2'], 'L0_ffn_gc_b2': _L0_ffn_in['gc_b2'], 'L0_ffn_gc_w3': _L0_ffn_in['gc_w3'], 'L0_ffn_gc_b3': _L0_ffn_in['gc_b3'], 'L0_ffn_adaptive_range': _L0_ffn_in['adaptive_range']}
    _x0 = _d['L0_attn_x']
    _d['L0_attn_x'] = jax.random.normal(jax.random.fold_in(jax.random.key(seed), 1), (2, 2048, 256), dtype=_x0.dtype)
    del _x0
    return _d

def reference(L0_attn_x, L0_attn_w_qkv, L0_attn_w_o, L0_attn_w_qi, L0_attn_w_ki, L0_attn_w_wi, L0_ffn_cn_w1, L0_ffn_cn_b1, L0_ffn_cn_w2, L0_ffn_cn_b2, L0_ffn_cn_w3, L0_ffn_cn_b3, L0_ffn_cn_w4, L0_ffn_cn_b4, L0_ffn_gc_w1, L0_ffn_gc_b1, L0_ffn_gc_w2, L0_ffn_gc_b2, L0_ffn_gc_w3, L0_ffn_gc_b3, L0_ffn_adaptive_range):

    def _L0_attn_ref(x, w_qkv, w_o, w_qi, w_ki, w_wi):
        import jax, jax.numpy as jnp
        import numpy as np
        D = 256
        H = 16
        DK = D // H
        HI = 4
        DI = 64
        K = 128
        B, S = (2, 512)

        def _rope(x):
            d = x.shape[-1]
            s = x.shape[1]
            inv = 1.0 / 10000.0 ** (jnp.arange(0, d, 2, dtype=jnp.float32) / d)
            ang = jnp.arange(s, dtype=jnp.float32)[:, None] * inv
            cos = jnp.cos(ang)[None, :, None, :]
            sin = jnp.sin(ang)[None, :, None, :]
            x1, x2 = (x[..., ::2], x[..., 1::2])
            return jnp.stack([x1 * cos - x2 * sin, x1 * sin + x2 * cos], axis=-1).reshape(x.shape)
        b, s, _ = x.shape
        qkv = (x @ w_qkv.T).reshape(b, s, 3, H, DK)
        q, k, v = (qkv[:, :, 0], qkv[:, :, 1], qkv[:, :, 2])
        q = _rope(q)
        k = _rope(k)
        qi = (x @ w_qi.T).reshape(b, s, HI, DI)
        ki = x @ w_ki.T
        wi = x @ w_wi.T
        dots = jnp.einsum('bthd,bsd->bths', qi, ki)
        idx_scores = (jax.nn.relu(dots) * wi[:, :, :, None]).sum(axis=2)
        causal = jnp.triu(jnp.ones((s, s), dtype=bool), 1)
        masked_scores = jnp.where(causal[None], -jnp.inf, idx_scores)
        _, top_idx = jax.lax.top_k(masked_scores, K)
        allow = jnp.zeros((b, s, s), dtype=bool).at[jnp.arange(b)[:, None, None], jnp.arange(s)[None, :, None], top_idx].set(True)
        scores = jnp.einsum('bthd,bshd->bhts', q, k) / jnp.sqrt(jnp.float32(DK))
        scores = jnp.where(allow[:, None], scores, -jnp.inf)
        attn = jax.nn.softmax(scores, axis=-1)
        out = jnp.einsum('bhts,bshd->bthd', attn, v).reshape(b, s, D)
        return out @ w_o.T

    def _L0_ffn_ref(x, cn_w1, cn_b1, cn_w2, cn_b2, cn_w3, cn_b3, cn_w4, cn_b4, gc_w1, gc_b1, gc_w2, gc_b2, gc_w3, gc_b3, adaptive_range):
        import jax, jax.numpy as jnp
        import numpy as np
        B, S, DIM = (4, 1024, 256)
        BASE_COUPLING = 0.1
        NUM_CYCLES = 3

        def _gelu(x):
            return jax.nn.gelu(x, approximate=False)

        def _coupling_net(h, w1, b1, w2, b2, w3, b3, w4, b4):
            h = _gelu(h @ w1 + b1)
            h = _gelu(h @ w2 + b2)
            h = _gelu(h @ w3 + b3)
            return jax.nn.sigmoid(h @ w4 + b4)

        def _global_net(h, w1, b1, w2, b2, w3, b3):
            h = _gelu(h @ w1 + b1)
            h = _gelu(h @ w2 + b2)
            return jax.nn.sigmoid(h @ w3 + b3)

        def _twist(x):
            o_r, o_i, p_r, p_i = jnp.split(x, 4, axis=-1)
            return jnp.concatenate([p_r, -p_i, -o_r, o_i], axis=-1)
        global_context = x.mean(axis=1, keepdims=True)
        gf = _global_net(global_context, gc_w1, gc_b1, gc_w2, gc_b2, gc_w3, gc_b3)
        out = x
        for _ in range(NUM_CYCLES):
            tf = _coupling_net(out, cn_w1, cn_b1, cn_w2, cn_b2, cn_w3, cn_b3, cn_w4, cn_b4)
            combined = 0.7 * gf + 0.3 * tf
            coupling = BASE_COUPLING + adaptive_range * (combined - 0.5) * 2.0
            out = out + coupling * _twist(out)
        return out
    x = L0_attn_x
    x = x + _L0_attn_ref(_layernorm(x, axis=-1), L0_attn_w_qkv, L0_attn_w_o, L0_attn_w_qi, L0_attn_w_ki, L0_attn_w_wi)
    x = x + _L0_ffn_ref(_layernorm(x, axis=-1), L0_ffn_cn_w1, L0_ffn_cn_b1, L0_ffn_cn_w2, L0_ffn_cn_b2, L0_ffn_cn_w3, L0_ffn_cn_b3, L0_ffn_cn_w4, L0_ffn_cn_b4, L0_ffn_gc_w1, L0_ffn_gc_b1, L0_ffn_gc_w2, L0_ffn_gc_b2, L0_ffn_gc_w3, L0_ffn_gc_b3, L0_ffn_adaptive_range)
    return x

_drawn_inputs = setup_inputs


def setup_inputs(seed=0):
    import zlib

    import numpy as np

    out = dict(_drawn_inputs(seed))
    spreads = {'L0_ffn_cn_b1': (0.0, 2.0),
     'L0_ffn_cn_b2': (0.0, 2.0),
     'L0_ffn_cn_b3': (0.0, 2.0),
     'L0_ffn_gc_b1': (0.0, 0.8),
     'L0_ffn_gc_b2': (0.0, 2.0)}
    factors = {'L0_attn_w_qkv': 4.235,
     'L0_attn_w_o': 4.116,
     'L0_attn_w_qi': 4.349,
     'L0_attn_w_ki': 4.339,
     'L0_attn_w_wi': 4.56,
     'L0_ffn_cn_w1': 7.411,
     'L0_ffn_cn_w2': 7.761,
     'L0_ffn_cn_w3': 6.212,
     'L0_ffn_cn_w4': 6.946,
     'L0_ffn_gc_w1': 64.0,
     'L0_ffn_gc_w2': 8.0,
     'L0_ffn_gc_w3': 5.638}
    for name, (base, spread) in spreads.items():
        noise = np.random.default_rng([zlib.crc32(name.encode()), seed]).standard_normal(out[name].shape)
        drawn = base * np.exp(spread * noise) if base else spread * noise
        out[name] = jnp.asarray(drawn.astype(out[name].dtype))
    for name, factor in factors.items():
        out[name] = (out[name] * factor).astype(out[name].dtype)
    return out
```

```python
import concourse.bass as bass
import numpy as np
from concourse import mybir
from contextlib import ExitStack

FP32 = mybir.dt.float32
BF16 = mybir.dt.bfloat16
ALU = mybir.AluOpType
ACT = mybir.ActivationFunctionType
AX = mybir.AxisListType

B, S, D = 2, 2048, 256
H, DK = 16, 16
HI, DI = 4, 64
TOPK = 128
EPS = 1e-5
P = 128
NT = S // P
GT = 4
GW = GT * P
NG = NT // GT
KD = D // P
QUAD = 4
NQ = H // QUAD
PW = 1024
RING = 3
PARTS = 3
Q_SLOTS = (0, 0, 0, 1, 1, 2)
K_SLOTS = (0, 1, 2, 0, 1, 0)
KR = len(Q_SLOTS) * DK
KM = KR + PARTS
VW = DK + 1
VP = H * VW + 32 - VW
CAUSAL = -3.3e38
TAKEN = -3.4e38
HIDE = -1.0e30
CYCLES = 3


def rope_tables():
    inv = (np.float32(1.0) / np.float32(10000.0) ** (np.arange(0, DK, 2, dtype=np.float32) / np.float32(DK))).astype(np.float32)
    ang = (np.arange(S, dtype=np.float32)[:, None] * inv).astype(np.float32)
    lay = lambda a: np.ascontiguousarray(a.astype(np.float32).reshape(NT, P, -1).transpose(1, 0, 2))
    cos, sin = np.cos(ang), np.sin(ang)
    return lay(np.repeat(cos, 2, axis=1)), lay(sin), lay(-sin)


class Steps:

    def __init__(self):
        self.groups = list(range(NG))[::-1]
        self.n = NT + GT
        self.slot, self.order, self.count = {}, [], {}
        self.dots(0)
        for u in range(self.n):
            a = self.attend(u)
            if a:
                for j in range(GT * (a[0] + 1)):
                    for p in range(2):
                        self.use("exp", ("exp", u, j, p))
            if u < NT:
                self.use("mask", ("mask", u))
                for h in range(H):
                    for k, _ in self.parts(u):
                        self.use("max", ("max", u, h, k))
            if a and a[1] == NQ - 1:
                self.use("out", ("out", u))
            if u + 1 < NT:
                self.dots(u + 1)

    def dots(self, u):
        if self.tile(u):
            for k, _ in self.parts(u):
                for h in range(HI):
                    self.use("dot", ("dot", u, k, h))

    def use(self, kind, key):
        self.count[kind] = self.count.get(kind, 0) + 1
        self.slot[key] = (len(self.order) % RING, self.count[kind])
        self.order.append((kind, self.count[kind]))

    def tile(self, u):
        return GT * self.groups[u // GT] + u % GT

    def width(self, u):
        return P * (self.tile(u) + 1)

    def parts(self, u):
        n = self.width(u)
        return [(k, min(PW, n - k * PW)) for k in range((n + PW - 1) // PW)]

    def attend(self, u):
        return (self.groups[(u - GT) // GT], (u - GT) % GT) if u >= GT else None


def prepare(nc, b, x, w, tabs, consts, keep, scratch):
    K99, V, kiT, wi = keep
    qkD, qiD = scratch
    identf, identb = consts
    with ExitStack() as ctx:
        sb = lambda n, s, d: ctx.enter_context(nc.sbuf_tensor(n, s, d))
        ps = lambda n, s, d: ctx.enter_context(nc.psum_tensor(n, s, d))
        sems = []

        def sem(n):
            sems.append(ctx.enter_context(nc.semaphore(n)))
            return sems[-1]

        xn = sb("xn", [P, NT, D], FP32)
        stats = sb("stats", [P, NT, 6], FP32)
        mv = sb("mv", [P, NT, 2], FP32)
        sd = sb("sd", [P, NT], FP32)
        rstd = sb("rstd", [P, NT], FP32)
        eps = sb("eps", [P, 1], FP32)
        xnT = sb("xnT", [P, KD, S], FP32)
        wqkv = sb("wqkv", [P, KD, 3 * D + HI], FP32)
        wqi = sb("wqi", [P, KD, HI * DI], FP32)
        wki = sb("wki", [P, KD, 2 * DI], FP32)
        cos = sb("cos", [P, NT, DK], FP32)
        sin = sb("sin", [P, NT, DK // 2], FP32)
        nsin = sb("nsin", [P, NT, DK // 2], FP32)
        t1 = sb("t1", [P, 2, 2 * D], FP32)
        t2 = sb("t2", [P, 2, 2 * D], FP32)
        rot = sb("rot", [P, 3, 2 * D], FP32)
        rem = sb("rem", [P, 3, 2 * D], FP32)
        split = sb("split", [P, 3, 2 * H * PARTS * DK], BF16)
        stage = sb("stage", [2 * PARTS * DK, 2, 2, H // 2, GW], BF16)
        qi = sb("qi", [P, 2, 2, GW], FP32)
        pT = [ps(f"pT{k}", [P, KD, P], FP32) for k in range(2)]
        pA = [ps(f"pA{k}", [P, 512], FP32) for k in range(2)]
        pB = [ps(f"pB{k}", [P, 512], FP32) for k in range(2)]
        pS = [ps(f"pS{k}", [P, H // 2, P], BF16) for k in range(2)]
        x_in = [sem(f"x_in{g}") for g in range(NG)]
        w_in, wi_in, tab_in = sem("w_in"), sem("wi_in"), sem("tab_in")
        eps_set, stats_done, mv_done, sd_done, rstd_done = (sem(n) for n in ("eps_set", "stats_done", "mv_done", "sd_done", "rstd_done"))
        xn_done, turned, xT_done = sem("xn_done"), sem("turned"), sem("xT_done")
        qkv_done, v_taken, t_done = sem("qkv_done"), sem("v_taken"), sem("t_done")
        rot_done, hi_done, rem_done, mid_done, lo_done = (sem(n) for n in ("rot_done", "hi_done", "rem_done", "mid_done", "lo_done"))
        split_turned, staged, index_done, index_taken = (sem(n) for n in ("split_turned", "staged", "index_done", "index_taken"))
        stored = [sem(f"stored{k}") for k in range(2)]
        qi_out, k_in = [sem(f"qi_out{k}") for k in range(2)], sem("k_in")

        wide = lambda a, i: a[:, i % 3, :].rearrange("p (h d) -> p h d", d=DK)
        parts = lambda i: split[:, i % 3, :].rearrange("p (h s d) -> p h s d", s=PARTS, d=DK)

        with nc.Block() as block:

            @block.sync
            def _(sp):
                xb = x.rearrange("(b t p) d -> b p t d", b=B, p=P)
                for g in range(NG):
                    sp.dma_start(xn[:, g * GT:(g + 1) * GT, :], xb[bass.ds(b, 1), :, g * GT:(g + 1) * GT, :].rearrange("o p t d -> (o p) t d")).then_inc(x_in[g], 16)
                sp.dma_start(wqkv[:, :, 0:3 * D], w["qkvT"].rearrange("(k p) n -> p k n", p=P)).then_inc(w_in, 16)
                sp.dma_start(wqkv[:, :, 3 * D:], w["wiT"].rearrange("(k p) n -> p k n", p=P)).then_inc(w_in, 16)
                for a, t in zip((cos, sin, nsin), tabs):
                    sp.dma_start(a[:], t).then_inc(tab_in, 16)
                sp.dma_start(wqi[:], w["qiT"].rearrange("(k p) n -> p k n", p=P)).then_inc(wi_in, 16)
                for c in range(2):
                    sp.dma_start(wki[:, :, c * DI:(c + 1) * DI], w["kiT"].rearrange("(k p) n -> p k n", p=P)).then_inc(wi_in, 16)
                for g in range(NG):
                    sp.wait_ge(staged, 2 * GT * (g + 1))
                    for c in range(2):
                        sp.dma_start(qkD[c].rearrange("(hp p) t -> p hp t", p=2 * PARTS * DK)[:, :, g * GW:(g + 1) * GW],
                                     stage[:, g % 2, c]).then_inc(stored[g % 2], 16)
                for g in range(NG):
                    sp.wait_ge(index_taken, 3 * (g + 1))
                    sp.dma_start(qiD[:, :, g * GW:(g + 1) * GW], qi[:, g % 2]).then_inc(qi_out[g % 2], 16)
                for k in range(2):
                    sp.wait_ge(stored[k], 16 * 2 * (NG // 2))
                for r, part in enumerate(K_SLOTS):
                    sp.dma_start(K99[r * DK:(r + 1) * DK, :, :],
                                 qkD[1].rearrange("(h s d) t -> s d h t", s=PARTS, d=DK)[part]).then_inc(k_in, 16)
                sp.wait_ge(k_in, 16 * len(K_SLOTS))
                for k in range(2):
                    sp.wait_ge(qi_out[k], 16 * (NG // 2))

            @block.vector
            def _(dve):
                dve.memset(eps[:], EPS).then_inc(eps_set, 1)
                for i in range(NT):
                    if i % GT == 0:
                        dve.wait_ge(x_in[i // GT], 16)
                    dve.bn_stats(out=stats[:, i, :], in_=xn[:, i, :]).then_inc(stats_done, 1)
                for i in range(NT):
                    dve.wait_ge(stats_done, i + 1)
                    dve.bn_aggr(out=mv[:, i, :], in_=stats[:, i, :]).then_inc(mv_done, 1)
                dve.wait_ge(sd_done, 1)
                dve.reciprocal(rstd[:], sd[:]).then_inc(rstd_done, 1)
                dve.wait_ge(rstd_done, 1)
                for i in range(NT):
                    dve.tensor_scalar(xn[:, i, :], xn[:, i, :], mv[:, i, 0:1], rstd[:, i:i + 1], ALU.subtract, ALU.mult).then_inc(xn_done, 1)
                dve.wait_ge(tab_in, 16 * len(tabs))

                def rope(i):
                    q = pA[i % 2][:, :].rearrange("p (h d) -> p h d", d=DK)
                    a = t1[:, i % 2, :].rearrange("p (h d) -> p h d", d=DK)
                    c = t2[:, i % 2, :].rearrange("p (h d) -> p h d", d=DK)
                    bc = lambda t, n: t[:, i, :].unsqueeze(1).to_broadcast([P, 2 * H, n])
                    dve.wait_ge(qkv_done, i + 1)
                    if i >= 2:
                        dve.wait_ge(rot_done, i - 1)
                    dve.tensor_tensor(a, q, bc(cos, DK), ALU.mult).then_inc(t_done, 1)
                    dve.tensor_tensor(c[:, :, 0::2], q[:, :, 1::2], bc(nsin, DK // 2), ALU.mult).then_inc(t_done, 1)
                    dve.tensor_tensor(c[:, :, 1::2], q[:, :, 0::2], bc(sin, DK // 2), ALU.mult).then_inc(t_done, 1)

                def take_parts(i):
                    g, t = i // GT, i % GT
                    dve.wait_ge(split_turned, 2 * (i + 1))
                    if t == 0 and g >= 2:
                        dve.wait_ge(stored[g % 2], 32 * (g // 2))
                    for c in range(2):
                        dve.tensor_copy(stage[:, g % 2, c, :, t * P:(t + 1) * P], pS[c][0:2 * PARTS * DK, :, :]).then_inc(staged, 1)

                for i in range(NT + 3):
                    if i < NT:
                        rope(i)
                    if i >= 3:
                        take_parts(i - 3)

            @block.gpsimd
            def _(pool):
                for i in range(NT + 2):
                    if i < NT:
                        pool.wait_ge(t_done, 3 * (i + 1))
                        if i >= 3:
                            pool.wait_ge(rem_done, i - 2)
                            pool.wait_ge(hi_done, i - 2)
                        pool.tensor_tensor(rot[:, i % 3, :], t1[:, i % 2, :], t2[:, i % 2, :], ALU.add).then_inc(rot_done, 1)
                    if 1 <= i <= NT:
                        k = i - 1
                        pool.wait_ge(hi_done, k + 1)
                        pool.wait_ge(rot_done, k + 1)
                        if k >= 3:
                            pool.wait_ge(lo_done, k - 2)
                            pool.wait_ge(mid_done, k - 2)
                        pool.tensor_tensor(wide(rem, k), wide(rot, k), parts(k)[:, :, 0, :], ALU.subtract).then_inc(rem_done, 1)
                    if i >= 2:
                        k = i - 2
                        pool.wait_ge(mid_done, k + 1)
                        pool.wait_ge(rem_done, k + 1)
                        pool.tensor_tensor(parts(k)[:, :, 2, :], wide(rem, k), parts(k)[:, :, 1, :], ALU.subtract).then_inc(lo_done, 1)

            @block.scalar
            def _(act):
                act.wait_ge(mv_done, NT)
                act.wait_ge(eps_set, 1)
                act.activation(sd[:], mv[:, :, 1], ACT.Sqrt, bias=eps[:, 0:1]).then_inc(sd_done, 1)
                for i in range(NT + 2):
                    if i < NT:
                        act.wait_ge(turned, i + 1)
                        act.activation(xnT[:, :, i * P:(i + 1) * P], pT[i % 2][:], ACT.Copy).then_inc(xT_done, 1)
                    if 1 <= i <= NT:
                        k = i - 1
                        act.wait_ge(qkv_done, k + 1)
                        act.activation(V[:, k, 0:H * VW].rearrange("p (h d) -> p h d", d=VW)[:, :, 0:DK],
                                       pB[k % 2][:, 0:D].rearrange("p (h d) -> p h d", d=DK), ACT.Copy).then_inc(v_taken, 1)
                        act.activation(wi[:, k, :], pB[k % 2][:, D:D + HI], ACT.Copy).then_inc(v_taken, 1)
                        act.wait_ge(rot_done, k + 1)
                        if k >= 3:
                            act.wait_ge(split_turned, 2 * (k - 2))
                        act.activation(parts(k)[:, :, 0, :], wide(rot, k), ACT.Copy).then_inc(hi_done, 1)
                    if i >= 2:
                        k = i - 2
                        act.wait_ge(rem_done, k + 1)
                        act.activation(parts(k)[:, :, 1, :], wide(rem, k), ACT.Copy).then_inc(mid_done, 1)
                banks = pA + pB
                for n in range(3 * NG):
                    g, m = n // 3, n % 3
                    act.wait_ge(index_done, n + 1)
                    if m == 0 and g >= 2:
                        act.wait_ge(qi_out[g % 2], 16 * (g // 2))
                    dst = kiT[:, g * GW:(g + 1) * GW] if m == 2 else qi[:, g % 2, m, :]
                    act.activation(dst, banks[n % 4][:], ACT.Copy).then_inc(index_taken, 1)

            @block.tensor
            def _(pe):
                def turn(i):
                    pe.wait_ge(xn_done, i + 1)
                    if i >= 2:
                        pe.wait_ge(xT_done, i - 1)
                    for k in range(KD):
                        mm = pe.transpose(pT[i % 2][:, k, :], xn[:, i, k * P:(k + 1) * P], identf[:])
                    mm.then_inc(turned, 1)

                def project(i):
                    pe.wait_ge(xT_done, i + 1)
                    if i >= 2:
                        pe.wait_ge(t_done, 3 * (i - 1))
                        pe.wait_ge(v_taken, 2 * (i - 1))
                    for dst, c0, c1 in ((pA, 0, 2 * D), (pB, 2 * D, 3 * D + HI)):
                        for k in range(KD):
                            mm = pe.matmul(dst[i % 2][:, 0:c1 - c0], xnT[:, k, i * P:(i + 1) * P], wqkv[:, k, c0:c1],
                                           start=(k == 0), stop=(k == KD - 1))
                    mm.then_inc(qkv_done, 1)

                def turn_parts(i):
                    pe.wait_ge(lo_done, i + 1)
                    for c in range(2):
                        if i >= 1:
                            pe.wait_ge(staged, 2 * (i - 1) + c + 1)
                        for hp in range(H // 2):
                            c0 = (c * (H // 2) + hp) * 2 * PARTS * DK
                            mm = pe.transpose(pS[c][0:2 * PARTS * DK, hp, :], split[:, i % 3, c0:c0 + 2 * PARTS * DK], identb[:])
                        mm.then_inc(split_turned, 1)

                turn(0)
                pe.wait_ge(w_in, 32)
                for i in range(NT + 3):
                    if i + 1 < NT:
                        turn(i + 1)
                    if i < NT:
                        project(i)
                    if i >= 3:
                        turn_parts(i - 3)
                pe.wait_ge(wi_in, 48)
                pe.wait_ge(t_done, 3 * NT)
                pe.wait_ge(v_taken, 2 * NT)
                banks = pA + pB
                for n in range(3 * NG):
                    g, m = n // 3, n % 3
                    if n >= 4:
                        pe.wait_ge(index_taken, n - 3)
                    for k in range(KD):
                        lhs = wki[:, k, :] if m == 2 else wqi[:, k, m * P:(m + 1) * P]
                        mm = pe.matmul(banks[n % 4][:], lhs, xnT[:, k, g * GW:(g + 1) * GW], start=(k == 0), stop=(k == KD - 1))
                    mm.then_inc(index_done, 1)

        clear(nc, sems)


def clear(nc, sems):
    nc.all_engine_barrier()
    for s in sems:
        nc.sync.sem_clear(s)
    nc.all_engine_barrier()


def attention(nc, b, x, consts, keep, scratch):
    K99, V, kiT, wi = keep
    qkD, qiD, x2D = scratch
    identf, identb, woT = consts
    st = Steps()
    with ExitStack() as ctx:
        sb = lambda n, s, d: ctx.enter_context(nc.sbuf_tensor(n, s, d))
        ps = lambda n, s, d: ctx.enter_context(nc.psum_tensor(n, s, d))
        sems = []

        def sem(n):
            sems.append(ctx.enter_context(nc.semaphore(n)))
            return sems[-1]

        Q99 = [sb(f"Q99_{k}", [KM, H, GW], BF16) for k in range(2)]
        maskT = [sb(f"maskT{k}", [P, (NT if k == (NG - 1) % 2 else NT - GT), GW], BF16) for k in range(2)]
        sc = sb("sc", [P, S], FP32)
        top8 = sb("top8", [P, 8], FP32)
        relu = sb("relu", [P, 2, PW], FP32)
        bias = sb("bias", [P, S], BF16)
        junk = sb("junk", [P, 2, PW], BF16)
        mx = sb("mx", [P, 2, H], FP32)
        mall = sb("mall", [P, H], FP32)
        mrem = sb("mrem", [P, H], FP32)
        msplit = sb("msplit", [P, PARTS, H], BF16)
        mT = sb("mT", [PARTS * H, GW], BF16)
        qi = sb("qi_t", [P, 2, 2, P], FP32)
        prob = sb("prob", [P, 4, 2, GW], FP32)
        oT = sb("oT", [P, GW], FP32)
        rsum = sb("rsum", [P, GT, QUAD], FP32)
        otok = sb("otok", [P, GT, D], FP32)
        otokT = relu[:, 0, :].rearrange("p (k q) -> p k q", k=KD)
        xg = sb("xg", [P, GT, D], FP32)
        ring = [ps(f"ring{k}", [P, 2, 512], FP32) for k in range(RING)]
        pO = ps("pO", [P, GW], FP32)
        pX = ps("pX", [P, 512], FP32)

        kinds = ("exp", "mask", "max", "out", "dot")
        filled = {k: sem(f"{k}_filled") for k in kinds}
        taken = {k: sem(f"{k}_taken") for k in kinds}
        q_in = [sem(f"q_in{k}") for k in range(2)]
        qm_in = sem("qm_in")
        qi_in = [sem(f"qi_in{k}") for k in range(2)]
        x_in, x2_out = sem("xg_in"), sem("x2_out")
        summed, causal_done, chain = sem("summed"), sem("causal_done"), sem("chain")
        bias_done, msplit_done, m_turned, mT_done = sem("bias_done"), sem("msplit_done"), sem("m_turned"), sem("mT_done")
        pv_done, oT_done, o_turned, normed = sem("pv_done"), sem("oT_done"), sem("o_turned"), sem("normed")
        ot_turned, otT_done = sem("ot_turned"), sem("otT_done")

        def view(key, w=PW):
            return ring[st.slot[key][0]][:, :, :].rearrange("p a b -> p (a b)")[:, 0:w]

        chunks = [0]
        for u in range(st.n):
            a = st.attend(u)
            chunks.append(chunks[-1] + (GT * (a[0] + 1) if a else 0))
        dots_upto = {}
        for (key, (_, c)) in st.slot.items():
            if key[0] == "dot":
                dots_upto[key[1]] = max(dots_upto.get(key[1], 0), c)

        with nc.Block() as block:

            @block.sync
            def _(sp):
                xb = x.rearrange("(b t p) d -> b p t d", b=B, p=P)
                x2 = x2D.rearrange("(t p) d -> p t d", p=P)

                def load_q(g):
                    for r, part in enumerate(Q_SLOTS):
                        sp.dma_start(Q99[g % 2][r * DK:(r + 1) * DK, :, :],
                                     qkD[0].rearrange("(h s d) t -> s d h t", s=PARTS, d=DK)[part][:, :, g * GW:(g + 1) * GW]).then_inc(q_in[g % 2], 16)

                def load_qi(u):
                    i = st.tile(u)
                    sp.dma_start(qi[:, u % 2], qiD[:, :, i * P:(i + 1) * P]).then_inc(qi_in[u % 2], 16)

                load_qi(0)
                load_qi(1)
                load_q(st.groups[0])
                load_q(st.groups[1])
                for u in range(st.n):
                    a = st.attend(u)
                    if u + 2 < NT and st.tile(u + 2):
                        sp.wait_ge(filled["dot"], dots_upto[u if st.tile(u) else u - 2])
                        load_qi(u + 2)
                    if a and a[1] == 0:
                        if a[0] != st.groups[0]:
                            sp.wait_ge(x2_out, 16 * st.groups.index(a[0]))
                        sp.dma_start(xg[:], xb[bass.ds(b, 1), :, a[0] * GT:(a[0] + 1) * GT, :].rearrange("o p t d -> (o p) t d")).then_inc(x_in, 16)
                    if u < NT and u % GT == GT - 1:
                        sp.wait_ge(mT_done, u + 1)
                        for r in range(PARTS):
                            sp.dma_start(Q99[st.groups[u // GT] % 2][KR + r:KR + r + 1, :, :], mT[r * H:(r + 1) * H, :]).then_inc(qm_in, 16)
                    if a and a[1] == NQ - 1:
                        if a[0] - 2 >= 0:
                            sp.wait_ge(pv_done, chunks[u + 1])
                            load_q(a[0] - 2)
                        sp.wait_ge(taken["out"], st.slot[("out", u)][1])
                        sp.dma_start(x2[:, a[0] * GT:(a[0] + 1) * GT, :], xg[:]).then_inc(x2_out, 16)
                sp.wait_ge(x2_out, 16 * NG)

            @block.vector
            def _(dve):
                links = [0]

                def link(ins):
                    links[0] += 1
                    ins.then_inc(chain, 1)
                    dve.wait_ge(chain, links[0])

                def add_dots(u):
                    i = st.tile(u)
                    if i == 0:
                        return
                    for k, w in st.parts(u):
                        part = sc[:, k * PW:k * PW + w]
                        for h in range(HI):
                            c = st.slot[("dot", u, k, h)][1]
                            dve.wait_ge(taken["dot"], c)
                            r = relu[:, (c - 1) % 2, 0:w]
                            if h == 0:
                                ins = dve.tensor_scalar(part, r, wi[:, i, 0:1], 0.0, ALU.mult, ALU.add)
                            else:
                                ins = dve.scalar_tensor_tensor(out=part, in0=r, scalar=wi[:, i, h:h + 1], in1=part, op0=ALU.mult, op1=ALU.add)
                            ins.then_inc(summed, 1)
                            dve.wait_ge(summed, c)

                def choose(u):
                    i, n = st.tile(u), st.width(u)
                    if i == 0:
                        dve.memset(bias[:, 0:n], 0.0).then_inc(bias_done, 1)
                        return
                    dve.wait_ge(causal_done, sum(1 for v in range(u + 1) if st.tile(v)))
                    for _ in range(TOPK // 8):
                        link(dve.max(out=top8[:], in_=sc[:, 0:n]))
                        link(dve.match_replace(out=sc[:, 0:n], in_to_replace=top8[:], in_values=sc[:, 0:n], imm_value=TAKEN))
                    dve.tensor_scalar(bias[:, 0:n], sc[:, 0:n], TAKEN, HIDE, ALU.not_equal, ALU.mult).then_inc(bias_done, 1)

                def maxima(u):
                    dve.wait_ge(bias_done, u + 1)
                    for h in range(H):
                        for k, w in st.parts(u):
                            key = ("max", u, h, k)
                            c = st.slot[key][1]
                            dve.wait_ge(filled["max"], c)
                            if c > 2:
                                dve.wait_ge(taken["max"], c - 2)
                            dve.tensor_tensor_reduce(out=junk[:, c % 2, 0:w], in0=view(key, w), in1=bias[:, k * PW:k * PW + w], scale=1.0, scalar=-3.0e38,
                                                     op0=ALU.add, op1=ALU.max, accum_out=mx[:, k, h:h + 1]).then_inc(taken["max"], 1)
                    dve.wait_ge(taken["max"], st.slot[("max", u, H - 1, len(st.parts(u)) - 1)][1])
                    last = mx[:, 0, :]
                    if len(st.parts(u)) == 2:
                        link(dve.tensor_tensor(mall[:], mx[:, 0, :], mx[:, 1, :], ALU.max))
                        last = mall[:]
                    link(dve.tensor_scalar(mrem[:], last, -1.0, None, ALU.mult))
                    if u >= 1:
                        dve.wait_ge(m_turned, u)
                    for r in range(PARTS - 1):
                        link(dve.tensor_copy(msplit[:, r, :], mrem[:]))
                        link(dve.tensor_tensor(mrem[:], mrem[:], msplit[:, r, :], ALU.subtract))
                    dve.tensor_copy(msplit[:, PARTS - 1, :], mrem[:]).then_inc(msplit_done, 1)

                def norm(u):
                    g, hq = st.attend(u)
                    dve.wait_ge(o_turned, u - GT + 1)
                    o = pX[:, :].rearrange("p (t h d) -> p t h d", t=GT, d=32)
                    link(dve.reciprocal(rsum[:], o[:, :, :, DK]))
                    if hq == 0 and g != st.groups[0]:
                        dve.wait_ge(ot_turned, KD * st.groups.index(g))
                    dst = otok[:, :, hq * QUAD * DK:(hq + 1) * QUAD * DK].rearrange("p t (h d) -> p t h d", d=DK)
                    for t in range(GT):
                        dve.tensor_tensor(dst[:, t], o[:, t, :, 0:DK], rsum[:, t].unsqueeze(2).to_broadcast([P, QUAD, DK]),
                                          ALU.mult).then_inc(normed, 1)

                def residual(u):
                    g, _ = st.attend(u)
                    dve.wait_ge(filled["out"], st.slot[("out", u)][1])
                    dve.wait_ge(x_in, 16 * (st.groups.index(g) + 1))
                    flat = xg[:, :, :].rearrange("p t d -> p (t d)")
                    dve.tensor_tensor(flat, view(("out", u)), flat, ALU.add).then_inc(taken["out"], 1)

                add_dots(0)
                for u in range(st.n):
                    if u < NT:
                        choose(u)
                    if u >= GT:
                        norm(u)
                    if u < NT:
                        maxima(u)
                    if u >= GT and st.attend(u)[1] == NQ - 1:
                        residual(u)
                    if u + 1 < NT:
                        add_dots(u + 1)

            @block.gpsimd
            def _(pool):
                done = 0
                for u in range(NT):
                    i, n = st.tile(u), st.width(u)
                    if i == 0:
                        continue
                    done += HI * len(st.parts(u))
                    pool.wait_ge(summed, done)
                    pool.affine_select(out=sc[:, n - P:n], in_=sc[:, n - P:n], compare_op=ALU.is_ge, fill=CAUSAL,
                                       base=0, pattern=[[-1, P]], channel_multiplier=1).then_inc(causal_done, 1)

            @block.scalar
            def _(act):
                def exps(u):
                    g, _ = st.attend(u)
                    for j in range(GT * (g + 1)):
                        c0 = max(0, j - GT * g) * P
                        n = chunks[u] + j
                        for p in range(2):
                            key = ("exp", u, j, p)
                            slot, c = st.slot[key]
                            act.wait_ge(filled["exp"], c)
                            if p == 0 and n >= 2:
                                act.wait_ge(pv_done, n - 1)
                            act.activation(prob[:, (2 * n + p) % 4, :, c0:GW], ring[slot][:, :, c0:GW], ACT.Exp, scale=float(DK) ** -0.5).then_inc(taken["exp"], 1)
                    act.wait_ge(pv_done, chunks[u + 1])
                    if u > GT:
                        act.wait_ge(o_turned, u - GT)
                    act.activation(oT[:], pO[:], ACT.Copy).then_inc(oT_done, 1)

                def mask_out(u):
                    i = st.tile(u)
                    key = ("mask", u)
                    act.wait_ge(filled["mask"], u + 1)
                    v = view(key).bitcast(BF16).rearrange("p (j q) -> p j q", q=P)
                    m = maskT[st.groups[u // GT] % 2]
                    act.activation(m[:, 0:i + 1, (u % GT) * P:(u % GT + 1) * P], v[:, 0:i + 1, :], ACT.Copy).then_inc(taken["mask"], 1)

                def m_out(u):
                    act.wait_ge(m_turned, u + 1)
                    if u % GT == 0 and u >= GT:
                        act.wait_ge(qm_in, 16 * PARTS * (u // GT))
                    act.activation(mT[:, (u % GT) * P:(u % GT + 1) * P], pX[0:PARTS * H, :].bitcast(BF16)[:, 0:P], ACT.Copy).then_inc(mT_done, 1)

                def final(u):
                    n = st.groups.index(st.attend(u)[0])
                    for k in range(KD):
                        act.wait_ge(ot_turned, KD * n + k + 1)
                        act.activation(otokT[:, k, :], pX[:], ACT.Copy).then_inc(otT_done, 1)

                def relus(u):
                    if st.tile(u) == 0:
                        return
                    for k, w in st.parts(u):
                        for h in range(HI):
                            key = ("dot", u, k, h)
                            c = st.slot[key][1]
                            act.wait_ge(filled["dot"], c)
                            if c > 2:
                                act.wait_ge(summed, c - 2)
                            act.activation(relu[:, (c - 1) % 2, 0:w], view(key, w), ACT.Relu).then_inc(taken["dot"], 1)

                relus(0)
                for u in range(st.n):
                    if u >= GT:
                        exps(u)
                    if u < NT:
                        mask_out(u)
                        m_out(u)
                    if u >= GT and st.attend(u)[1] == NQ - 1:
                        final(u)
                    if u + 1 < NT:
                        relus(u + 1)

            @block.tensor
            def _(pe):
                used = [0]

                def slot(key):
                    n = used[0]
                    assert st.order[n] == (key[0], st.slot[key][1])
                    used[0] += 1
                    if n >= RING:
                        kind, c = st.order[n - RING]
                        pe.wait_ge(taken[kind], c)
                    return ring[st.slot[key][0]]

                def dots(u):
                    i = st.tile(u)
                    if i == 0:
                        return
                    pe.wait_ge(qi_in[u % 2], 16 * sum(1 for v in range(u % 2, u + 1, 2) if st.tile(v)))
                    for k, w in st.parts(u):
                        for h in range(HI):
                            r = slot(("dot", u, k, h))
                            rows = slice((h % 2) * DI, (h % 2 + 1) * DI)
                            for c in range(0, w, 512):
                                cw = min(512, w - c)
                                mm = pe.matmul(r[:, c // 512, 0:cw], qi[rows, u % 2, h // 2, :], kiT[rows, k * PW + c:k * PW + c + cw], start=True, stop=True)
                            mm.then_inc(filled["dot"], 1)

                def scores(u, j):
                    g, hq = st.attend(u)
                    c0 = max(0, j - GT * g) * P
                    for p in range(2):
                        r = slot(("exp", u, j, p))
                        for a in range(2):
                            h = hq * QUAD + 2 * p + a
                            pe.matmul(r[:, a, c0:GW], K99[:, h, j * P:(j + 1) * P], Q99[g % 2][:, h, c0:GW], start=True, stop=False)
                            mm = pe.matmul(r[:, a, c0:GW], identb[:], maskT[g % 2][:, j, c0:GW], start=False, stop=True)
                        mm.then_inc(filled["exp"], 1)

                def values(u, j):
                    g, hq = st.attend(u)
                    c0 = max(0, j - GT * g) * P
                    n = chunks[u] + j
                    pe.wait_ge(taken["exp"], 2 * (n + 1))
                    if j == 0 and u > GT:
                        pe.wait_ge(oT_done, u - GT)
                    for q in range(QUAD):
                        h = hq * QUAD + q
                        mm = pe.matmul(pO[32 * q:32 * q + 32, c0:GW], V[:, j, h * VW:h * VW + 32], prob[:, (2 * n + q // 2) % 4, q % 2, c0:GW],
                                       start=(j == 0), stop=(j == GT * (g + 1) - 1))
                    mm.then_inc(pv_done, 1)

                def attend(u):
                    g, hq = st.attend(u)
                    n = GT * (g + 1)
                    if hq == 0:
                        pe.wait_ge(qm_in, 16 * PARTS * (st.groups.index(g) + 1))
                        pe.wait_ge(taken["mask"], GT * (st.groups.index(g) + 1))
                    for j in range(n + 1):
                        if j < n:
                            scores(u, j)
                        if j >= 1:
                            values(u, j - 1)
                    pe.wait_ge(oT_done, u - GT + 1)
                    if u <= NT and u >= 1:
                        pe.wait_ge(mT_done, u)
                    elif u > NT:
                        pe.wait_ge(normed, GT * (u - GT))
                    if u > GT and st.attend(u - 1)[1] == NQ - 1:
                        pe.wait_ge(otT_done, KD * (st.groups.index(st.attend(u - 1)[0]) + 1))
                    for t in range(GT):
                        mm = pe.transpose(pX[:, t * P:(t + 1) * P], oT[:, t * P:(t + 1) * P], identf[:])
                    mm.then_inc(o_turned, 1)

                def turn_mask(u):
                    i = st.tile(u)
                    pe.wait_ge(bias_done, u + 1)
                    slot(("mask", u))
                    v = view(("mask", u)).bitcast(BF16)
                    for j in range(i + 1):
                        mm = pe.transpose(v[:, j * P:(j + 1) * P], bias[:, j * P:(j + 1) * P], identb[:])
                    mm.then_inc(filled["mask"], 1)

                def max_scores(u):
                    g, s = st.groups[u // GT], u % GT
                    if s == 0:
                        pe.wait_ge(q_in[g % 2], 16 * len(Q_SLOTS) * (1 if g >= NG - 2 else 2))
                    for h in range(H):
                        for k, w in st.parts(u):
                            r = slot(("max", u, h, k))
                            for c in range(0, w, 512):
                                cw = min(512, w - c)
                                mm = pe.matmul(r[:, c // 512, 0:cw], Q99[g % 2][0:KR, h, s * P:(s + 1) * P], K99[0:KR, h, k * PW + c:k * PW + c + cw], start=True, stop=True)
                            mm.then_inc(filled["max"], 1)

                def turn_m(u):
                    pe.wait_ge(msplit_done, u + 1)
                    if u >= GT:
                        pe.wait_ge(normed, GT * (u - GT + 1))
                    elif u >= 1:
                        pe.wait_ge(mT_done, u)
                    pe.transpose(pX[0:PARTS * H, :].bitcast(BF16)[:, 0:P], msplit[:, :, :].rearrange("p r h -> p (r h)"), identb[:]).then_inc(m_turned, 1)

                def project(u):
                    n = st.groups.index(st.attend(u)[0])
                    pe.wait_ge(normed, GT * (u - GT + 1))
                    if u < NT:
                        pe.wait_ge(mT_done, u + 1)
                    for k in range(KD):
                        if k:
                            pe.wait_ge(otT_done, KD * n + k)
                        for t in range(GT):
                            mm = pe.transpose(pX[:, t * P:(t + 1) * P], otok[:, t, k * P:(k + 1) * P], identf[:])
                        mm.then_inc(ot_turned, 1)
                    pe.wait_ge(otT_done, KD * (n + 1))
                    slot(("out", u))
                    v = view(("out", u))
                    for t in range(GT):
                        for k in range(KD):
                            mm = pe.matmul(v[:, t * D:(t + 1) * D], otokT[:, k, t * P:(t + 1) * P], woT[:, k, :], start=(k == 0), stop=(k == KD - 1))
                    mm.then_inc(filled["out"], 1)

                dots(0)
                for u in range(st.n):
                    if u >= GT:
                        attend(u)
                    if u < NT:
                        turn_mask(u)
                        max_scores(u)
                        turn_m(u)
                    if u >= GT and st.attend(u)[1] == NQ - 1:
                        project(u)
                    if u + 1 < NT:
                        dots(u + 1)

        clear(nc, sems)


def feed_forward(nc, b, w, consts, x2D, out):
    identf, _, sign = consts
    D2, D4 = D // 2, D // 4
    with ExitStack() as ctx:
        sb = lambda n, s, d: ctx.enter_context(nc.sbuf_tensor(n, s, d))
        ps = lambda n, s, d: ctx.enter_context(nc.psum_tensor(n, s, d))
        sems = []

        def sem(n):
            sems.append(ctx.enter_context(nc.semaphore(n)))
            return sems[-1]

        x2 = sb("x2", [P, NT, D], FP32)
        hn = sb("hn", [P, 2, D], FP32)
        stats = sb("fstats", [P, NT, 6], FP32)
        mv = sb("fmv", [P, NT, 2], FP32)
        sd = sb("fsd", [P, NT], FP32)
        rstd = sb("frstd", [P, NT], FP32)
        eps = sb("feps", [P, 1], FP32)
        hT = sb("hT", [P, KD, S], FP32)
        h1 = sb("h1", [P, 2, KD, GW], FP32)
        h2 = sb("h2", [P, 2, GW], FP32)
        h3 = sb("h3", [D4, 2, GW], FP32)
        th = sb("th", [P, 2, GW], FP32)
        tw = sb("tw", [P, 2, 2, GW], FP32)
        w1 = sb("w1", [P, KD, D], FP32)
        w2 = sb("w2", [P, KD, D2], FP32)
        w3 = sb("w3", [P, D4], FP32)
        w4 = sb("w4", [D4, P], FP32)
        g1 = sb("g1", [P, KD, D2], FP32)
        g2 = sb("g2", [P, D4], FP32)
        g3 = sb("g3", [D4, P], FP32)
        g3c = sb("g3c", [D4, 1], FP32)
        w4c = sb("w4c", [D4, 1], FP32)
        b1 = sb("b1", [P, KD], FP32)
        b2 = sb("b2", [P, 1], FP32)
        b3 = sb("b3", [D4, 1], FP32)
        b4 = sb("b4", [P, 1], FP32)
        c1 = sb("c1", [P, 1], FP32)
        c2 = sb("c2", [D4, 1], FP32)
        c3 = sb("c3", [P, 1], FP32)
        ar = sb("ar", [P, 1], FP32)
        half = sb("half", [P, 2], FP32)
        mean = sb("mean", [P, KD], FP32)
        gh1 = sb("gh1", [P, 1], FP32)
        gh2 = sb("gh2", [D4, 1], FP32)
        gt = sb("gt", [P, 1], FP32)
        base = sb("base", [P, 1], FP32)
        slope = sb("slope", [P, 1], FP32)
        pW = [ps(f"pW{k}", [P, 512], FP32) for k in range(8)]
        x2_in = [sem(f"x2_in{g}") for g in range(NG)]
        w_in, eps_set, stats_done, mv_done, sd_done, rstd_done = (sem(n) for n in ("fw_in", "feps_set", "fstats_done", "fmv_done", "fsd_done", "frstd_done"))
        hn_done, h_turned, hT_done, half_done, mean_done = (sem(n) for n in ("hn_done", "h_turned", "hT_done", "half_done", "mean_done"))
        gz1, gz2, gz3, ga1, ga2, ga3, coef = (sem(n) for n in ("gz1", "gz2", "gz3", "ga1", "ga2", "ga3", "coef"))
        z1, z2, z3, z4, a1, a2, a3, a4 = (sem(n) for n in ("z1", "z2", "z3", "z4", "a1", "a2", "a3", "a4"))
        c_done, tw_done, h_new, y_turned, y_done, y_out = (sem(n) for n in ("c_done", "tw_done", "h_new", "y_turned", "y_done", "y_out"))
        NC = CYCLES * NG

        with nc.Block() as block:

            @block.sync
            def _(sp):
                x2v = x2D.rearrange("(t p) d -> p t d", p=P)
                for g in range(NG):
                    sp.dma_start(x2[:, g * GT:(g + 1) * GT, :], x2v[:, g * GT:(g + 1) * GT, :]).then_inc(x2_in[g], 16)
                col = lambda a: a.rearrange("(p o) -> p o", o=1)
                kp = lambda a: a.rearrange("(k p) n -> p k n", p=P)
                loads = [(g1[:], kp(w["g1"])), (g2[:], w["g2"]), (g3c[:], w["g3"]), (c1[:], col(w["c1"])),
                         (c2[:], col(w["c2"])), (c3[:], w["c3"].partition_broadcast(P)), (ar[:], w["ar"].partition_broadcast(P)),
                         (b4[:], w["b4"].partition_broadcast(P)), (w1[:], kp(w["w1"])), (w2[:], kp(w["w2"])), (w3[:], w["w3"]),
                         (w4c[:], w["w4"]), (b1[:, 0:1], col(w["b1"][0:P])), (b1[:, 1:2], col(w["b1"][P:D])), (b2[:], col(w["b2"])), (b3[:], col(w["b3"]))]
                for dst, src in loads:
                    sp.dma_start(dst, src).then_inc(w_in, 16)
                ob = out.rearrange("(b t p) d -> b p t d", b=B, p=P)
                for g in range(NG):
                    sp.wait_ge(y_done, GT * (g + 1))
                    sp.dma_start(ob[bass.ds(b, 1), :, g * GT:(g + 1) * GT, :].rearrange("o p t d -> (o p) t d"), x2[:, g * GT:(g + 1) * GT, :]).then_inc(y_out, 16)
                sp.wait_ge(y_out, 16 * NG)

            NW = 16

            @block.vector
            def _(dve):
                dve.memset(eps[:], EPS).then_inc(eps_set, 1)
                for i in range(NT):
                    if i % GT == 0:
                        dve.wait_ge(x2_in[i // GT], 16)
                    dve.bn_stats(out=stats[:, i, :], in_=x2[:, i, :]).then_inc(stats_done, 1)
                for i in range(NT):
                    dve.wait_ge(stats_done, i + 1)
                    dve.bn_aggr(out=mv[:, i, :], in_=stats[:, i, :]).then_inc(mv_done, 1)
                dve.wait_ge(w_in, 16 * NW)
                dve.tensor_scalar(half[:, 0:1], b4[:], 0.5, None, ALU.mult).then_inc(half_done, 1)
                dve.tensor_scalar(half[:, 1:2], c3[:], 0.5, None, ALU.mult).then_inc(half_done, 1)
                dve.tensor_copy(w4[:], w4c[:, 0:1].to_broadcast([D4, P])).then_inc(half_done, 1)
                dve.tensor_copy(g3[:], g3c[:, 0:1].to_broadcast([D4, P])).then_inc(half_done, 1)
                dve.tensor_scalar(slope[:], ar[:], sign[:, 0:1], 0.3, ALU.mult, ALU.mult).then_inc(half_done, 1)
                dve.wait_ge(sd_done, 1)
                dve.reciprocal(rstd[:], sd[:]).then_inc(rstd_done, 1)
                dve.wait_ge(rstd_done, 1)
                for i in range(NT):
                    if i >= 2:
                        dve.wait_ge(h_turned, i - 1)
                    dve.tensor_scalar(hn[:, i % 2, :], x2[:, i, :], mv[:, i, 0:1], rstd[:, i:i + 1], ALU.subtract, ALU.mult).then_inc(hn_done, 1)
                dve.wait_ge(hT_done, NT)
                dve.tensor_reduce(mean[:], hT[:], AX.X, ALU.add).then_inc(mean_done, 1)
                dve.wait_ge(ga3, 1)
                dve.tensor_scalar(gt[:], gt[:], ar[:, 0:1], 0.7, ALU.mult, ALU.mult).then_inc(coef, 1)
                dve.wait_ge(coef, 1)
                dve.tensor_scalar(base[:], gt[:], 0.1, sign[:, 0:1], ALU.add, ALU.mult).then_inc(coef, 1)
                dve.wait_ge(coef, 2)
                dve.wait_ge(half_done, 5)
                for n in range(NC):
                    g = n % NG
                    k = n % 2
                    cols = slice(g * GW, (g + 1) * GW)
                    dve.wait_ge(a4, n + 1)
                    dve.tensor_scalar(th[:, k, :], th[:, k, :], slope[:, 0:1], base[:, 0:1], ALU.mult, ALU.add).then_inc(c_done, 1)
                    dve.wait_ge(c_done, n + 1)
                    if n >= NG:
                        dve.wait_ge(h_new, 2 * (n - NG + 1))
                    if n >= 2:
                        dve.wait_ge(h_new, 2 * (n - 1))
                    dve.tensor_tensor(tw[:, k, 0, :], th[:, k, :], hT[:, 1, cols], ALU.mult).then_inc(tw_done, 1)
                    dve.tensor_tensor(tw[:, k, 1, :], th[:, k, :], hT[:, 0, cols], ALU.mult).then_inc(tw_done, 1)
                    dve.wait_ge(tw_done, 2 * (n + 1))
                    dve.tensor_tensor(hT[:, 0, cols], hT[:, 0, cols], tw[:, k, 0, :], ALU.add).then_inc(h_new, 1)
                    dve.tensor_tensor(hT[:, 1, cols], hT[:, 1, cols], tw[:, k, 1, :], ALU.subtract).then_inc(h_new, 1)
                for i in range(NT):
                    dve.wait_ge(y_turned, i + 1)
                    dve.tensor_tensor(x2[:, i, :], pW[i % 2][:, 0:D], x2[:, i, :], ALU.add).then_inc(y_done, 1)

            @block.scalar
            def _(act):
                act.wait_ge(mv_done, NT)
                act.wait_ge(eps_set, 1)
                act.activation(sd[:], mv[:, :, 1], ACT.Sqrt, bias=eps[:, 0:1]).then_inc(sd_done, 1)
                for i in range(NT):
                    act.wait_ge(h_turned, i + 1)
                    act.activation(hT[:, :, i * P:(i + 1) * P], pW[i % 2][:, 0:D].rearrange("p (k q) -> p k q", q=P), ACT.Copy).then_inc(hT_done, 1)
                act.wait_ge(w_in, 16 * NW)
                act.wait_ge(gz1, 1)
                act.activation(gh1[:], pW[2][:, 0:1], ACT.Gelu, bias=c1[:, 0:1], scale=1.0 / S).then_inc(ga1, 1)
                act.wait_ge(gz2, 1)
                act.activation(gh2[:], pW[3][0:D4, 0:1], ACT.Gelu, bias=c2[:, 0:1]).then_inc(ga2, 1)
                act.wait_ge(gz3, 1)
                act.wait_ge(half_done, 5)
                act.activation(gt[:], pW[2][:, 0:1], ACT.Tanh, bias=half[:, 1:2], scale=0.5).then_inc(ga3, 1)
                for m in range(NC + 3):
                    if m < NC:
                        n, k = m, m % 2
                        for q in range(KD):
                            act.wait_ge(z1, 2 * n + q + 1)
                            if n >= 2:
                                act.wait_ge(z2, n - 1)
                            act.activation(h1[:, k, q, :], pW[q][:], ACT.Gelu, bias=b1[:, q:q + 1]).then_inc(a1, 1)
                    if 1 <= m <= NC:
                        n = m - 1
                        k = n % 2
                        act.wait_ge(z2, n + 1)
                        if n >= 2:
                            act.wait_ge(z3, n - 1)
                        act.activation(h2[:, k, :], pW[2 + k][:], ACT.Gelu, bias=b2[:, 0:1]).then_inc(a2, 1)
                    if 2 <= m <= NC + 1:
                        n = m - 2
                        k = n % 2
                        act.wait_ge(z3, n + 1)
                        if n >= 2:
                            act.wait_ge(z4, n - 1)
                        act.activation(h3[:, k, :], pW[4 + k][0:D4, :], ACT.Gelu, bias=b3[:, 0:1]).then_inc(a3, 1)
                    if m >= 3:
                        n = m - 3
                        k = n % 2
                        act.wait_ge(z4, n + 1)
                        if n >= 2:
                            act.wait_ge(tw_done, 2 * (n - 1))
                        act.activation(th[:, k, :], pW[6 + k][:], ACT.Tanh, bias=half[:, 0:1], scale=0.5).then_inc(a4, 1)

            @block.tensor
            def _(pe):
                for i in range(NT):
                    pe.wait_ge(hn_done, i + 1)
                    if i >= 2:
                        pe.wait_ge(hT_done, i - 1)
                    for k in range(KD):
                        mm = pe.transpose(pW[i % 2][:, k * P:(k + 1) * P], hn[:, i % 2, k * P:(k + 1) * P], identf[:])
                    mm.then_inc(h_turned, 1)
                pe.wait_ge(w_in, 16 * NW)
                pe.wait_ge(mean_done, 1)
                pe.wait_ge(half_done, 5)
                for k in range(KD):
                    mm = pe.matmul(pW[2][:, 0:1], g1[:, k, :], mean[:, k:k + 1], start=(k == 0), stop=(k == KD - 1))
                mm.then_inc(gz1, 1)
                pe.wait_ge(ga1, 1)
                pe.matmul(pW[3][0:D4, 0:1], g2[:], gh1[:], start=True, stop=True).then_inc(gz2, 1)
                pe.wait_ge(ga2, 1)
                pe.matmul(pW[2][:, 0:1], g3[:], gh2[:], start=True, stop=True).then_inc(gz3, 1)
                pe.wait_ge(ga3, 1)
                for m in range(NC + 3):
                    if m < NC:
                        n = m
                        cols = slice((n % NG) * GW, (n % NG + 1) * GW)
                        if n >= NG:
                            pe.wait_ge(h_new, 2 * (n - NG + 1))
                        else:
                            pe.wait_ge(hT_done, NT)
                        for q in range(KD):
                            if n >= 1:
                                pe.wait_ge(a1, 2 * (n - 1) + q + 1)
                            for k in range(KD):
                                mm = pe.matmul(pW[q][:], w1[:, k, q * P:(q + 1) * P], hT[:, k, cols], start=(k == 0), stop=(k == KD - 1))
                            mm.then_inc(z1, 1)
                    if 1 <= m <= NC:
                        n = m - 1
                        pe.wait_ge(a1, 2 * (n + 1))
                        if n >= 2:
                            pe.wait_ge(a2, n - 1)
                        for k in range(KD):
                            mm = pe.matmul(pW[2 + n % 2][:], w2[:, k, :], h1[:, n % 2, k, :], start=(k == 0), stop=(k == KD - 1))
                        mm.then_inc(z2, 1)
                    if 2 <= m <= NC + 1:
                        n = m - 2
                        pe.wait_ge(a2, n + 1)
                        if n >= 2:
                            pe.wait_ge(a3, n - 1)
                        pe.matmul(pW[4 + n % 2][0:D4, :], w3[:], h2[:, n % 2, :], start=True, stop=True).then_inc(z3, 1)
                    if m >= 3:
                        n = m - 3
                        pe.wait_ge(a3, n + 1)
                        if n >= 2:
                            pe.wait_ge(a4, n - 1)
                        pe.matmul(pW[6 + n % 2][:], w4[:], h3[:, n % 2, :], start=True, stop=True).then_inc(z4, 1)
                for i in range(NT):
                    pe.wait_ge(h_new, 2 * (NC - NG + i // GT + 1))
                    if i >= 2:
                        pe.wait_ge(y_done, i - 1)
                    else:
                        pe.wait_ge(a1, 2 * NC)
                    for k in range(KD):
                        mm = pe.transpose(pW[i % 2][:, k * P:(k + 1) * P], hT[:, k, i * P:(i + 1) * P], identf[:])
                    mm.then_inc(y_turned, 1)

        clear(nc, sems)


def build(nc, x, w, tabs, out):
    with ExitStack() as ctx:
        sb = lambda n, s, d: ctx.enter_context(nc.sbuf_tensor(n, s, d))
        K99 = sb("K99", [KM, H, S], BF16)
        V = sb("V", [P, NT, VP], FP32)
        kiT = sb("kiT", [P, S], FP32)
        wi = sb("wi", [P, NT, HI], FP32)
        identf = sb("identf", [P, P], FP32)
        identb = sb("identb", [P, P], BF16)
        woT = sb("woT", [P, KD, D], FP32)
        sign = sb("sign", [P, 1], FP32)
        qkD = [nc.dram_tensor(f"qk{c}_parts", (H * PARTS * DK, S), BF16, kind="Internal").ap() for c in range(2)]
        qiD = nc.dram_tensor("qi_scratch", (P, 2, S), FP32, kind="Internal").ap()
        x2D = nc.dram_tensor("x2_scratch", (S, D), FP32, kind="Internal").ap()
        zeroed = ctx.enter_context(nc.semaphore("zeroed"))
        const_done = ctx.enter_context(nc.semaphore("const_done"))
        ones_set = ctx.enter_context(nc.semaphore("ones_set"))
        wo_in = ctx.enter_context(nc.semaphore("wo_in"))
        with nc.Block() as block:

            @block.sync
            def _(sp):
                sp.dma_start(woT[:], w["oT"].rearrange("(k p) n -> p k n", p=P)).then_inc(wo_in, 16)
                sp.wait_ge(wo_in, 16)

            @block.gpsimd
            def _(pool):
                pool.memset(identf[:], 0.0).then_inc(zeroed, 1)
                pool.memset(identb[:], 0.0).then_inc(zeroed, 1)
                pool.memset(sign[:], 1.0).then_inc(zeroed, 1)
                pool.wait_ge(zeroed, 3)
                for m in (identf, identb):
                    pool.affine_select(out=m[:], in_=m[:], compare_op=ALU.not_equal, fill=1.0, base=0,
                                       pattern=[[-1, P]], channel_multiplier=1).then_inc(const_done, 1)
                pool.affine_select(out=sign[:], in_=sign[:], compare_op=ALU.is_gt, fill=-1.0, base=D // 4,
                                   pattern=[[0, 1]], channel_multiplier=-1).then_inc(const_done, 1)
                pool.wait_ge(const_done, 3)

            @block.vector
            def _(dve):
                dve.memset(V[:], 1.0).then_inc(ones_set, 1)
                dve.memset(K99[KR:KM, :, :], 1.0).then_inc(ones_set, 1)
                dve.wait_ge(ones_set, 2)

        clear(nc, [zeroed, const_done, ones_set, wo_in])
        keep = (K99, V, kiT, wi)
        with nc.Fori(0, B) as b:
            prepare(nc, b, x, w, tabs, (identf, identb), keep, (qkD, qiD))
            attention(nc, b, x, (identf, identb, woT), keep, (qkD, qiD, x2D))
            feed_forward(nc, b, w, (identf, identb, sign), x2D, out)


_TURNED = {'L0_attn_w_qkv': 'qkvT', 'L0_attn_w_o': 'oT', 'L0_attn_w_qi': 'qiT', 'L0_attn_w_ki': 'kiT', 'L0_attn_w_wi': 'wiT'}
_PLAIN = {'L0_ffn_cn_w1': 'w1', 'L0_ffn_cn_b1': 'b1', 'L0_ffn_cn_w2': 'w2', 'L0_ffn_cn_b2': 'b2', 'L0_ffn_cn_w3': 'w3',
          'L0_ffn_cn_b3': 'b3', 'L0_ffn_cn_w4': 'w4', 'L0_ffn_cn_b4': 'b4', 'L0_ffn_gc_w1': 'g1', 'L0_ffn_gc_b1': 'c1',
          'L0_ffn_gc_w2': 'g2', 'L0_ffn_gc_b2': 'c2', 'L0_ffn_gc_w3': 'g3', 'L0_ffn_gc_b3': 'c3', 'L0_ffn_adaptive_range': 'ar'}


def kernel(**inputs):
    import numpy as _np
    import concourse.bacc as _bacc
    from concourse import mybir as _mybir
    from concourse.bass_utils import run_bass_kernel_spmd as _run

    nc = _bacc.Bacc("TRN2", target_bir_lowering=False, num_devices=1)
    arrays = {}

    def tensor(name, a):
        a = _np.ascontiguousarray(a)
        arrays[name] = a
        return nc.dram_tensor(name, a.shape, _mybir.dt.from_np(a.dtype), kind="ExternalInput").ap()

    xs = _np.asarray(inputs['L0_attn_x'])
    x = tensor("x_dram", xs.reshape(B * S, D))
    w = {k: tensor(f"{k}_dram", _np.asarray(inputs[n]).T) for n, k in _TURNED.items()}
    w.update({k: tensor(f"{k}_dram", _np.asarray(inputs[n])) for n, k in _PLAIN.items()})
    tabs = [tensor(f"table{k}_dram", t) for k, t in enumerate(rope_tables())]
    out = nc.dram_tensor("out_dram", (B * S, D), _mybir.dt.float32, kind="ExternalOutput").ap()
    build(nc, x, w, tabs, out)
    r = _run(nc, [arrays], core_ids=[0])
    return r.results[0]["out_dram"].reshape(xs.shape)
```

```python
import concourse.bass as bass
import numpy as np
from concourse import mybir
from contextlib import ExitStack

FP32 = mybir.dt.float32
BF16 = mybir.dt.bfloat16
FP8 = mybir.dt.float8e4
ALU = mybir.AluOpType
ACT = mybir.ActivationFunctionType
AX = mybir.AxisListType

B, S, D = 2, 2048, 256
H, DK = 16, 16
HI, DI = 4, 64
TOPK = 128
EPS = 1e-5
P = 128
NT = S // P
GT = 4
GW = GT * P
NG = NT // GT
KD = D // P
QUAD = 4
NQ = H // QUAD
PW = 1024
RING = 3
PARTS = 3
Q_SLOTS = (0, 0, 0, 1, 1, 2)
K_SLOTS = (0, 1, 2, 0, 1, 0)
KR = len(Q_SLOTS) * DK
KM = KR + PARTS
VW = DK + 1
VP = H * VW + 32 - VW
CAUSAL = -3.3e38
TAKEN = -3.4e38
HIDE = -1.0e30
CYCLES = 3
CHOOSE_US = 33 / 960
CHUNK_US = 2.9


def rope_tables():
    inv = (np.float32(1.0) / np.float32(10000.0) ** (np.arange(0, DK, 2, dtype=np.float32) / np.float32(DK))).astype(np.float32)
    ang = (np.arange(S, dtype=np.float32)[:, None] * inv).astype(np.float32)
    lay = lambda a: np.ascontiguousarray(a.astype(np.float32).reshape(NT, P, -1).transpose(1, 0, 2))
    cos, sin = np.cos(ang), np.sin(ang)
    return lay(np.repeat(cos, 2, axis=1)), lay(sin), lay(-sin)


class Steps:

    def __init__(self):
        self.groups = list(range(NG))[::-1]
        self.n = NT + GT
        self.plan = [self.events(u) for u in range(self.n)]
        self.slot, self.order, self.count = {}, [], {}
        for k, _ in self.parts(0):
            for hp in range(HI // 2):
                self.use_dots(0, k, hp)
        for u, events in enumerate(self.plan):
            for e in events:
                if e[0] == "a":
                    for p in range(2):
                        self.use("exp", ("exp", u, e[1], p))
                elif e[0] == "m":
                    self.use("max", ("max", u, *e[1:]))
                elif e[0] == "d":
                    self.use_dots(u + 1, *e[1:])
                elif e[0] == "mask":
                    self.use("mask", ("mask", u))
                elif e[0] == "project":
                    self.use("out", ("out", u - 1))
        self.use("out", ("out", self.n - 1))

    def events(self, u):
        a = self.attend(u)
        chunks = [("a", j) for j in range(GT * (a[0] + 1))] if a else []
        first = min(len(chunks), int(self.width(u) * CHOOSE_US / CHUNK_US)) if u < NT else 0
        maxima = [("m", h, k) for h in range(H) for k, _ in self.parts(u)] if u < NT else []
        dots = [("d", k, hp) for k, _ in self.parts(u + 1) for hp in range(HI // 2)] if u + 1 < NT and self.tile(u + 1) else []
        early = [((i + 0.5) / first, e) for i, e in enumerate(chunks[:first])]
        early += [(0.8 * i / len(dots), e) for i, e in enumerate(dots)]
        out = [e for _, e in sorted(early, key=lambda r: r[0])]
        if u > GT and self.attend(u - 1)[1] == NQ - 1:
            out.append(("project",))
        rest = [((i + 0.5) / len(maxima), e) for i, e in enumerate(maxima)]
        rest += [((i + 0.7) / (len(chunks) - first), e) for i, e in enumerate(chunks[first:])]
        out += [e for _, e in sorted(rest, key=lambda r: r[0])]
        if a:
            out.append(("end",))
        if u < NT:
            out += [("mask",), ("turn_m",)]
        if a:
            out.append(("turn_o",))
        return out

    def use_dots(self, u, k, hp):
        for h in (2 * hp, 2 * hp + 1):
            self.use("dot", ("dot", u, k, h))

    def use(self, kind, key):
        self.count[kind] = self.count.get(kind, 0) + 1
        self.slot[key] = (len(self.order) % RING, self.count[kind])
        self.order.append((kind, self.count[kind]))

    def tile(self, u):
        return GT * self.groups[u // GT] + u % GT

    def width(self, u):
        return P * (self.tile(u) + 1)

    def parts(self, u):
        n = self.width(u)
        return [(k, min(PW, n - k * PW)) for k in range((n + PW - 1) // PW)]

    def attend(self, u):
        return (self.groups[(u - GT) // GT], (u - GT) % GT) if u >= GT else None


def prepare(nc, b, x, w, tabs, consts, keep, scratch):
    K99, V, kiT, wi = keep
    qkD, qiD = scratch
    identf, identb = consts
    with ExitStack() as ctx:
        sb = lambda n, s, d: ctx.enter_context(nc.sbuf_tensor(n, s, d))
        ps = lambda n, s, d: ctx.enter_context(nc.psum_tensor(n, s, d))
        sems = []

        def sem(n):
            sems.append(ctx.enter_context(nc.semaphore(n)))
            return sems[-1]

        xn = sb("xn", [P, NT, D], FP32)
        stats = sb("stats", [P, NT, 6], FP32)
        mv = sb("mv", [P, NT, 2], FP32)
        sd = sb("sd", [P, NT], FP32)
        rstd = sb("rstd", [P, NT], FP32)
        eps = sb("eps", [P, 1], FP32)
        xnT = sb("xnT", [P, KD, S], FP32)
        wqkv = sb("wqkv", [P, KD, 3 * D + HI], FP32)
        wqi = sb("wqi", [P, KD, HI * DI], FP32)
        wki = sb("wki", [P, KD, 2 * DI], FP32)
        cos = sb("cos", [P, NT, DK], FP32)
        sin = sb("sin", [P, NT, DK // 2], FP32)
        nsin = sb("nsin", [P, NT, DK // 2], FP32)
        t1 = sb("t1", [P, 2, 2 * D], FP32)
        t2 = sb("t2", [P, 2, 2 * D], FP32)
        rot = sb("rot", [P, 3, 2 * D], FP32)
        rem = sb("rem", [P, 3, 2 * D], FP32)
        split = sb("split", [P, 3, 2 * H * PARTS * DK], BF16)
        stage = sb("stage", [2 * PARTS * DK, 2, 2, H // 2, GW], BF16)
        qi = sb("qi", [P, 2, 2, GW], FP32)
        pT = [ps(f"pT{k}", [P, KD, P], FP32) for k in range(2)]
        pA = [ps(f"pA{k}", [P, 512], FP32) for k in range(2)]
        pB = [ps(f"pB{k}", [P, 512], FP32) for k in range(2)]
        pS = [ps(f"pS{k}", [P, H // 2, P], BF16) for k in range(2)]
        x_in = [sem(f"x_in{g}") for g in range(NG)]
        w_in, wi_in, tab_in = sem("w_in"), sem("wi_in"), sem("tab_in")
        eps_set, stats_done, mv_done, sd_done, rstd_done = (sem(n) for n in ("eps_set", "stats_done", "mv_done", "sd_done", "rstd_done"))
        xn_done, turned, xT_done = sem("xn_done"), sem("turned"), sem("xT_done")
        qkv_done, v_taken, t_done = sem("qkv_done"), sem("v_taken"), sem("t_done")
        rot_done, hi_done, rem_done, mid_done, lo_done = (sem(n) for n in ("rot_done", "hi_done", "rem_done", "mid_done", "lo_done"))
        split_turned, staged, index_done, index_taken = (sem(n) for n in ("split_turned", "staged", "index_done", "index_taken"))
        stored = [sem(f"stored{k}") for k in range(2)]
        qi_out, k_in = [sem(f"qi_out{k}") for k in range(2)], sem("k_in")

        wide = lambda a, i: a[:, i % 3, :].rearrange("p (h d) -> p h d", d=DK)
        parts = lambda i: split[:, i % 3, :].rearrange("p (h s d) -> p h s d", s=PARTS, d=DK)

        with nc.Block() as block:

            @block.sync
            def _(sp):
                xb = x.rearrange("(b t p) d -> b p t d", b=B, p=P)
                for g in range(NG):
                    sp.dma_start(xn[:, g * GT:(g + 1) * GT, :], xb[bass.ds(b, 1), :, g * GT:(g + 1) * GT, :].rearrange("o p t d -> (o p) t d")).then_inc(x_in[g], 16)
                sp.dma_start(wqkv[:, :, 0:3 * D], w["qkvT"].rearrange("(k p) n -> p k n", p=P)).then_inc(w_in, 16)
                sp.dma_start(wqkv[:, :, 3 * D:], w["wiT"].rearrange("(k p) n -> p k n", p=P)).then_inc(w_in, 16)
                for a, t in zip((cos, sin, nsin), tabs):
                    sp.dma_start(a[:], t).then_inc(tab_in, 16)
                sp.dma_start(wqi[:], w["qiT"].rearrange("(k p) n -> p k n", p=P)).then_inc(wi_in, 16)
                for c in range(2):
                    sp.dma_start(wki[:, :, c * DI:(c + 1) * DI], w["kiT"].rearrange("(k p) n -> p k n", p=P)).then_inc(wi_in, 16)
                def load_keys(g):
                    sp.wait_ge(stored[g % 2], 32 * (g // 2 + 1))
                    for r, part in enumerate(K_SLOTS):
                        sp.dma_start(K99[r * DK:(r + 1) * DK, :, g * GW:(g + 1) * GW],
                                     qkD[1].rearrange("(h s d) t -> s d h t", s=PARTS, d=DK)[part][:, :, g * GW:(g + 1) * GW]).then_inc(k_in, 16)

                for g in range(NG):
                    sp.wait_ge(staged, 2 * GT * (g + 1))
                    for c in range(2):
                        sp.dma_start(qkD[c].rearrange("(hp p) t -> p hp t", p=2 * PARTS * DK)[:, :, g * GW:(g + 1) * GW],
                                     stage[:, g % 2, c]).then_inc(stored[g % 2], 16)
                    if g >= 1:
                        load_keys(g - 1)
                load_keys(NG - 1)
                for g in range(NG):
                    sp.wait_ge(index_taken, 3 * (g + 1))
                    sp.dma_start(qiD[:, :, g * GW:(g + 1) * GW], qi[:, g % 2]).then_inc(qi_out[g % 2], 16)
                sp.wait_ge(k_in, 16 * len(K_SLOTS) * NG)
                for k in range(2):
                    sp.wait_ge(qi_out[k], 16 * (NG // 2))

            @block.vector
            def _(dve):
                dve.memset(eps[:], EPS).then_inc(eps_set, 1)
                for i in range(NT):
                    if i % GT == 0:
                        dve.wait_ge(x_in[i // GT], 16)
                    dve.bn_stats(out=stats[:, i, :], in_=xn[:, i, :]).then_inc(stats_done, 1)
                for i in range(NT):
                    dve.wait_ge(stats_done, i + 1)
                    dve.bn_aggr(out=mv[:, i, :], in_=stats[:, i, :]).then_inc(mv_done, 1)
                dve.wait_ge(sd_done, 1)
                dve.reciprocal(rstd[:], sd[:]).then_inc(rstd_done, 1)
                dve.wait_ge(rstd_done, 1)
                for i in range(NT):
                    dve.tensor_scalar(xn[:, i, :], xn[:, i, :], mv[:, i, 0:1], rstd[:, i:i + 1], ALU.subtract, ALU.mult).then_inc(xn_done, 1)
                dve.wait_ge(tab_in, 16 * len(tabs))

                def rope(i):
                    q = pA[i % 2][:, :].rearrange("p (h d) -> p h d", d=DK)
                    a = t1[:, i % 2, :].rearrange("p (h d) -> p h d", d=DK)
                    c = t2[:, i % 2, :].rearrange("p (h d) -> p h d", d=DK)
                    bc = lambda t, n: t[:, i, :].unsqueeze(1).to_broadcast([P, 2 * H, n])
                    dve.wait_ge(qkv_done, i + 1)
                    if i >= 2:
                        dve.wait_ge(rot_done, i - 1)
                    dve.tensor_tensor(a, q, bc(cos, DK), ALU.mult).then_inc(t_done, 1)
                    dve.tensor_tensor(c[:, :, 0::2], q[:, :, 1::2], bc(nsin, DK // 2), ALU.mult).then_inc(t_done, 1)
                    dve.tensor_tensor(c[:, :, 1::2], q[:, :, 0::2], bc(sin, DK // 2), ALU.mult).then_inc(t_done, 1)

                def take_parts(i):
                    g, t = i // GT, i % GT
                    dve.wait_ge(split_turned, 2 * (i + 1))
                    if t == 0 and g >= 2:
                        dve.wait_ge(stored[g % 2], 32 * (g // 2))
                    for c in range(2):
                        dve.tensor_copy(stage[:, g % 2, c, :, t * P:(t + 1) * P], pS[c][0:2 * PARTS * DK, :, :]).then_inc(staged, 1)

                for i in range(NT + 3):
                    if i < NT:
                        rope(i)
                    if i >= 3:
                        take_parts(i - 3)

            @block.gpsimd
            def _(pool):
                for i in range(NT + 2):
                    if i < NT:
                        pool.wait_ge(t_done, 3 * (i + 1))
                        if i >= 3:
                            pool.wait_ge(rem_done, i - 2)
                            pool.wait_ge(hi_done, i - 2)
                        pool.tensor_tensor(rot[:, i % 3, :], t1[:, i % 2, :], t2[:, i % 2, :], ALU.add).then_inc(rot_done, 1)
                    if 1 <= i <= NT:
                        k = i - 1
                        pool.wait_ge(hi_done, k + 1)
                        pool.wait_ge(rot_done, k + 1)
                        if k >= 3:
                            pool.wait_ge(lo_done, k - 2)
                            pool.wait_ge(mid_done, k - 2)
                        pool.tensor_tensor(wide(rem, k), wide(rot, k), parts(k)[:, :, 0, :], ALU.subtract).then_inc(rem_done, 1)
                    if i >= 2:
                        k = i - 2
                        pool.wait_ge(mid_done, k + 1)
                        pool.wait_ge(rem_done, k + 1)
                        pool.tensor_tensor(parts(k)[:, :, 2, :], wide(rem, k), parts(k)[:, :, 1, :], ALU.subtract).then_inc(lo_done, 1)

            @block.scalar
            def _(act):
                act.wait_ge(mv_done, NT)
                act.wait_ge(eps_set, 1)
                act.activation(sd[:], mv[:, :, 1], ACT.Sqrt, bias=eps[:, 0:1]).then_inc(sd_done, 1)
                for i in range(NT + 2):
                    if i < NT:
                        act.wait_ge(turned, i + 1)
                        act.activation(xnT[:, :, i * P:(i + 1) * P], pT[i % 2][:], ACT.Copy).then_inc(xT_done, 1)
                    if 1 <= i <= NT:
                        k = i - 1
                        act.wait_ge(qkv_done, k + 1)
                        act.activation(V[:, k, 0:H * VW].rearrange("p (h d) -> p h d", d=VW)[:, :, 0:DK],
                                       pB[k % 2][:, 0:D].rearrange("p (h d) -> p h d", d=DK), ACT.Copy).then_inc(v_taken, 1)
                        act.activation(wi[:, k, :], pB[k % 2][:, D:D + HI], ACT.Copy).then_inc(v_taken, 1)
                        act.wait_ge(rot_done, k + 1)
                        if k >= 3:
                            act.wait_ge(split_turned, 2 * (k - 2))
                        act.activation(parts(k)[:, :, 0, :], wide(rot, k), ACT.Copy).then_inc(hi_done, 1)
                    if i >= 2:
                        k = i - 2
                        act.wait_ge(rem_done, k + 1)
                        act.activation(parts(k)[:, :, 1, :], wide(rem, k), ACT.Copy).then_inc(mid_done, 1)
                banks = pA + pB
                for n in range(3 * NG):
                    g, m = n // 3, n % 3
                    act.wait_ge(index_done, n + 1)
                    if m == 0 and g >= 2:
                        act.wait_ge(qi_out[g % 2], 16 * (g // 2))
                    dst = kiT[:, g * GW:(g + 1) * GW] if m == 2 else qi[:, g % 2, m, :]
                    act.activation(dst, banks[n % 4][:], ACT.Copy).then_inc(index_taken, 1)

            @block.tensor
            def _(pe):
                def turn(i):
                    pe.wait_ge(xn_done, i + 1)
                    if i >= 2:
                        pe.wait_ge(xT_done, i - 1)
                    for k in range(KD):
                        mm = pe.transpose(pT[i % 2][:, k, :], xn[:, i, k * P:(k + 1) * P], identf[:])
                    mm.then_inc(turned, 1)

                def project(i):
                    pe.wait_ge(xT_done, i + 1)
                    if i >= 2:
                        pe.wait_ge(t_done, 3 * (i - 1))
                        pe.wait_ge(v_taken, 2 * (i - 1))
                    for dst, c0, c1 in ((pA, 0, 2 * D), (pB, 2 * D, 3 * D + HI)):
                        for k in range(KD):
                            mm = pe.matmul(dst[i % 2][:, 0:c1 - c0], xnT[:, k, i * P:(i + 1) * P], wqkv[:, k, c0:c1],
                                           start=(k == 0), stop=(k == KD - 1))
                    mm.then_inc(qkv_done, 1)

                def turn_parts(i):
                    pe.wait_ge(lo_done, i + 1)
                    for c in range(2):
                        if i >= 1:
                            pe.wait_ge(staged, 2 * (i - 1) + c + 1)
                        for hp in range(H // 2):
                            c0 = (c * (H // 2) + hp) * 2 * PARTS * DK
                            mm = pe.transpose(pS[c][0:2 * PARTS * DK, hp, :], split[:, i % 3, c0:c0 + 2 * PARTS * DK], identb[:])
                        mm.then_inc(split_turned, 1)

                turn(0)
                pe.wait_ge(w_in, 32)
                for i in range(NT + 3):
                    if i + 1 < NT:
                        turn(i + 1)
                    if i < NT:
                        project(i)
                    if i >= 3:
                        turn_parts(i - 3)
                pe.wait_ge(wi_in, 48)
                pe.wait_ge(t_done, 3 * NT)
                pe.wait_ge(v_taken, 2 * NT)
                banks = pA + pB
                for n in range(3 * NG):
                    g, m = n // 3, n % 3
                    if n >= 4:
                        pe.wait_ge(index_taken, n - 3)
                    for k in range(KD):
                        lhs = wki[:, k, :] if m == 2 else wqi[:, k, m * P:(m + 1) * P]
                        mm = pe.matmul(banks[n % 4][:], lhs, xnT[:, k, g * GW:(g + 1) * GW], start=(k == 0), stop=(k == KD - 1))
                    mm.then_inc(index_done, 1)

        clear(nc, sems)


def clear(nc, sems):
    nc.all_engine_barrier()
    for s in sems:
        nc.sync.sem_clear(s)
    nc.all_engine_barrier()


def attention(nc, b, x, consts, keep, scratch):
    K99, V, kiT, wi = keep
    qkD, qiD, x2D = scratch
    identf, identb, hide, woT = consts
    st = Steps()
    with ExitStack() as ctx:
        sb = lambda n, s, d: ctx.enter_context(nc.sbuf_tensor(n, s, d))
        ps = lambda n, s, d: ctx.enter_context(nc.psum_tensor(n, s, d))
        sems = []

        def sem(n):
            sems.append(ctx.enter_context(nc.semaphore(n)))
            return sems[-1]

        Q99 = [sb(f"Q99_{k}", [KM, H, GW], BF16) for k in range(2)]
        maskT = [sb(f"maskT{k}", [P, (NT if k == (NG - 1) % 2 else NT - GT), GW], FP8) for k in range(2)]
        sc = sb("sc", [P, 2, S], FP32)
        top8 = sb("top8", [P, 8], FP32)
        relu = sb("relu", [P, 3, PW], FP32)
        bias = sb("bias", [P, S], BF16)
        junk = sb("junk", [P, 2, PW], BF16)
        mx = sb("mx", [P, 2, H], FP32)
        mall = sb("mall", [P, H], FP32)
        mrem = sb("mrem", [P, H], FP32)
        msplit = sb("msplit", [P, PARTS, H], BF16)
        mT = sb("mT", [PARTS * H, GW], BF16)
        qi = sb("qi_t", [P, 2, 2, P], FP32)
        prob = sb("prob", [P, 4, 2, GW], FP32)
        oT = sb("oT", [P, GW], FP32)
        rsum = sb("rsum", [P, GT, QUAD], FP32)
        otok = sb("otok", [P, GT, D], FP32)
        otokT = relu[:, 0, :].rearrange("p (k q) -> p k q", k=KD)
        xg = sb("xg", [P, GT, D], FP32)
        ring = [ps(f"ring{k}", [P, 2, 512], FP32) for k in range(RING)]
        pO = ps("pO", [P, GW], FP32)
        pX = ps("pX", [P, 512], FP32)

        kinds = ("exp", "mask", "max", "out", "dot")
        filled = {k: sem(f"{k}_filled") for k in kinds}
        taken = {k: sem(f"{k}_taken") for k in kinds}
        q_in = [sem(f"q_in{k}") for k in range(2)]
        qm_in = sem("qm_in")
        qi_in = [sem(f"qi_in{k}") for k in range(2)]
        x_in, x2_out = sem("xg_in"), sem("x2_out")
        weighted = sem("weighted")
        summed, causal_done, chain = sem("summed"), sem("causal_done"), sem("chain")
        bias_done, msplit_done, m_turned, mT_done = sem("bias_done"), sem("msplit_done"), sem("m_turned"), sem("mT_done")
        pv_done, oT_done, o_turned, normed = sem("pv_done"), sem("oT_done"), sem("o_turned"), sem("normed")
        ot_turned, otT_done = sem("ot_turned"), sem("otT_done")

        def view(key, w=PW):
            return ring[st.slot[key][0]][:, :, :].rearrange("p a b -> p (a b)")[:, 0:w]

        def sums(c):
            return (HI - 1) * ((c - 1) // HI) + (c - 1) % HI

        chunks = [0]
        for u in range(st.n):
            a = st.attend(u)
            chunks.append(chunks[-1] + (GT * (a[0] + 1) if a else 0))
        dots_upto = {}
        for (key, (_, c)) in st.slot.items():
            if key[0] == "dot":
                dots_upto[key[1]] = max(dots_upto.get(key[1], 0), c)

        with nc.Block() as block:

            @block.sync
            def _(sp):
                xb = x.rearrange("(b t p) d -> b p t d", b=B, p=P)
                x2 = x2D.rearrange("(b t p) d -> b p t d", b=B, p=P)

                def load_q(g):
                    for r, part in enumerate(Q_SLOTS):
                        sp.dma_start(Q99[g % 2][r * DK:(r + 1) * DK, :, :],
                                     qkD[0].rearrange("(h s d) t -> s d h t", s=PARTS, d=DK)[part][:, :, g * GW:(g + 1) * GW]).then_inc(q_in[g % 2], 16)

                def load_qi(u):
                    i = st.tile(u)
                    sp.dma_start(qi[:, u % 2], qiD[:, :, i * P:(i + 1) * P]).then_inc(qi_in[u % 2], 16)

                def store(u):
                    g, _ = st.attend(u)
                    sp.wait_ge(taken["out"], st.slot[("out", u)][1])
                    sp.dma_start(x2[bass.ds(b, 1), :, g * GT:(g + 1) * GT, :].rearrange("o p t d -> (o p) t d"), xg[:]).then_inc(x2_out, 16)

                load_qi(0)
                load_qi(1)
                load_q(st.groups[0])
                load_q(st.groups[1])
                for u in range(st.n):
                    a = st.attend(u)
                    if u + 2 < NT and st.tile(u + 2):
                        sp.wait_ge(filled["dot"], dots_upto[u if st.tile(u) else u - 2])
                        load_qi(u + 2)
                    if u > GT and st.attend(u - 1)[1] == NQ - 1:
                        store(u - 1)
                    if a and a[1] == 1:
                        if a[0] != st.groups[0]:
                            sp.wait_ge(x2_out, 16 * st.groups.index(a[0]))
                        sp.dma_start(xg[:], xb[bass.ds(b, 1), :, a[0] * GT:(a[0] + 1) * GT, :].rearrange("o p t d -> (o p) t d")).then_inc(x_in, 16)
                    if u < NT and u % GT == GT - 1:
                        sp.wait_ge(mT_done, u + 1)
                        for r in range(PARTS):
                            sp.dma_start(Q99[st.groups[u // GT] % 2][KR + r:KR + r + 1, :, :], mT[r * H:(r + 1) * H, :]).then_inc(qm_in, 16)
                    if a and a[1] == NQ - 1:
                        if a[0] - 2 >= 0:
                            sp.wait_ge(pv_done, chunks[u + 1])
                            load_q(a[0] - 2)
                store(st.n - 1)
                sp.wait_ge(x2_out, 16 * NG)

            @block.vector
            def _(dve):
                links = [0]

                def link(ins):
                    links[0] += 1
                    ins.then_inc(chain, 1)
                    dve.wait_ge(chain, links[0])

                def choose(u):
                    i, n = st.tile(u), st.width(u)
                    if i == 0:
                        dve.wait_ge(filled["mask"], u)
                        dve.memset(bias[:, 0:n], 0.0).then_inc(bias_done, 1)
                        return
                    dve.wait_ge(causal_done, sum(1 for v in range(u + 1) if st.tile(v)))
                    scores = sc[:, u % 2, 0:n]
                    for _ in range(TOPK // 8):
                        link(dve.max(out=top8[:], in_=scores))
                        link(dve.match_replace(out=scores, in_to_replace=top8[:], in_values=scores, imm_value=TAKEN))
                    if u >= 1:
                        dve.wait_ge(filled["mask"], u)
                    dve.tensor_scalar(bias[:, 0:n], scores, TAKEN, HIDE, ALU.not_equal, ALU.mult).then_inc(bias_done, 1)

                def maximum(u, h, k):
                    w = dict(st.parts(u))[k]
                    key = ("max", u, h, k)
                    c = st.slot[key][1]
                    dve.wait_ge(filled["max"], c)
                    if c > 2:
                        dve.wait_ge(taken["max"], c - 2)
                    dve.tensor_tensor_reduce(out=junk[:, c % 2, 0:w], in0=view(key, w), in1=bias[:, k * PW:k * PW + w], scale=1.0, scalar=-3.0e38,
                                             op0=ALU.add, op1=ALU.max, accum_out=mx[:, k, h:h + 1]).then_inc(taken["max"], 1)

                def split_maxima(u):
                    dve.wait_ge(taken["max"], st.slot[("max", u, H - 1, len(st.parts(u)) - 1)][1])
                    last = mx[:, 0, :]
                    if len(st.parts(u)) == 2:
                        link(dve.tensor_tensor(mall[:], mx[:, 0, :], mx[:, 1, :], ALU.max))
                        last = mall[:]
                    link(dve.tensor_scalar(mrem[:], last, -1.0, None, ALU.mult))
                    if u >= 1:
                        dve.wait_ge(m_turned, u)
                    for r in range(PARTS - 1):
                        link(dve.tensor_copy(msplit[:, r, :], mrem[:]))
                        link(dve.tensor_tensor(mrem[:], mrem[:], msplit[:, r, :], ALU.subtract))
                    dve.tensor_copy(msplit[:, PARTS - 1, :], mrem[:]).then_inc(msplit_done, 1)

                def norm(u):
                    g, hq = st.attend(u)
                    dve.wait_ge(o_turned, u - GT + 1)
                    o = pX[:, :].rearrange("p (t h d) -> p t h d", t=GT, d=32)
                    link(dve.reciprocal(rsum[:], o[:, :, :, DK]))
                    if hq == 0 and g != st.groups[0]:
                        dve.wait_ge(ot_turned, KD * st.groups.index(g))
                    dst = otok[:, :, hq * QUAD * DK:(hq + 1) * QUAD * DK].rearrange("p t (h d) -> p t h d", d=DK)
                    for t in range(GT):
                        dve.tensor_tensor(dst[:, t], o[:, t, :, 0:DK], rsum[:, t].unsqueeze(2).to_broadcast([P, QUAD, DK]),
                                          ALU.mult).then_inc(normed, 1)

                def residual(u):
                    g, _ = st.attend(u)
                    dve.wait_ge(filled["out"], st.slot[("out", u)][1])
                    dve.wait_ge(x_in, 16 * (st.groups.index(g) + 1))
                    flat = xg[:, :, :].rearrange("p t d -> p (t d)")
                    dve.tensor_tensor(flat, view(("out", u)), flat, ALU.add).then_inc(taken["out"], 1)

                for u in range(st.n):
                    if u < NT:
                        choose(u)
                        dve.wait_ge(bias_done, u + 1)
                    if u > GT:
                        norm(u - 1)
                    owed = None
                    for e in st.plan[u]:
                        uses = {"a": 2, "m": 1, "d": 2, "mask": 1}.get(e[0], 0)
                        if e[0] == "project":
                            owed = RING - 1
                        elif owed is not None and uses:
                            owed -= uses
                            if owed < 0:
                                residual(u - 1)
                                owed = None
                        if e[0] == "m":
                            maximum(u, *e[1:])
                        elif e[0] == "turn_m":
                            split_maxima(u)
                    if owed is not None:
                        residual(u - 1)
                norm(st.n - 1)
                residual(st.n - 1)

            @block.gpsimd
            def _(pool):
                for u in range(NT):
                    i, n = st.tile(u), st.width(u)
                    if i == 0:
                        continue
                    for k, w in st.parts(u):
                        part = sc[:, u % 2, k * PW:k * PW + w]
                        for h in range(1, HI):
                            c = st.slot[("dot", u, k, h)][1]
                            pool.wait_ge(weighted, c)
                            if sums(c) > 1:
                                pool.wait_ge(summed, sums(c) - 1)
                            pool.tensor_tensor(part, part, relu[:, c % 3, 0:w], ALU.add).then_inc(summed, 1)
                    pool.wait_ge(summed, sums(c))
                    own = sc[:, u % 2, n - P:n]
                    pool.affine_select(out=own, in_=own, compare_op=ALU.is_ge, fill=CAUSAL,
                                       base=0, pattern=[[-1, P]], channel_multiplier=1).then_inc(causal_done, 1)

            @block.scalar
            def _(act):
                def exps(u, j):
                    g, _ = st.attend(u)
                    c0 = max(0, j - GT * g) * P
                    n = chunks[u] + j
                    for p in range(2):
                        slot, c = st.slot[("exp", u, j, p)]
                        act.wait_ge(filled["exp"], c)
                        if p == 0 and n >= 2:
                            act.wait_ge(pv_done, n - 1)
                        act.activation(prob[:, (2 * n + p) % 4, :, c0:GW], ring[slot][:, :, c0:GW], ACT.Exp, scale=float(DK) ** -0.5).then_inc(taken["exp"], 1)

                def quad_out(u):
                    act.wait_ge(pv_done, chunks[u + 1])
                    if u > GT:
                        act.wait_ge(o_turned, u - GT)
                    act.activation(oT[:], pO[:], ACT.Copy).then_inc(oT_done, 1)

                def mask_out(u):
                    i = st.tile(u)
                    key = ("mask", u)
                    act.wait_ge(filled["mask"], u + 1)
                    v = view(key).bitcast(BF16).rearrange("p (j q) -> p j q", q=P)
                    m = maskT[st.groups[u // GT] % 2]
                    act.activation(m[:, 0:i + 1, (u % GT) * P:(u % GT + 1) * P], v[:, 0:i + 1, :], ACT.Copy,
                                   scale=1.0 / HIDE, saturate=False).then_inc(taken["mask"], 1)

                def m_out(u):
                    act.wait_ge(m_turned, u + 1)
                    if u % GT == 0 and u >= GT:
                        act.wait_ge(qm_in, 16 * PARTS * (u // GT))
                    act.activation(mT[:, (u % GT) * P:(u % GT + 1) * P], pX[0:PARTS * H, :].bitcast(BF16)[:, 0:P], ACT.Copy).then_inc(mT_done, 1)

                def final(u):
                    n = st.groups.index(st.attend(u)[0])
                    if u + 1 < NT:
                        c = max(c for (key, (_, c)) in st.slot.items() if key[0] == "dot" and key[1] <= u + 2)
                        act.wait_ge(summed, sums(c))
                    for k in range(KD):
                        act.wait_ge(ot_turned, KD * n + k + 1)
                        act.activation(otokT[:, k, :], pX[:], ACT.Copy).then_inc(otT_done, 1)

                def relus(u, k, hp):
                    w = dict(st.parts(u))[k]
                    for h in (2 * hp, 2 * hp + 1):
                        key = ("dot", u, k, h)
                        c = st.slot[key][1]
                        r = relu[:, c % 3, 0:w]
                        act.wait_ge(filled["dot"], c)
                        if c > 3:
                            if (c - 4) % HI:
                                act.wait_ge(summed, sums(c - 3))
                            else:
                                act.wait_ge(weighted, c - 3)
                        act.activation(r, view(key, w), ACT.Relu).then_inc(taken["dot"], 1)
                        act.wait_ge(taken["dot"], c)
                        if h == 0 and k == 0 and u >= 2:
                            act.wait_ge(bias_done, u - 1)
                        act.activation(sc[:, u % 2, k * PW:k * PW + w] if h == 0 else r, r, ACT.Identity, scale=wi[:, st.tile(u), h:h + 1]).then_inc(weighted, 1)

                for k, _ in st.parts(0):
                    for hp in range(HI // 2):
                        relus(0, k, hp)
                for u in range(st.n):
                    for e in st.plan[u]:
                        if e[0] == "a":
                            exps(u, e[1])
                        elif e[0] == "d":
                            relus(u + 1, *e[1:])
                        elif e[0] == "project":
                            final(u - 1)
                        elif e[0] == "end":
                            quad_out(u)
                        elif e[0] == "mask":
                            mask_out(u)
                        elif e[0] == "turn_m":
                            m_out(u)
                final(st.n - 1)

            @block.tensor
            def _(pe):
                used = [0]

                def slot(key):
                    n = used[0]
                    assert st.order[n] == (key[0], st.slot[key][1])
                    used[0] += 1
                    if n >= RING:
                        kind, c = st.order[n - RING]
                        pe.wait_ge(taken[kind], c)
                    return ring[st.slot[key][0]]

                def dots(u, k, hp):
                    w = dict(st.parts(u))[k]
                    if k == 0 and hp == 0:
                        pe.wait_ge(qi_in[u % 2], 16 * sum(1 for v in range(u % 2, u + 1, 2) if st.tile(v)))
                    rs = [slot(("dot", u, k, 2 * hp + a)) for a in range(2)]
                    for c in range(0, w, 512):
                        cw = min(512, w - c)
                        for a in range(2):
                            rows = slice(a * DI, (a + 1) * DI)
                            mm = pe.matmul(rs[a][:, c // 512, 0:cw], qi[rows, u % 2, hp, :], kiT[rows, k * PW + c:k * PW + c + cw], start=True, stop=True)
                            if c + cw == w:
                                mm.then_inc(filled["dot"], 1)

                def scores(u, j):
                    g, hq = st.attend(u)
                    c0 = max(0, j - GT * g) * P
                    for p in range(2):
                        r = slot(("exp", u, j, p))
                        for a in range(2):
                            h = hq * QUAD + 2 * p + a
                            pe.matmul(r[:, a, c0:GW], K99[:, h, j * P:(j + 1) * P], Q99[g % 2][:, h, c0:GW], start=True, stop=False)
                            mm = pe.matmul(r[:, a, c0:GW], hide[:], maskT[g % 2][:, j, c0:GW], start=False, stop=True)
                        mm.then_inc(filled["exp"], 1)

                def values(u, j):
                    g, hq = st.attend(u)
                    c0 = max(0, j - GT * g) * P
                    n = chunks[u] + j
                    pe.wait_ge(taken["exp"], 2 * (n + 1))
                    if j == 0 and u > GT:
                        pe.wait_ge(oT_done, u - GT)
                    for q in range(QUAD):
                        h = hq * QUAD + q
                        mm = pe.matmul(pO[32 * q:32 * q + 32, c0:GW], V[:, j, h * VW:h * VW + 32], prob[:, (2 * n + q // 2) % 4, q % 2, c0:GW],
                                       start=(j == 0), stop=(j == GT * (g + 1) - 1))
                    mm.then_inc(pv_done, 1)

                def chunk(u, j):
                    g, hq = st.attend(u)
                    if hq == 0 and j == 0:
                        pe.wait_ge(qm_in, 16 * PARTS * (st.groups.index(g) + 1))
                        pe.wait_ge(taken["mask"], GT * (st.groups.index(g) + 1))
                    scores(u, j)
                    if j >= 1:
                        values(u, j - 1)

                def turn_o(u):
                    pe.wait_ge(oT_done, u - GT + 1)
                    if u < NT:
                        pe.wait_ge(mT_done, u + 1)
                    else:
                        pe.wait_ge(normed, GT * (u - GT))
                        if ("project",) in st.plan[u]:
                            pe.wait_ge(otT_done, KD * (st.groups.index(st.attend(u - 1)[0]) + 1))
                    for t in range(GT):
                        mm = pe.transpose(pX[:, t * P:(t + 1) * P], oT[:, t * P:(t + 1) * P], identf[:])
                    mm.then_inc(o_turned, 1)

                def turn_mask(u):
                    i = st.tile(u)
                    pe.wait_ge(bias_done, u + 1)
                    slot(("mask", u))
                    v = view(("mask", u)).bitcast(BF16)
                    for j in range(i + 1):
                        mm = pe.transpose(v[:, j * P:(j + 1) * P], bias[:, j * P:(j + 1) * P], identb[:])
                    mm.then_inc(filled["mask"], 1)

                def max_scores(u, h, k):
                    g, t = st.groups[u // GT], u % GT
                    w = dict(st.parts(u))[k]
                    if t == 0 and h == 0 and k == 0:
                        pe.wait_ge(q_in[g % 2], 16 * len(Q_SLOTS) * (1 if g >= NG - 2 else 2))
                    r = slot(("max", u, h, k))
                    for c in range(0, w, 512):
                        cw = min(512, w - c)
                        mm = pe.matmul(r[:, c // 512, 0:cw], Q99[g % 2][0:KR, h, t * P:(t + 1) * P], K99[0:KR, h, k * PW + c:k * PW + c + cw], start=True, stop=True)
                    mm.then_inc(filled["max"], 1)

                def turn_m(u):
                    pe.wait_ge(msplit_done, u + 1)
                    if u > GT:
                        pe.wait_ge(normed, GT * (u - GT))
                    elif u >= 1:
                        pe.wait_ge(mT_done, u)
                    if ("project",) in st.plan[u]:
                        pe.wait_ge(otT_done, KD * (st.groups.index(st.attend(u - 1)[0]) + 1))
                    pe.transpose(pX[0:PARTS * H, :].bitcast(BF16)[:, 0:P], msplit[:, :, :].rearrange("p r h -> p (r h)"), identb[:]).then_inc(m_turned, 1)

                def project(u):
                    n = st.groups.index(st.attend(u)[0])
                    pe.wait_ge(normed, GT * (u - GT + 1))
                    for k in range(KD):
                        if k:
                            pe.wait_ge(otT_done, KD * n + k)
                        for t in range(GT):
                            mm = pe.transpose(pX[:, t * P:(t + 1) * P], otok[:, t, k * P:(k + 1) * P], identf[:])
                        mm.then_inc(ot_turned, 1)
                    pe.wait_ge(otT_done, KD * (n + 1))
                    slot(("out", u))
                    v = view(("out", u))
                    for t in range(GT):
                        for k in range(KD):
                            mm = pe.matmul(v[:, t * D:(t + 1) * D], otokT[:, k, t * P:(t + 1) * P], woT[:, k, :], start=(k == 0), stop=(k == KD - 1))
                    mm.then_inc(filled["out"], 1)

                for k, _ in st.parts(0):
                    for hp in range(HI // 2):
                        dots(0, k, hp)
                for u in range(st.n):
                    for e in st.plan[u]:
                        if e[0] == "a":
                            chunk(u, e[1])
                        elif e[0] == "m":
                            max_scores(u, *e[1:])
                        elif e[0] == "d":
                            dots(u + 1, *e[1:])
                        elif e[0] == "project":
                            project(u - 1)
                        elif e[0] == "end":
                            values(u, GT * (st.attend(u)[0] + 1) - 1)
                        elif e[0] == "mask":
                            turn_mask(u)
                        elif e[0] == "turn_m":
                            turn_m(u)
                        else:
                            turn_o(u)
                project(st.n - 1)

        clear(nc, sems)


def feed_forward(nc, w, identf, sign, x2D, out):
    NTA, NGA = B * NT, B * NG
    D2, D4 = D // 2, D // 4
    with ExitStack() as ctx:
        sb = lambda n, s, d: ctx.enter_context(nc.sbuf_tensor(n, s, d))
        ps = lambda n, s, d: ctx.enter_context(nc.psum_tensor(n, s, d))
        sems = []

        def sem(n):
            sems.append(ctx.enter_context(nc.semaphore(n)))
            return sems[-1]

        x2 = sb("x2", [P, NTA, D], FP32)
        hn = sb("hn", [P, 2, D], FP32)
        stats = sb("fstats", [P, NTA, 6], FP32)
        mv = sb("fmv", [P, NTA, 2], FP32)
        sd = sb("fsd", [P, NTA], FP32)
        rstd = sb("frstd", [P, NTA], FP32)
        eps = sb("feps", [P, 1], FP32)
        hT = sb("hT", [P, KD, B * S], FP32)
        h1 = sb("h1", [P, 2, KD, GW], FP32)
        h2 = sb("h2", [P, 2, GW], FP32)
        h3 = sb("h3", [D4, 2, GW], FP32)
        th = sb("th", [P, 2, GW], FP32)
        tw = sb("tw", [P, 2, 2, GW], FP32)
        w1 = sb("w1", [P, KD, D], FP32)
        w2 = sb("w2", [P, KD, D2], FP32)
        w3 = sb("w3", [P, D4], FP32)
        w4 = sb("w4", [D4, P], FP32)
        g1 = sb("g1", [P, KD, D2], FP32)
        g2 = sb("g2", [P, D4], FP32)
        g3 = sb("g3", [D4, P], FP32)
        g3c = sb("g3c", [D4, 1], FP32)
        w4c = sb("w4c", [D4, 1], FP32)
        b1 = sb("b1", [P, KD], FP32)
        b2 = sb("b2", [P, 1], FP32)
        b3 = sb("b3", [D4, 1], FP32)
        b4 = sb("b4", [P, 1], FP32)
        c1 = sb("c1", [P, 1], FP32)
        c2 = sb("c2", [D4, 1], FP32)
        c3 = sb("c3", [P, 1], FP32)
        ar = sb("ar", [P, 1], FP32)
        half = sb("half", [P, 2], FP32)
        mean = sb("mean", [P, KD, B], FP32)
        gh1 = sb("gh1", [P, B], FP32)
        gh2 = sb("gh2", [D4, B], FP32)
        gt = sb("gt", [P, B], FP32)
        base = sb("base", [P, B], FP32)
        slope = sb("slope", [P, 1], FP32)
        pW = [ps(f"pW{k}", [P, 512], FP32) for k in range(8)]
        x2_in = [sem(f"x2_in{g}") for g in range(NGA)]
        w_in, eps_set, stats_done, mv_done, sd_done, rstd_done = (sem(n) for n in ("fw_in", "feps_set", "fstats_done", "fmv_done", "fsd_done", "frstd_done"))
        hn_done, h_turned, hT_done, half_done, mean_done = (sem(n) for n in ("hn_done", "h_turned", "hT_done", "half_done", "mean_done"))
        gz1, gz2, gz3, ga1, ga2, ga3, coef = (sem(n) for n in ("gz1", "gz2", "gz3", "ga1", "ga2", "ga3", "coef"))
        z1, z2, z3, z4, a1, a2, a3, a4 = (sem(n) for n in ("z1", "z2", "z3", "z4", "a1", "a2", "a3", "a4"))
        c_done, tw_done, h_new, y_turned, y_done, y_out = (sem(n) for n in ("c_done", "tw_done", "h_new", "y_turned", "y_done", "y_out"))
        NC = CYCLES * NGA

        with nc.Block() as block:

            @block.sync
            def _(sp):
                x2v = x2D.rearrange("(t p) d -> p t d", p=P)
                for g in range(NGA):
                    sp.dma_start(x2[:, g * GT:(g + 1) * GT, :], x2v[:, g * GT:(g + 1) * GT, :]).then_inc(x2_in[g], 16)
                col = lambda a: a.rearrange("(p o) -> p o", o=1)
                kp = lambda a: a.rearrange("(k p) n -> p k n", p=P)
                loads = [(g1[:], kp(w["g1"])), (g2[:], w["g2"]), (g3c[:], w["g3"]), (c1[:], col(w["c1"])),
                         (c2[:], col(w["c2"])), (c3[:], w["c3"].partition_broadcast(P)), (ar[:], w["ar"].partition_broadcast(P)),
                         (b4[:], w["b4"].partition_broadcast(P)), (w1[:], kp(w["w1"])), (w2[:], kp(w["w2"])), (w3[:], w["w3"]),
                         (w4c[:], w["w4"]), (b1[:, 0:1], col(w["b1"][0:P])), (b1[:, 1:2], col(w["b1"][P:D])), (b2[:], col(w["b2"])), (b3[:], col(w["b3"]))]
                for dst, src in loads:
                    sp.dma_start(dst, src).then_inc(w_in, 16)
                ob = out.rearrange("(t p) d -> p t d", p=P)
                for g in range(NGA):
                    sp.wait_ge(y_done, GT * (g + 1))
                    sp.dma_start(ob[:, g * GT:(g + 1) * GT, :], x2[:, g * GT:(g + 1) * GT, :]).then_inc(y_out, 16)
                sp.wait_ge(y_out, 16 * NGA)

            NW = 16

            @block.vector
            def _(dve):
                dve.memset(eps[:], EPS).then_inc(eps_set, 1)
                for i in range(NTA):
                    if i % GT == 0:
                        dve.wait_ge(x2_in[i // GT], 16)
                    dve.bn_stats(out=stats[:, i, :], in_=x2[:, i, :]).then_inc(stats_done, 1)
                for i in range(NTA):
                    dve.wait_ge(stats_done, i + 1)
                    dve.bn_aggr(out=mv[:, i, :], in_=stats[:, i, :]).then_inc(mv_done, 1)
                dve.wait_ge(w_in, 16 * NW)
                dve.tensor_scalar(half[:, 0:1], b4[:], 0.5, None, ALU.mult).then_inc(half_done, 1)
                dve.tensor_scalar(half[:, 1:2], c3[:], 0.5, None, ALU.mult).then_inc(half_done, 1)
                dve.tensor_copy(w4[:], w4c[:, 0:1].to_broadcast([D4, P])).then_inc(half_done, 1)
                dve.tensor_copy(g3[:], g3c[:, 0:1].to_broadcast([D4, P])).then_inc(half_done, 1)
                dve.tensor_scalar(slope[:], ar[:], sign[:, 0:1], 0.3, ALU.mult, ALU.mult).then_inc(half_done, 1)
                dve.wait_ge(sd_done, 1)
                dve.reciprocal(rstd[:], sd[:]).then_inc(rstd_done, 1)
                dve.wait_ge(rstd_done, 1)
                for i in range(NTA):
                    if i >= 2:
                        dve.wait_ge(h_turned, i - 1)
                    dve.tensor_scalar(hn[:, i % 2, :], x2[:, i, :], mv[:, i, 0:1], rstd[:, i:i + 1], ALU.subtract, ALU.mult).then_inc(hn_done, 1)
                dve.wait_ge(hT_done, NTA)
                dve.tensor_reduce(mean[:], hT[:, :, :].rearrange("p k (b s) -> p k b s", b=B), AX.X, ALU.add).then_inc(mean_done, 1)
                dve.wait_ge(ga3, 1)
                dve.tensor_scalar(gt[:], gt[:], ar[:, 0:1], 0.7, ALU.mult, ALU.mult).then_inc(coef, 1)
                dve.wait_ge(coef, 1)
                dve.tensor_scalar(base[:], gt[:], 0.1, sign[:, 0:1], ALU.add, ALU.mult).then_inc(coef, 1)
                dve.wait_ge(coef, 2)
                dve.wait_ge(half_done, 5)
                for n in range(NC):
                    g = n % NGA
                    k = n % 2
                    cols = slice(g * GW, (g + 1) * GW)
                    dve.wait_ge(a4, n + 1)
                    dve.tensor_scalar(th[:, k, :], th[:, k, :], slope[:, 0:1], base[:, g // NG:g // NG + 1], ALU.mult, ALU.add).then_inc(c_done, 1)
                    dve.wait_ge(c_done, n + 1)
                    if n >= NGA:
                        dve.wait_ge(h_new, 2 * (n - NGA + 1))
                    if n >= 2:
                        dve.wait_ge(h_new, 2 * (n - 1))
                    dve.tensor_tensor(tw[:, k, 0, :], th[:, k, :], hT[:, 1, cols], ALU.mult).then_inc(tw_done, 1)
                    dve.tensor_tensor(tw[:, k, 1, :], th[:, k, :], hT[:, 0, cols], ALU.mult).then_inc(tw_done, 1)
                    dve.wait_ge(tw_done, 2 * (n + 1))
                    dve.tensor_tensor(hT[:, 0, cols], hT[:, 0, cols], tw[:, k, 0, :], ALU.add).then_inc(h_new, 1)
                    dve.tensor_tensor(hT[:, 1, cols], hT[:, 1, cols], tw[:, k, 1, :], ALU.subtract).then_inc(h_new, 1)
                for i in range(NTA):
                    dve.wait_ge(y_turned, i + 1)
                    dve.tensor_tensor(x2[:, i, :], pW[i % 4][:, 0:D], x2[:, i, :], ALU.add).then_inc(y_done, 1)

            @block.scalar
            def _(act):
                act.wait_ge(mv_done, NTA)
                act.wait_ge(eps_set, 1)
                act.activation(sd[:], mv[:, :, 1], ACT.Sqrt, bias=eps[:, 0:1]).then_inc(sd_done, 1)
                for i in range(NTA):
                    act.wait_ge(h_turned, i + 1)
                    act.activation(hT[:, :, i * P:(i + 1) * P], pW[i % 2][:, 0:D].rearrange("p (k q) -> p k q", q=P), ACT.Copy).then_inc(hT_done, 1)
                act.wait_ge(w_in, 16 * NW)
                act.wait_ge(half_done, 5)

                def global_net():
                    act.wait_ge(gz1, 1)
                    act.activation(gh1[:], pW[6][:, 0:B], ACT.Gelu, bias=c1[:, 0:1], scale=1.0 / S).then_inc(ga1, 1)
                    act.wait_ge(gz2, 1)
                    act.activation(gh2[:], pW[7][0:D4, 0:B], ACT.Gelu, bias=c2[:, 0:1]).then_inc(ga2, 1)
                    act.wait_ge(gz3, 1)
                    act.activation(gt[:], pW[6][:, 0:B], ACT.Tanh, bias=half[:, 1:2], scale=0.5).then_inc(ga3, 1)

                for m in range(NC + 3):
                    if m < NC:
                        n, k = m, m % 2
                        for q in range(KD):
                            act.wait_ge(z1, 2 * n + q + 1)
                            if n >= 2:
                                act.wait_ge(z2, n - 1)
                            act.activation(h1[:, k, q, :], pW[q][:], ACT.Gelu, bias=b1[:, q:q + 1]).then_inc(a1, 1)
                    if m == 1:
                        global_net()
                    if 1 <= m <= NC:
                        n = m - 1
                        k = n % 2
                        act.wait_ge(z2, n + 1)
                        if n >= 2:
                            act.wait_ge(z3, n - 1)
                        act.activation(h2[:, k, :], pW[2 + k][:], ACT.Gelu, bias=b2[:, 0:1]).then_inc(a2, 1)
                    if 2 <= m <= NC + 1:
                        n = m - 2
                        k = n % 2
                        act.wait_ge(z3, n + 1)
                        if n >= 2:
                            act.wait_ge(z4, n - 1)
                        act.activation(h3[:, k, :], pW[4 + k][0:D4, :], ACT.Gelu, bias=b3[:, 0:1]).then_inc(a3, 1)
                    if m >= 3:
                        n = m - 3
                        k = n % 2
                        act.wait_ge(z4, n + 1)
                        if n >= 2:
                            act.wait_ge(tw_done, 2 * (n - 1))
                        act.activation(th[:, k, :], pW[6 + k][:], ACT.Tanh, bias=half[:, 0:1], scale=0.5).then_inc(a4, 1)

            @block.tensor
            def _(pe):
                for i in range(NTA):
                    pe.wait_ge(hn_done, i + 1)
                    if i >= 2:
                        pe.wait_ge(hT_done, i - 1)
                    for k in range(KD):
                        mm = pe.transpose(pW[i % 2][:, k * P:(k + 1) * P], hn[:, i % 2, k * P:(k + 1) * P], identf[:])
                    mm.then_inc(h_turned, 1)
                pe.wait_ge(w_in, 16 * NW)
                pe.wait_ge(half_done, 5)

                def global_net():
                    pe.wait_ge(mean_done, 1)
                    for k in range(KD):
                        mm = pe.matmul(pW[6][:, 0:B], g1[:, k, :], mean[:, k, :], start=(k == 0), stop=(k == KD - 1))
                    mm.then_inc(gz1, 1)
                    pe.wait_ge(ga1, 1)
                    pe.matmul(pW[7][0:D4, 0:B], g2[:], gh1[:], start=True, stop=True).then_inc(gz2, 1)
                    pe.wait_ge(ga2, 1)
                    pe.matmul(pW[6][:, 0:B], g3[:], gh2[:], start=True, stop=True).then_inc(gz3, 1)

                for m in range(NC + 3):
                    if m < NC:
                        n = m
                        cols = slice((n % NGA) * GW, (n % NGA + 1) * GW)
                        if n >= NGA:
                            pe.wait_ge(h_new, 2 * (n - NGA + 1))
                        else:
                            pe.wait_ge(hT_done, NTA)
                        for q in range(KD):
                            if n >= 1:
                                pe.wait_ge(a1, 2 * (n - 1) + q + 1)
                            for k in range(KD):
                                mm = pe.matmul(pW[q][:], w1[:, k, q * P:(q + 1) * P], hT[:, k, cols], start=(k == 0), stop=(k == KD - 1))
                            mm.then_inc(z1, 1)
                    if m == 1:
                        global_net()
                    if 1 <= m <= NC:
                        n = m - 1
                        pe.wait_ge(a1, 2 * (n + 1))
                        if n >= 2:
                            pe.wait_ge(a2, n - 1)
                        for k in range(KD):
                            mm = pe.matmul(pW[2 + n % 2][:], w2[:, k, :], h1[:, n % 2, k, :], start=(k == 0), stop=(k == KD - 1))
                        mm.then_inc(z2, 1)
                    if 2 <= m <= NC + 1:
                        n = m - 2
                        pe.wait_ge(a2, n + 1)
                        if n >= 2:
                            pe.wait_ge(a3, n - 1)
                        pe.matmul(pW[4 + n % 2][0:D4, :], w3[:], h2[:, n % 2, :], start=True, stop=True).then_inc(z3, 1)
                    if m >= 3:
                        n = m - 3
                        pe.wait_ge(a3, n + 1)
                        if n >= 2:
                            pe.wait_ge(a4, n - 1)
                        else:
                            pe.wait_ge(ga3, 1)
                        pe.matmul(pW[6 + n % 2][:], w4[:], h3[:, n % 2, :], start=True, stop=True).then_inc(z4, 1)
                for i in range(NTA):
                    pe.wait_ge(h_new, 2 * (NC - NGA + i // GT + 1))
                    if i >= 4:
                        pe.wait_ge(y_done, i - 3)
                    else:
                        pe.wait_ge(a2, NC)
                    for k in range(KD):
                        mm = pe.transpose(pW[i % 4][:, k * P:(k + 1) * P], hT[:, k, i * P:(i + 1) * P], identf[:])
                    mm.then_inc(y_turned, 1)

        clear(nc, sems)


def build(nc, x, w, tabs, out):
    with ExitStack() as ctx:
        sb = lambda n, s, d: ctx.enter_context(nc.sbuf_tensor(n, s, d))
        identf = sb("identf", [P, P], FP32)
        sign = sb("sign", [P, 1], FP32)
        x2D = nc.dram_tensor("x2_scratch", (B * S, D), FP32, kind="Internal").ap()
        attend_all(nc, x, w, tabs, x2D, identf, sign)
        feed_forward(nc, w, identf, sign, x2D, out)


def attend_all(nc, x, w, tabs, x2D, identf, sign):
    with ExitStack() as ctx:
        sb = lambda n, s, d: ctx.enter_context(nc.sbuf_tensor(n, s, d))
        K99 = sb("K99", [KM, H, S], BF16)
        V = sb("V", [P, NT, VP], FP32)
        kiT = sb("kiT", [P, S], FP32)
        wi = sb("wi", [P, NT, HI], FP32)
        identb = sb("identb", [P, P], BF16)
        hide = sb("hide", [P, P], BF16)
        woT = sb("woT", [P, KD, D], FP32)
        qkD = [nc.dram_tensor(f"qk{c}_parts", (H * PARTS * DK, S), BF16, kind="Internal").ap() for c in range(2)]
        qiD = nc.dram_tensor("qi_scratch", (P, 2, S), FP32, kind="Internal").ap()
        zeroed = ctx.enter_context(nc.semaphore("zeroed"))
        const_done = ctx.enter_context(nc.semaphore("const_done"))
        ones_set = ctx.enter_context(nc.semaphore("ones_set"))
        wo_in = ctx.enter_context(nc.semaphore("wo_in"))
        with nc.sbuf_tensor("ones", [PARTS, S], BF16) as ones, nc.Block() as block:

            @block.sync
            def _(sp):
                sp.dma_start(woT[:], w["oT"].rearrange("(k p) n -> p k n", p=P)).then_inc(wo_in, 16)
                sp.wait_ge(ones_set, 2)
                for h in range(H):
                    sp.dma_start(K99[KR:KM, h, :], ones[:]).then_inc(wo_in, 16)
                sp.wait_ge(wo_in, 16 * (1 + H))

            @block.gpsimd
            def _(pool):
                pool.memset(identf[:], 0.0).then_inc(zeroed, 1)
                pool.memset(identb[:], 0.0).then_inc(zeroed, 1)
                pool.memset(sign[:], 1.0).then_inc(zeroed, 1)
                pool.memset(hide[:], 0.0).then_inc(zeroed, 1)
                pool.wait_ge(zeroed, 4)
                for m, one in ((identf, 1.0), (identb, 1.0), (hide, HIDE)):
                    pool.affine_select(out=m[:], in_=m[:], compare_op=ALU.not_equal, fill=one, base=0,
                                       pattern=[[-1, P]], channel_multiplier=1).then_inc(const_done, 1)
                pool.affine_select(out=sign[:], in_=sign[:], compare_op=ALU.is_gt, fill=-1.0, base=D // 4,
                                   pattern=[[0, 1]], channel_multiplier=-1).then_inc(const_done, 1)
                pool.wait_ge(const_done, 4)

            @block.vector
            def _(dve):
                dve.memset(V[:], 1.0).then_inc(ones_set, 1)
                dve.memset(ones[:], 1.0).then_inc(ones_set, 1)
                dve.wait_ge(ones_set, 2)

        clear(nc, [zeroed, const_done, ones_set, wo_in])
        keep = (K99, V, kiT, wi)
        with nc.Fori(0, B) as b:
            prepare(nc, b, x, w, tabs, (identf, identb), keep, (qkD, qiD))
            attention(nc, b, x, (identf, identb, hide, woT), keep, (qkD, qiD, x2D))


_TURNED = {'L0_attn_w_qkv': 'qkvT', 'L0_attn_w_o': 'oT', 'L0_attn_w_qi': 'qiT', 'L0_attn_w_ki': 'kiT', 'L0_attn_w_wi': 'wiT'}
_PLAIN = {'L0_ffn_cn_w1': 'w1', 'L0_ffn_cn_b1': 'b1', 'L0_ffn_cn_w2': 'w2', 'L0_ffn_cn_b2': 'b2', 'L0_ffn_cn_w3': 'w3',
          'L0_ffn_cn_b3': 'b3', 'L0_ffn_cn_w4': 'w4', 'L0_ffn_cn_b4': 'b4', 'L0_ffn_gc_w1': 'g1', 'L0_ffn_gc_b1': 'c1',
          'L0_ffn_gc_w2': 'g2', 'L0_ffn_gc_b2': 'c2', 'L0_ffn_gc_w3': 'g3', 'L0_ffn_gc_b3': 'c3', 'L0_ffn_adaptive_range': 'ar'}


def kernel(**inputs):
    import numpy as _np
    import concourse.bacc as _bacc
    from concourse import mybir as _mybir
    from concourse.bass_utils import run_bass_kernel_spmd as _run

    nc = _bacc.Bacc("TRN2", target_bir_lowering=False, num_devices=1)
    arrays = {}

    def tensor(name, a):
        a = _np.ascontiguousarray(a)
        arrays[name] = a
        return nc.dram_tensor(name, a.shape, _mybir.dt.from_np(a.dtype), kind="ExternalInput").ap()

    xs = _np.asarray(inputs['L0_attn_x'])
    x = tensor("x_dram", xs.reshape(B * S, D))
    w = {k: tensor(f"{k}_dram", _np.asarray(inputs[n]).T) for n, k in _TURNED.items()}
    w.update({k: tensor(f"{k}_dram", _np.asarray(inputs[n])) for n, k in _PLAIN.items()})
    tabs = [tensor(f"table{k}_dram", t) for k, t in enumerate(rope_tables())]
    out = nc.dram_tensor("out_dram", (B * S, D), _mybir.dt.float32, kind="ExternalOutput").ap()
    build(nc, x, w, tabs, out)
    r = _run(nc, [arrays], core_ids=[0])
    return r.results[0]["out_dram"].reshape(xs.shape)
```

```python
import concourse.bass as bass
import numpy as np
from concourse import mybir
from contextlib import ExitStack

FP32 = mybir.dt.float32
BF16 = mybir.dt.bfloat16
FP8 = mybir.dt.float8e4
ALU = mybir.AluOpType
ACT = mybir.ActivationFunctionType
AX = mybir.AxisListType

B, S, D = 2, 2048, 256
H, DK = 16, 16
HI, DI = 4, 64
TOPK = 128
EPS = 1e-5
P = 128
NT = S // P
GT = 4
GW = GT * P
NG = NT // GT
KD = D // P
QUAD = 4
NQ = H // QUAD
PW = 1024
RING = 3
PARTS = 3
Q_SLOTS = (0, 0, 0, 1, 1, 2)
K_SLOTS = (0, 1, 2, 0, 1, 0)
KR = len(Q_SLOTS) * DK
KM = KR + PARTS
VW = DK + 1
VP = H * VW + 32 - VW
CAUSAL = -3.3e38
TAKEN = -3.4e38
HIDE = -1.0e30
BELOW = -1.7e38
STEP = 2.0 ** -115
ZERO = 2.0 ** -103
TRIALS = 8
SPREAD = 4.7
MEAN_OF = 512
COUNTS = 3 + TRIALS + 1
RANKS = 15
CYCLES = 3
CHOOSE_US = 6 / 960
EARLY = 3
DOTS_BY = 0.75
PAIR_US = 1.6


def rope_tables():
    inv = (np.float32(1.0) / np.float32(10000.0) ** (np.arange(0, DK, 2, dtype=np.float32) / np.float32(DK))).astype(np.float32)
    ang = (np.arange(S, dtype=np.float32)[:, None] * inv).astype(np.float32)
    lay = lambda a: np.ascontiguousarray(a.astype(np.float32).reshape(NT, P, -1).transpose(1, 0, 2))
    cos, sin = np.cos(ang), np.sin(ang)
    return lay(np.repeat(cos, 2, axis=1)), lay(sin), lay(-sin)


def rank_tables():
    row = np.concatenate([-STEP * np.arange(P), -STEP * P * np.arange(NT), np.arange(RANKS) + 1.0, P * np.arange(1, NT + 1) - 2 * TOPK + 1])
    return np.ascontiguousarray(np.broadcast_to(row.astype(np.float32), (P, row.size)))


ORDER = (0, 1, 2, 3)


class Steps:

    def __init__(self):
        self.groups = ORDER
        self.n = NT + GT
        self.plan = [self.events(u) for u in range(self.n)]
        self.slot, self.order, self.count = {}, [], {}
        for e in self.dots(0) + self.dots(1):
            self.use_dots(*e)
        for u, events in enumerate(self.plan):
            for e in events:
                if e[0] == "a":
                    self.use("exp", ("exp", u, *e[1:]))
                elif e[0] == "m":
                    self.use("max", ("max", u, *e[1:]))
                elif e[0] == "d":
                    self.use_dots(u + 2, *e[1:])
                elif e[0] in ("mask", "check"):
                    self.use(e[0], (e[0], u))
                elif e == ("project", KD):
                    self.use("out", ("out", u - 1))
        self.use("out", ("out", self.n - 1))

    def events(self, u):
        a = self.attend(u)
        pairs = [("a", j, p) for j in range(GT * (a[0] + 1)) for p in range(2)] if a else []
        maxima = [("m", h, k) for h in range(H) for k, _ in self.parts(u)] if u < NT else []
        dots = [("d", k, hp) for _, k, hp in self.dots(u + 2)]
        passes = [("c", k) for k in range(COUNTS)] if u + 1 < NT and self.tile(u + 1) else []
        first = min(len(pairs), round(self.width(u) * CHOOSE_US / PAIR_US)) if u < NT else 0
        soon = EARLY if u < NT else len(passes)
        early = [((i + 0.5) / first, e) for i, e in enumerate(pairs[:first])]
        early += [((i + 0.5) / soon, e) for i, e in enumerate(passes[:soon])]
        out = [e for _, e in sorted(early, key=lambda r: r[0])]
        if self.projects(u):
            out.insert(min(1, len(out)), ("project", 0))
            out.insert(min(5, len(out)), ("project", 1))
        elif u and (u - 1) % GT != GT - 1:
            out[1:1] = self.turns(u - 1)
        if u < NT and self.tile(u):
            out.append(("check",))
        if self.projects(u):
            out.append(("project", KD))
        rest = [((i + 0.5) / len(maxima), e) for i, e in enumerate(maxima)]
        rest += [((i + 0.3) / (len(pairs) - first), e) for i, e in enumerate(pairs[first:])]
        rest += [(DOTS_BY * (i + 0.4) / len(dots), e) for i, e in enumerate(dots)]
        rest += [((i + 0.2) / (len(passes) - soon), e) for i, e in enumerate(passes[soon:])]
        out += [e for _, e in sorted(rest, key=lambda r: r[0])]
        if a:
            out.append(("end",))
        if u < NT:
            out.append(("mask",))
        if u % GT == GT - 1:
            out += self.turns(u)
        return out

    def projects(self, u):
        return u > GT and self.attend(u - 1)[1] == NQ - 1

    def turns(self, u):
        return [("turn_m", u)] * (u < NT) + [("turn_o", u)] * (u >= GT)

    def dots(self, u):
        return [(u, k, hp) for k in range(-(-self.width(u) // GW)) for hp in range(HI // 2)] if u < NT and self.tile(u) else []

    def use_dots(self, u, k, hp):
        self.use("dot", ("dot", u, k, hp))

    def use(self, kind, key):
        self.count[kind] = self.count.get(kind, 0) + 1
        self.slot[key] = (len(self.order) % RING, self.count[kind])
        self.order.append((kind, self.count[kind]))

    def tile(self, u):
        return GT * self.groups[u // GT] + u % GT

    def side(self, g):
        return self.groups.index(g) % 2

    def width(self, u):
        return P * (self.tile(u) + 1)

    def parts(self, u):
        n = self.width(u)
        return [(k, min(PW, n - k * PW)) for k in range((n + PW - 1) // PW)]

    def attend(self, u):
        return (self.groups[(u - GT) // GT], (u - GT) % GT) if u >= GT else None


def prepare(nc, b, x, w, tabs, consts, keep, scratch):
    K99, V, kiT, wi = keep
    qkD, qiD = scratch
    identf, identb = consts
    with ExitStack() as ctx:
        sb = lambda n, s, d: ctx.enter_context(nc.sbuf_tensor(n, s, d))
        ps = lambda n, s, d: ctx.enter_context(nc.psum_tensor(n, s, d))
        sems = []

        def sem(n):
            sems.append(ctx.enter_context(nc.semaphore(n)))
            return sems[-1]

        xn = sb("xn", [P, NT, D], FP32)
        stats = sb("stats", [P, NT, 6], FP32)
        mv = sb("mv", [P, NT, 2], FP32)
        sd = sb("sd", [P, NT], FP32)
        rstd = sb("rstd", [P, NT], FP32)
        eps = sb("eps", [P, 1], FP32)
        xnT = sb("xnT", [P, KD, S], FP32)
        wqkv = sb("wqkv", [P, KD, 3 * D + HI], FP32)
        wqi = sb("wqi", [P, KD, HI * DI], FP32)
        wki = sb("wki", [P, KD, 2 * DI], FP32)
        cos = sb("cos", [P, NT, DK], FP32)
        sin = sb("sin", [P, NT, DK // 2], FP32)
        nsin = sb("nsin", [P, NT, DK // 2], FP32)
        t1 = sb("t1", [P, 2, 2 * D], FP32)
        t2 = sb("t2", [P, 2, 2 * D], FP32)
        rot = sb("rot", [P, 3, 2 * D], FP32)
        rem = sb("rem", [P, 3, 2 * D], FP32)
        split = sb("split", [P, 3, 2 * H * PARTS * DK], BF16)
        stage = sb("stage", [2 * PARTS * DK, 2, 2, H // 2, GW], BF16)
        qi = sb("qi", [P, 2, 2, GW], FP32)
        pT = [ps(f"pT{k}", [P, KD, P], FP32) for k in range(2)]
        pA = [ps(f"pA{k}", [P, 512], FP32) for k in range(2)]
        pB = [ps(f"pB{k}", [P, 512], FP32) for k in range(2)]
        pS = [ps(f"pS{k}", [P, H // 2, P], BF16) for k in range(2)]
        x_in = [sem(f"x_in{g}") for g in range(NG)]
        w_in, wi_in, tab_in = sem("w_in"), sem("wi_in"), sem("tab_in")
        eps_set, stats_done, mv_done, sd_done, rstd_done = (sem(n) for n in ("eps_set", "stats_done", "mv_done", "sd_done", "rstd_done"))
        xn_done, turned, xT_done = sem("xn_done"), sem("turned"), sem("xT_done")
        qkv_done, v_taken, t_done = sem("qkv_done"), sem("v_taken"), sem("t_done")
        rot_done, hi_done, rem_done, mid_done, lo_done = (sem(n) for n in ("rot_done", "hi_done", "rem_done", "mid_done", "lo_done"))
        split_turned, staged, index_done, index_taken = (sem(n) for n in ("split_turned", "staged", "index_done", "index_taken"))
        stored = [sem(f"stored{k}") for k in range(2)]
        qi_out, k_in = [sem(f"qi_out{k}") for k in range(2)], sem("k_in")

        wide = lambda a, i: a[:, i % 3, :].rearrange("p (h d) -> p h d", d=DK)
        parts = lambda i: split[:, i % 3, :].rearrange("p (h s d) -> p h s d", s=PARTS, d=DK)

        with nc.Block() as block:

            @block.sync
            def _(sp):
                xb = x.rearrange("(b t p) d -> b p t d", b=B, p=P)
                for g in range(NG):
                    sp.dma_start(xn[:, g * GT:(g + 1) * GT, :], xb[bass.ds(b, 1), :, g * GT:(g + 1) * GT, :].rearrange("o p t d -> (o p) t d")).then_inc(x_in[g], 16)
                sp.dma_start(wqkv[:, :, 0:3 * D], w["qkvT"].rearrange("(k p) n -> p k n", p=P)).then_inc(w_in, 16)
                sp.dma_start(wqkv[:, :, 3 * D:], w["wiT"].rearrange("(k p) n -> p k n", p=P)).then_inc(w_in, 16)
                for a, t in zip((cos, sin, nsin), tabs):
                    sp.dma_start(a[:], t).then_inc(tab_in, 16)
                sp.dma_start(wqi[:], w["qiT"].rearrange("(k p) n -> p k n", p=P)).then_inc(wi_in, 16)
                for c in range(2):
                    sp.dma_start(wki[:, :, c * DI:(c + 1) * DI], w["kiT"].rearrange("(k p) n -> p k n", p=P)).then_inc(wi_in, 16)
                def load_keys(g):
                    sp.wait_ge(stored[g % 2], 32 * (g // 2 + 1))
                    for r, part in enumerate(K_SLOTS):
                        sp.dma_start(K99[r * DK:(r + 1) * DK, :, g * GW:(g + 1) * GW],
                                     qkD[1].rearrange("(h s d) t -> s d h t", s=PARTS, d=DK)[part][:, :, g * GW:(g + 1) * GW]).then_inc(k_in, 16)

                for g in range(NG):
                    sp.wait_ge(staged, 2 * GT * (g + 1))
                    for c in range(2):
                        sp.dma_start(qkD[c].rearrange("(hp p) t -> p hp t", p=2 * PARTS * DK)[:, :, g * GW:(g + 1) * GW],
                                     stage[:, g % 2, c]).then_inc(stored[g % 2], 16)
                    if g >= 1:
                        load_keys(g - 1)
                load_keys(NG - 1)
                for g in range(NG):
                    sp.wait_ge(index_taken, 3 * (g + 1))
                    sp.dma_start(qiD[:, :, g * GW:(g + 1) * GW], qi[:, g % 2]).then_inc(qi_out[g % 2], 16)
                sp.wait_ge(k_in, 16 * len(K_SLOTS) * NG)
                for k in range(2):
                    sp.wait_ge(qi_out[k], 16 * (NG // 2))

            @block.vector
            def _(dve):
                dve.memset(eps[:], EPS).then_inc(eps_set, 1)
                for i in range(NT):
                    if i % GT == 0:
                        dve.wait_ge(x_in[i // GT], 16)
                    dve.bn_stats(out=stats[:, i, :], in_=xn[:, i, :]).then_inc(stats_done, 1)
                for i in range(NT):
                    dve.wait_ge(stats_done, i + 1)
                    dve.bn_aggr(out=mv[:, i, :], in_=stats[:, i, :]).then_inc(mv_done, 1)
                dve.wait_ge(sd_done, 1)
                dve.reciprocal(rstd[:], sd[:]).then_inc(rstd_done, 1)
                dve.wait_ge(rstd_done, 1)
                for i in range(NT):
                    dve.tensor_scalar(xn[:, i, :], xn[:, i, :], mv[:, i, 0:1], rstd[:, i:i + 1], ALU.subtract, ALU.mult).then_inc(xn_done, 1)
                dve.wait_ge(tab_in, 16 * len(tabs))

                def rope(i):
                    q = pA[i % 2][:, :].rearrange("p (h d) -> p h d", d=DK)
                    a = t1[:, i % 2, :].rearrange("p (h d) -> p h d", d=DK)
                    c = t2[:, i % 2, :].rearrange("p (h d) -> p h d", d=DK)
                    bc = lambda t, n: t[:, i, :].unsqueeze(1).to_broadcast([P, 2 * H, n])
                    dve.wait_ge(qkv_done, i + 1)
                    if i >= 2:
                        dve.wait_ge(rot_done, i - 1)
                    dve.tensor_tensor(a, q, bc(cos, DK), ALU.mult).then_inc(t_done, 1)
                    dve.tensor_tensor(c[:, :, 0::2], q[:, :, 1::2], bc(nsin, DK // 2), ALU.mult).then_inc(t_done, 1)
                    dve.tensor_tensor(c[:, :, 1::2], q[:, :, 0::2], bc(sin, DK // 2), ALU.mult).then_inc(t_done, 1)

                def take_parts(i):
                    g, t = i // GT, i % GT
                    dve.wait_ge(split_turned, 2 * (i + 1))
                    if t == 0 and g >= 2:
                        dve.wait_ge(stored[g % 2], 32 * (g // 2))
                    for c in range(2):
                        dve.tensor_copy(stage[:, g % 2, c, :, t * P:(t + 1) * P], pS[c][0:2 * PARTS * DK, :, :]).then_inc(staged, 1)

                for i in range(NT + 3):
                    if i < NT:
                        rope(i)
                    if i >= 3:
                        take_parts(i - 3)

            @block.gpsimd
            def _(pool):
                for i in range(NT + 2):
                    if i < NT:
                        pool.wait_ge(t_done, 3 * (i + 1))
                        if i >= 3:
                            pool.wait_ge(rem_done, i - 2)
                            pool.wait_ge(hi_done, i - 2)
                        pool.tensor_tensor(rot[:, i % 3, :], t1[:, i % 2, :], t2[:, i % 2, :], ALU.add).then_inc(rot_done, 1)
                    if 1 <= i <= NT:
                        k = i - 1
                        pool.wait_ge(hi_done, k + 1)
                        pool.wait_ge(rot_done, k + 1)
                        if k >= 3:
                            pool.wait_ge(lo_done, k - 2)
                            pool.wait_ge(mid_done, k - 2)
                        pool.tensor_tensor(wide(rem, k), wide(rot, k), parts(k)[:, :, 0, :], ALU.subtract).then_inc(rem_done, 1)
                    if i >= 2:
                        k = i - 2
                        pool.wait_ge(mid_done, k + 1)
                        pool.wait_ge(rem_done, k + 1)
                        pool.tensor_tensor(parts(k)[:, :, 2, :], wide(rem, k), parts(k)[:, :, 1, :], ALU.subtract).then_inc(lo_done, 1)

            @block.scalar
            def _(act):
                act.wait_ge(mv_done, NT)
                act.wait_ge(eps_set, 1)
                act.activation(sd[:], mv[:, :, 1], ACT.Sqrt, bias=eps[:, 0:1]).then_inc(sd_done, 1)
                for i in range(NT + 2):
                    if i < NT:
                        act.wait_ge(turned, i + 1)
                        act.activation(xnT[:, :, i * P:(i + 1) * P], pT[i % 2][:], ACT.Copy).then_inc(xT_done, 1)
                    if 1 <= i <= NT:
                        k = i - 1
                        act.wait_ge(qkv_done, k + 1)
                        act.activation(V[:, k, 0:H * VW].rearrange("p (h d) -> p h d", d=VW)[:, :, 0:DK],
                                       pB[k % 2][:, 0:D].rearrange("p (h d) -> p h d", d=DK), ACT.Copy).then_inc(v_taken, 1)
                        act.activation(wi[:, k, :], pB[k % 2][:, D:D + HI], ACT.Copy).then_inc(v_taken, 1)
                        act.wait_ge(rot_done, k + 1)
                        if k >= 3:
                            act.wait_ge(split_turned, 2 * (k - 2))
                        act.activation(parts(k)[:, :, 0, :], wide(rot, k), ACT.Copy).then_inc(hi_done, 1)
                    if i >= 2:
                        k = i - 2
                        act.wait_ge(rem_done, k + 1)
                        act.activation(parts(k)[:, :, 1, :], wide(rem, k), ACT.Copy).then_inc(mid_done, 1)
                banks = pA + pB
                for n in range(3 * NG):
                    g, m = n // 3, n % 3
                    act.wait_ge(index_done, n + 1)
                    if m == 0 and g >= 2:
                        act.wait_ge(qi_out[g % 2], 16 * (g // 2))
                    dst = kiT[:, g * GW:(g + 1) * GW] if m == 2 else qi[:, g % 2, m, :]
                    act.activation(dst, banks[n % 4][:], ACT.Copy).then_inc(index_taken, 1)

            @block.tensor
            def _(pe):
                def turn(i):
                    pe.wait_ge(xn_done, i + 1)
                    if i >= 2:
                        pe.wait_ge(xT_done, i - 1)
                    for k in range(KD):
                        mm = pe.transpose(pT[i % 2][:, k, :], xn[:, i, k * P:(k + 1) * P], identf[:])
                    mm.then_inc(turned, 1)

                def project(i):
                    pe.wait_ge(xT_done, i + 1)
                    if i >= 2:
                        pe.wait_ge(t_done, 3 * (i - 1))
                        pe.wait_ge(v_taken, 2 * (i - 1))
                    for dst, c0, c1 in ((pA, 0, 2 * D), (pB, 2 * D, 3 * D + HI)):
                        for k in range(KD):
                            mm = pe.matmul(dst[i % 2][:, 0:c1 - c0], xnT[:, k, i * P:(i + 1) * P], wqkv[:, k, c0:c1],
                                           start=(k == 0), stop=(k == KD - 1))
                    mm.then_inc(qkv_done, 1)

                def turn_parts(i):
                    pe.wait_ge(lo_done, i + 1)
                    for c in range(2):
                        if i >= 1:
                            pe.wait_ge(staged, 2 * (i - 1) + c + 1)
                        for hp in range(H // 2):
                            c0 = (c * (H // 2) + hp) * 2 * PARTS * DK
                            mm = pe.transpose(pS[c][0:2 * PARTS * DK, hp, :], split[:, i % 3, c0:c0 + 2 * PARTS * DK], identb[:])
                        mm.then_inc(split_turned, 1)

                turn(0)
                pe.wait_ge(w_in, 32)
                for i in range(NT + 3):
                    if i + 1 < NT:
                        turn(i + 1)
                    if i < NT:
                        project(i)
                    if i >= 3:
                        turn_parts(i - 3)
                pe.wait_ge(wi_in, 48)
                pe.wait_ge(t_done, 3 * NT)
                pe.wait_ge(v_taken, 2 * NT)
                banks = pA + pB
                for n in range(3 * NG):
                    g, m = n // 3, n % 3
                    if n >= 4:
                        pe.wait_ge(index_taken, n - 3)
                    for k in range(KD):
                        lhs = wki[:, k, :] if m == 2 else wqi[:, k, m * P:(m + 1) * P]
                        mm = pe.matmul(banks[n % 4][:], lhs, xnT[:, k, g * GW:(g + 1) * GW], start=(k == 0), stop=(k == KD - 1))
                    mm.then_inc(index_done, 1)

        clear(nc, sems)


def clear(nc, sems):
    nc.all_engine_barrier()
    for s in sems:
        nc.sync.sem_clear(s)
    nc.all_engine_barrier()


def attention(nc, b, x, consts, keep, scratch):
    K99, V, kiT, wi = keep
    qkD, qiD, x2D = scratch
    identf, identb, hide, woT, tables = consts
    key_step, block_step, ranks = tables[:, 0:P], tables[:, P:P + NT], tables[:, P + NT:P + NT + RANKS]
    minus_most = tables[:, P + NT + RANKS:]
    st = Steps()
    with ExitStack() as ctx:
        sb = lambda n, s, d: ctx.enter_context(nc.sbuf_tensor(n, s, d))
        ps = lambda n, s, d: ctx.enter_context(nc.psum_tensor(n, s, d))
        sems = []

        def sem(n):
            sems.append(ctx.enter_context(nc.semaphore(n)))
            return sems[-1]

        Q99 = [sb(f"Q99_{k}", [KM, H, GW], BF16) for k in range(2)]
        maskT = [sb(f"maskT{k}", [P, GT * (max(st.groups[k::2]) + 1), GW], FP8) for k in range(2)]
        sc = sb("sc", [P, 2, S], FP32)
        above = sb("above", [P, S], FP8)
        unread = sb("unread", [P, S], FP8)
        best = sb("best", [P, 16], FP32)
        small = iter(range(24))
        row = sb("small", [P, 24], FP32)

        def columns(n):
            c = [next(small) for _ in range(n)]
            return row[:, c[0]:c[0] + n]

        rank = columns(1)
        is_rank = sb("is_rank", [P, RANKS], FP32)
        picked = sb("picked", [P, 2, RANKS], FP32)
        last2 = columns(2)
        bad = columns(1)
        one = columns(1)
        flag = sb("flag", [1, 1], mybir.dt.int32)
        passed = columns(1)
        sides = columns(3)
        f = columns(2)
        exceeds = columns(2)
        terms = columns(3)
        curve = columns(2)
        v = columns(1)
        side = columns(1)
        at = columns(1)
        last_half = columns(1)
        minus_t = columns(1)
        zero_bias = columns(1)
        relu = sb("relu", [P, 4, GW], FP32)
        work = sb("work", [P, S], FP32)
        bias = work[:, 0:S // 2].bitcast(BF16)
        junk = work[:, S // 2:].bitcast(BF16).rearrange("p (k w) -> p k w", k=2)
        mx = sb("mx", [P, 2, H], FP32)
        mall = sb("mall", [P, H], FP32)
        mrem = sb("mrem", [P, H], FP32)
        msplit = sb("msplit", [P, PARTS, H], BF16)
        mT = sb("mT", [PARTS * H, GW], BF16)
        qi = sb("qi_t", [P, 2, 2, P], FP32)
        prob = sb("prob", [P, 4, 2, GW], FP32)
        oT = sb("oT", [P, GW], FP32)
        rsum = sb("rsum", [P, GT, QUAD], FP32)
        otok = sb("otok", [P, GT, D], FP32)
        otokT = relu[:, 0:2, :]
        xg = sb("xg", [P, GT, D], FP32)
        ring = [ps(f"ring{k}", [P, 2, 512], FP32) for k in range(RING)]
        pO = ps("pO", [P, GW], FP32)
        pX = ps("pX", [P, 512], FP32)

        kinds = ("exp", "mask", "max", "out", "dot", "check")
        filled = {k: sem(f"{k}_filled") for k in kinds}
        taken = {k: sem(f"{k}_taken") for k in kinds}
        q_in = [sem(f"q_in{k}") for k in range(2)]
        qm_in = sem("qm_in")
        qi_in = [sem(f"qi_in{k}") for k in range(2)]
        x_in, x2_out = sem("xg_in"), sem("x2_out")
        weighted = sem("weighted")
        counted, ranged, pool_chain = sem("counted"), sem("ranged"), sem("pool_chain")
        act_chain = sem("act_chain")
        consts_set, bad_done, long_way = sem("consts_set"), sem("bad_done"), sem("long_way")
        summed, causal_done, chain = sem("summed"), sem("causal_done"), sem("chain")
        bias_done, msplit_done, m_turned, mT_done = sem("bias_done"), sem("msplit_done"), sem("m_turned"), sem("mT_done")
        pv_done, oT_done, o_turned, normed = sem("pv_done"), sem("oT_done"), sem("o_turned"), sem("normed")
        ot_turned, otT_done = sem("ot_turned"), sem("otT_done")

        def view(key, w=PW):
            return ring[st.slot[key][0]][:, :, :].rearrange("p a b -> p (a b)")[:, 0:w]

        def add_of(c, h):
            return (HI - 1) * ((c - 1) // (HI // 2)) + h

        def dots_of(u, k):
            return k * GW, min(GW, st.width(u) - k * GW)

        def nth(u):
            return sum(1 for v in range(u + 1) if st.tile(v))

        chunks = [0]
        for u in range(st.n):
            a = st.attend(u)
            chunks.append(chunks[-1] + (GT * (a[0] + 1) if a else 0))
        dots_upto = {}
        for (key, (_, c)) in st.slot.items():
            if key[0] == "dot":
                dots_upto[key[1]] = max(dots_upto.get(key[1], 0), c)

        with nc.Block() as block:

            @block.sync
            def _(sp):
                xb = x.rearrange("(b t p) d -> b p t d", b=B, p=P)
                x2 = x2D.rearrange("(b t p) d -> b p t d", b=B, p=P)

                def load_q(g):
                    for r, part in enumerate(Q_SLOTS):
                        sp.dma_start(Q99[st.side(g)][r * DK:(r + 1) * DK, :, :],
                                     qkD[0].rearrange("(h s d) t -> s d h t", s=PARTS, d=DK)[part][:, :, g * GW:(g + 1) * GW]).then_inc(q_in[st.side(g)], 16)

                def load_qi(u):
                    i = st.tile(u)
                    sp.dma_start(qi[:, u % 2], qiD[:, :, i * P:(i + 1) * P]).then_inc(qi_in[u % 2], 16)

                def store(u):
                    g, _ = st.attend(u)
                    sp.wait_ge(taken["out"], st.slot[("out", u)][1])
                    sp.dma_start(x2[bass.ds(b, 1), :, g * GT:(g + 1) * GT, :].rearrange("o p t d -> (o p) t d"), xg[:]).then_inc(x2_out, 16)

                if st.tile(0):
                    load_qi(0)
                load_qi(1)
                load_q(st.groups[0])
                if st.tile(0):
                    sp.wait_ge(filled["dot"], dots_upto[0])
                load_qi(2)
                load_q(st.groups[1])
                for u in range(st.n):
                    a = st.attend(u)
                    if u + 3 < NT and st.tile(u + 3):
                        sp.wait_ge(filled["dot"], dots_upto[u + 1 if st.tile(u + 1) else u - 1])
                        load_qi(u + 3)
                    if u > GT and st.attend(u - 1)[1] == NQ - 1:
                        store(u - 1)
                    if a and a[1] == 1:
                        if a[0] != st.groups[0]:
                            sp.wait_ge(x2_out, 16 * st.groups.index(a[0]))
                        sp.dma_start(xg[:], xb[bass.ds(b, 1), :, a[0] * GT:(a[0] + 1) * GT, :].rearrange("o p t d -> (o p) t d")).then_inc(x_in, 16)
                    if u < NT and u % GT == GT - 1:
                        sp.wait_ge(mT_done, u + 1)
                        for r in range(PARTS):
                            sp.dma_start(Q99[u // GT % 2][KR + r:KR + r + 1, :, :], mT[r * H:(r + 1) * H, :]).then_inc(qm_in, 16)
                    if a and a[1] == NQ - 1:
                        n = st.groups.index(a[0]) + 2
                        if n < NG:
                            sp.wait_ge(pv_done, chunks[u + 1])
                            load_q(st.groups[n])
                store(st.n - 1)
                sp.wait_ge(x2_out, 16 * NG)

            @block.vector
            def _(dve):
                links = [0]

                def link(ins):
                    links[0] += 1
                    ins.then_inc(chain, 1)
                    dve.wait_ge(chain, links[0])

                def choose(u):
                    i, n = st.tile(u), st.width(u)
                    if i == 0:
                        dve.wait_ge(filled["mask"], u)
                        dve.memset(bias[:, 0:n], 0.0).then_inc(bias_done, 1)
                        return
                    scores, rest = sc[:, u % 2, 0:n], work[:, 0:n]
                    dve.wait_ge(counted, COUNTS * nth(u))
                    if u >= 1:
                        dve.wait_ge(filled["mask"], u)
                    link(dve.tensor_scalar(rank[:], f[:, u % 2:u % 2 + 1], -0.5, (2 * TOPK - n) / 2, ALU.mult, ALU.add))
                    link(dve.tensor_scalar(is_rank[:], ranks, rank[:, 0:1], None, ALU.is_equal))
                    link(dve.scalar_tensor_tensor(rest, above[:, 0:n], BELOW, scores, ALU.mult, ALU.min))
                    link(dve.max(out=best[:, 0:8], in_=rest))
                    link(dve.match_replace(out=rest, in_to_replace=best[:, 0:8], in_values=rest, imm_value=TAKEN))
                    link(dve.max(out=best[:, 8:16], in_=rest))
                    for a in range(2):
                        link(dve.tensor_tensor(picked[:, a, :], is_rank[:], best[:, a:a + RANKS], ALU.mult))
                    link(dve.tensor_reduce(last2[:], picked[:], AX.X, ALU.add))
                    dve.tensor_tensor(bad[:], last2[:, 1:2], last2[:, 0:1], ALU.is_ge).then_inc(bad_done, 1)
                    link(dve.tensor_scalar(bias[:, 0:n], scores, last2[:, 0:1], HIDE, ALU.is_lt, ALU.mult))
                    c = st.slot[("check", u)][1]
                    dve.wait_ge(filled["check"], c)
                    dve.tensor_copy(flag[:], view(("check", u))[0:1, 0:1]).then_inc(taken["check"], 1)
                    dve.wait_ge(taken["check"], c)
                    rows = dve.value_load(flag[0:1, 0:1])
                    with dve.If(rows > 0):
                        with dve.Fori(0, TOPK // 8):
                            dve.max(out=best[:, 0:8], in_=scores).then_inc(long_way, 1)
                            dve.wait_ge(long_way, 1)
                            dve.match_replace(out=scores, in_to_replace=best[:, 0:8], in_values=scores, imm_value=TAKEN).then_inc(long_way, 1)
                            dve.wait_ge(long_way, 2)
                            dve.sem_clear(long_way)
                        dve.tensor_scalar(bias[:, 0:n], scores, TAKEN, HIDE, ALU.not_equal, ALU.mult).then_inc(long_way, 1)
                        dve.wait_ge(long_way, 1)
                        dve.sem_clear(long_way)
                    dve.memset(passed[:], 0.0).then_inc(bias_done, 1)

                def weigh(u, k, hp):
                    k0, w = dots_of(u, k)
                    slot, c = st.slot[("dot", u, k, hp)]
                    dve.wait_ge(filled["dot"], c)
                    for a, done in ((0, weighted), (1, taken["dot"])):
                        h = 2 * hp + a
                        n = add_of(c, h)
                        if h and n > 4:
                            dve.wait_ge(summed, n - 4)
                        dve.tensor_scalar(relu[:, n % 4, 0:w] if h else sc[:, u % 2, k0:k0 + w], ring[slot][:, a, 0:w], 0.0,
                                          wi[:, st.tile(u), h:h + 1], ALU.max, ALU.mult).then_inc(done, 1)

                def maximum(u, h, k):
                    w = dict(st.parts(u))[k]
                    key = ("max", u, h, k)
                    c = st.slot[key][1]
                    dve.wait_ge(filled["max"], c)
                    if c > 2:
                        dve.wait_ge(taken["max"], c - 2)
                    dve.tensor_tensor_reduce(out=junk[:, c % 2, 0:w], in0=view(key, w), in1=bias[:, k * PW:k * PW + w], scale=1.0, scalar=-3.0e38,
                                             op0=ALU.add, op1=ALU.max, accum_out=mx[:, k, h:h + 1]).then_inc(taken["max"], 1)

                def split_maxima(u):
                    dve.wait_ge(taken["max"], st.slot[("max", u, H - 1, len(st.parts(u)) - 1)][1])
                    last = mx[:, 0, :]
                    if len(st.parts(u)) == 2:
                        link(dve.tensor_tensor(mall[:], mx[:, 0, :], mx[:, 1, :], ALU.max))
                        last = mall[:]
                    link(dve.tensor_scalar(mrem[:], last, -1.0, None, ALU.mult))
                    if u >= 1:
                        dve.wait_ge(m_turned, u)
                    for r in range(PARTS - 1):
                        link(dve.tensor_copy(msplit[:, r, :], mrem[:]))
                        link(dve.tensor_tensor(mrem[:], mrem[:], msplit[:, r, :], ALU.subtract))
                    dve.tensor_copy(msplit[:, PARTS - 1, :], mrem[:]).then_inc(msplit_done, 1)

                def norm(u):
                    g, hq = st.attend(u)
                    dve.wait_ge(o_turned, u - GT + 1)
                    o = pX[:, :].rearrange("p (t h d) -> p t h d", t=GT, d=32)
                    link(dve.reciprocal(rsum[:], o[:, :, :, DK]))
                    if hq == 0 and g != st.groups[0]:
                        dve.wait_ge(ot_turned, KD * st.groups.index(g))
                    dst = otok[:, :, hq * QUAD * DK:(hq + 1) * QUAD * DK].rearrange("p t (h d) -> p t h d", d=DK)
                    for t in range(GT):
                        dve.tensor_tensor(dst[:, t], o[:, t, :, 0:DK], rsum[:, t].unsqueeze(2).to_broadcast([P, QUAD, DK]),
                                          ALU.mult).then_inc(normed, 1)

                def residual(u):
                    g, _ = st.attend(u)
                    dve.wait_ge(filled["out"], st.slot[("out", u)][1])
                    dve.wait_ge(x_in, 16 * (st.groups.index(g) + 1))
                    flat = xg[:, :, :].rearrange("p t d -> p (t d)")
                    dve.tensor_tensor(flat, view(("out", u)), flat, ALU.add).then_inc(taken["out"], 1)

                dve.memset(one[:], 1.0).then_inc(consts_set, 1)
                dve.memset(zero_bias[:], ZERO).then_inc(consts_set, 1)
                dve.memset(last_half[:], 0.5 ** (TRIALS + 1)).then_inc(consts_set, 1)
                for e in st.dots(0) + st.dots(1):
                    weigh(*e)
                for u in range(st.n):
                    if st.projects(u):
                        norm(u - 1)
                    if u < NT:
                        choose(u)
                        dve.wait_ge(bias_done, u + 1)
                    if u > GT and not st.projects(u):
                        norm(u - 1)
                    owed = None
                    for e in st.plan[u]:
                        uses = {"a": 1, "m": 1, "d": 1, "mask": 1, "check": 1}.get(e[0], 0)
                        if e == ("project", KD):
                            owed = RING - 1
                        elif owed is not None and uses:
                            owed -= uses
                            if owed < 0:
                                residual(u - 1)
                                owed = None
                        if e[0] == "m":
                            maximum(u, *e[1:])
                        elif e[0] == "d":
                            weigh(u + 2, *e[1:])
                    if owed is not None:
                        residual(u - 1)
                    if u < NT:
                        split_maxima(u)
                norm(st.n - 1)
                residual(st.n - 1)

            @block.gpsimd
            def _(pool):
                links = [0]

                def link(ins):
                    links[0] += 1
                    ins.then_inc(pool_chain, 1)
                    pool.wait_ge(pool_chain, links[0])

                most = lambda n: 2 * TOPK - 2 - n

                def set_range(u):
                    n = st.width(u)
                    pool.wait_ge(counted, COUNTS * (nth(u) - 1) + 3)
                    link(pool.tensor_scalar(exceeds[:], sides[:, 0:2], most(n), None, ALU.is_gt))
                    link(pool.tensor_tensor(terms[:, 0:1], exceeds[:, 0:1], exceeds[:, 1:2], ALU.subtract))
                    link(pool.tensor_scalar(curve[:, 1:2], terms[:, 0:1], (n + 1 / 3) * STEP, None, ALU.mult))
                    link(pool.tensor_tensor(terms[:, 1:2], exceeds[:, 0:1], exceeds[:, 1:2], ALU.add))
                    link(pool.tensor_scalar(terms[:, 2:3], sides[:, 2:3], -SPREAD / min(n - P, MEAN_OF), None, ALU.mult))
                    link(pool.tensor_scalar(curve[:, 0:1], terms[:, 1:2], -1.0, terms[:, 2:3], ALU.add, ALU.mult))
                    pool.tensor_scalar(v[:, 0:1], exceeds[:, 0:1], 0.5, None, ALU.subtract).then_inc(ranged, 1)

                def sum_heads(u, k, hp):
                    n = st.width(u)
                    k0, w = dots_of(u, k)
                    part = sc[:, u % 2, k0:k0 + w]
                    c = st.slot[("dot", u, k, hp)][1]
                    pool.wait_ge(weighted, c)
                    pool.wait_ge(taken["dot"], c)
                    for h in (2 * hp, 2 * hp + 1):
                        if h:
                            a = add_of(c, h)
                            if a > 1:
                                pool.wait_ge(summed, a - 1)
                            pool.tensor_tensor(part, part, relu[:, a % 4, 0:w], ALU.add).then_inc(summed, 1)
                    if hp == HI // 2 - 1:
                        pool.wait_ge(summed, add_of(c, HI - 1))
                        blocks = part.rearrange("p (j q) -> p j q", q=P)
                        m = w // P
                        link(pool.tensor_tensor(blocks, blocks, key_step.unsqueeze(1).to_broadcast([P, m, P]), ALU.add))
                        link(pool.tensor_tensor(blocks, blocks, block_step[:, k0 // P:k0 // P + m].unsqueeze(2).to_broadcast([P, m, P]), ALU.add))
                        if k0 + w == n:
                            own = sc[:, u % 2, n - P:n]
                            pool.affine_select(out=own, in_=own, compare_op=ALU.is_ge, fill=CAUSAL,
                                               base=0, pattern=[[-1, P]], channel_multiplier=1).then_inc(causal_done, 1)

                for e in st.dots(0) + st.dots(1):
                    sum_heads(*e)
                if st.tile(0):
                    set_range(0)
                for u in range(NT):
                    for e in st.plan[u]:
                        if e[0] == "d":
                            sum_heads(u + 2, *e[1:])
                        elif e == ("c", 2):
                            set_range(u + 1)

            @block.scalar
            def _(act):
                def exps(u, j, p):
                    g, _ = st.attend(u)
                    c0 = max(0, j - GT * g) * P
                    n = chunks[u] + j
                    slot, c = st.slot[("exp", u, j, p)]
                    act.wait_ge(filled["exp"], c)
                    if p == 0 and n >= 2:
                        act.wait_ge(pv_done, n - 1)
                    act.activation(prob[:, (2 * n + p) % 4, :, c0:GW], ring[slot][:, :, c0:GW], ACT.Exp, scale=float(DK) ** -0.5).then_inc(taken["exp"], 1)

                def quad_out(u):
                    act.wait_ge(pv_done, chunks[u + 1])
                    if u > GT:
                        act.wait_ge(o_turned, u - GT)
                    act.activation(oT[:], pO[:], ACT.Copy).then_inc(oT_done, 1)

                def mask_out(u):
                    i = st.tile(u)
                    key = ("mask", u)
                    act.wait_ge(filled["mask"], u + 1)
                    v = view(key).bitcast(BF16).rearrange("p (j q) -> p j q", q=P)
                    m = maskT[u // GT % 2]
                    act.activation(m[:, 0:i + 1, (u % GT) * P:(u % GT + 1) * P], v[:, 0:i + 1, :], ACT.Copy,
                                   scale=1.0 / HIDE, saturate=False).then_inc(taken["mask"], 1)

                def m_out(u):
                    act.wait_ge(m_turned, u + 1)
                    if u % GT == 0 and u >= GT:
                        act.wait_ge(qm_in, 16 * PARTS * (u // GT))
                    act.activation(mT[:, (u % GT) * P:(u % GT + 1) * P], pX[0:PARTS * H, :].bitcast(BF16)[:, 0:P], ACT.Copy).then_inc(mT_done, 1)

                def final(u, k):
                    n = st.groups.index(st.attend(u)[0])
                    if k == 0 and u + 1 < NT:
                        c = max(c for (key, (_, c)) in st.slot.items() if key[0] == "dot" and key[1] <= u + 2)
                        act.wait_ge(summed, add_of(c, HI - 1))
                    if k < KD:
                        act.wait_ge(ot_turned, KD * n + k + 1)
                        act.activation(otokT[:, k, :], pX[:], ACT.Copy).then_inc(otT_done, 1)

                links = [0]

                def link(ins):
                    links[0] += 1
                    ins.then_inc(act_chain, 1)
                    act.wait_ge(act_chain, links[0])

                def trial(u, k):
                    if k == 0:
                        act.wait_ge(ranged, nth(u))
                    else:
                        link(act.activation(side[:], f[:, u % 2:u % 2 + 1], ACT.Sign, bias=minus_most[:, st.tile(u):st.tile(u) + 1]))
                        link(act.activation(v[:], side[:], ACT.Identity, bias=v[:, 0:1], scale=0.5 ** (k + 1)))
                    if k == TRIALS:
                        link(act.activation(v[:], v[:], ACT.Identity, bias=last_half[:, 0:1]))
                    link(act.activation(at[:], v[:], ACT.Identity, bias=curve[:, 1:2], scale=curve[:, 0:1]))
                    link(act.activation(minus_t[:], at[:], ACT.Identity, scale=v[:, 0:1]))

                def count(u, k):
                    n = min(st.width(u) - P, MEAN_OF) if k == 2 else st.width(u)
                    c = COUNTS * (nth(u) - 1) + k
                    if k == 0:
                        act.wait_ge(causal_done, nth(u))
                        act.wait_ge(consts_set, 3)
                    if k == COUNTS - 1 and u >= 1:
                        act.wait_ge(bias_done, u)
                    if c:
                        act.wait_ge(counted, c)
                    if k >= 3:
                        trial(u, k - 3)
                    scores = sc[:, u % 2, 0:n]
                    off = unread[:, 0:n]
                    if k == 0:
                        ins = act.activation(off, scores, ACT.Sign, accum_out=sides[:, 0:1], saturate=False)
                    elif k == 1:
                        ins = act.activation(off, scores, ACT.Sign, bias=zero_bias[:, 0:1], accum_out=sides[:, 1:2], saturate=False)
                    elif k == 2:
                        ins = act.activation(off, scores, ACT.Abs, accum_out=sides[:, 2:3], saturate=False)
                    else:
                        ins = act.activation(above[:, 0:n] if k == COUNTS - 1 else off, scores, ACT.Sign, bias=minus_t[:, 0:1],
                                             accum_out=f[:, u % 2:u % 2 + 1], saturate=False)
                    ins.then_inc(counted, 1)

                if st.tile(0):
                    for k in range(COUNTS):
                        count(0, k)
                for u in range(st.n):
                    for e in st.plan[u]:
                        if e[0] == "a":
                            exps(u, *e[1:])
                        elif e[0] == "c":
                            count(u + 1, e[1])
                        elif e[0] == "project":
                            final(u - 1, e[1])
                        elif e[0] == "end":
                            quad_out(u)
                        elif e[0] == "mask":
                            mask_out(u)
                        elif e[0] == "turn_m":
                            m_out(e[1])
                for k in range(KD):
                    final(st.n - 1, k)

            @block.tensor
            def _(pe):
                used = [0]

                def slot(key):
                    n = used[0]
                    assert st.order[n] == (key[0], st.slot[key][1])
                    used[0] += 1
                    if n >= RING:
                        kind, c = st.order[n - RING]
                        pe.wait_ge(taken[kind], c)
                    return ring[st.slot[key][0]]

                def dots(u, k, hp):
                    k0, w = dots_of(u, k)
                    if k == 0 and hp == 0:
                        pe.wait_ge(qi_in[u % 2], 16 * sum(1 for v in range(u % 2, u + 1, 2) if st.tile(v)))
                    r = slot(("dot", u, k, hp))
                    for a in range(2):
                        rows = slice(a * DI, (a + 1) * DI)
                        mm = pe.matmul(r[:, a, 0:w], qi[rows, u % 2, hp, :], kiT[rows, k0:k0 + w], start=True, stop=True)
                    mm.then_inc(filled["dot"], 1)

                def scores(u, j, p):
                    g, hq = st.attend(u)
                    c0 = max(0, j - GT * g) * P
                    r = slot(("exp", u, j, p))
                    for a in range(2):
                        h = hq * QUAD + 2 * p + a
                        pe.matmul(r[:, a, c0:GW], K99[:, h, j * P:(j + 1) * P], Q99[st.side(g)][:, h, c0:GW], start=True, stop=False)
                        mm = pe.matmul(r[:, a, c0:GW], hide[:], maskT[st.side(g)][:, j, c0:GW], start=False, stop=True)
                    mm.then_inc(filled["exp"], 1)

                def values(u, j):
                    g, hq = st.attend(u)
                    c0 = max(0, j - GT * g) * P
                    n = chunks[u] + j
                    pe.wait_ge(taken["exp"], 2 * (n + 1))
                    if j == 0 and u > GT:
                        pe.wait_ge(oT_done, u - GT)
                    for q in range(QUAD):
                        h = hq * QUAD + q
                        mm = pe.matmul(pO[32 * q:32 * q + 32, c0:GW], V[:, j, h * VW:h * VW + 32], prob[:, (2 * n + q // 2) % 4, q % 2, c0:GW],
                                       start=(j == 0), stop=(j == GT * (g + 1) - 1))
                    mm.then_inc(pv_done, 1)

                def pair(u, j, p):
                    g, hq = st.attend(u)
                    if hq == 0 and j == 0 and p == 0:
                        pe.wait_ge(qm_in, 16 * PARTS * (st.groups.index(g) + 1))
                        pe.wait_ge(taken["mask"], GT * (st.groups.index(g) + 1))
                    scores(u, j, p)
                    if p == 1 and j >= 1:
                        values(u, j - 1)

                def turn_o(u):
                    pe.wait_ge(oT_done, u - GT + 1)
                    if u < NT:
                        pe.wait_ge(mT_done, u + 1)
                    else:
                        pe.wait_ge(normed, GT * (u - GT))
                        if st.projects(u):
                            pe.wait_ge(otT_done, KD * (st.groups.index(st.attend(u - 1)[0]) + 1))
                    for t in range(GT):
                        mm = pe.transpose(pX[:, t * P:(t + 1) * P], oT[:, t * P:(t + 1) * P], identf[:])
                    mm.then_inc(o_turned, 1)

                def turn_mask(u):
                    i = st.tile(u)
                    pe.wait_ge(bias_done, u + 1)
                    slot(("mask", u))
                    v = view(("mask", u)).bitcast(BF16)
                    for j in range(i + 1):
                        mm = pe.transpose(v[:, j * P:(j + 1) * P], bias[:, j * P:(j + 1) * P], identb[:])
                    mm.then_inc(filled["mask"], 1)

                def check(u):
                    pe.wait_ge(bad_done, nth(u))
                    slot(("check", u))
                    pe.matmul(view(("check", u))[0:1, 0:1], bad[:], one[:], start=True, stop=True).then_inc(filled["check"], 1)

                def max_scores(u, h, k):
                    g, t = st.groups[u // GT], u % GT
                    w = dict(st.parts(u))[k]
                    if t == 0 and h == 0 and k == 0:
                        pe.wait_ge(q_in[st.side(g)], 16 * len(Q_SLOTS) * (st.groups.index(g) // 2 + 1))
                    r = slot(("max", u, h, k))
                    for c in range(0, w, 512):
                        cw = min(512, w - c)
                        mm = pe.matmul(r[:, c // 512, 0:cw], Q99[st.side(g)][0:KR, h, t * P:(t + 1) * P], K99[0:KR, h, k * PW + c:k * PW + c + cw], start=True, stop=True)
                    mm.then_inc(filled["max"], 1)

                def turn_m(u):
                    pe.wait_ge(msplit_done, u + 1)
                    if u > GT:
                        pe.wait_ge(normed, GT * (u - GT))
                    elif u >= 1:
                        pe.wait_ge(mT_done, u)
                    if st.projects(u):
                        pe.wait_ge(otT_done, KD * (st.groups.index(st.attend(u - 1)[0]) + 1))
                    pe.transpose(pX[0:PARTS * H, :].bitcast(BF16)[:, 0:P], msplit[:, :, :].rearrange("p r h -> p (r h)"), identb[:]).then_inc(m_turned, 1)

                def project(u, k):
                    n = st.groups.index(st.attend(u)[0])
                    if k < KD:
                        pe.wait_ge(normed, GT * (u - GT + 1))
                        if k:
                            pe.wait_ge(otT_done, KD * n + k)
                        for t in range(GT):
                            mm = pe.transpose(pX[:, t * P:(t + 1) * P], otok[:, t, k * P:(k + 1) * P], identf[:])
                        mm.then_inc(ot_turned, 1)
                        return
                    pe.wait_ge(otT_done, KD * (n + 1))
                    slot(("out", u))
                    v = view(("out", u))
                    for t in range(GT):
                        for c in range(KD):
                            mm = pe.matmul(v[:, t * D:(t + 1) * D], otokT[:, c, t * P:(t + 1) * P], woT[:, c, :], start=(c == 0), stop=(c == KD - 1))
                    mm.then_inc(filled["out"], 1)

                for e in st.dots(0) + st.dots(1):
                    dots(*e)
                for u in range(st.n):
                    for e in st.plan[u]:
                        if e[0] == "a":
                            pair(u, *e[1:])
                        elif e[0] == "m":
                            max_scores(u, *e[1:])
                        elif e[0] == "d":
                            dots(u + 2, *e[1:])
                        elif e[0] == "project":
                            project(u - 1, e[1])
                        elif e[0] == "end":
                            values(u, GT * (st.attend(u)[0] + 1) - 1)
                        elif e[0] == "mask":
                            turn_mask(u)
                        elif e[0] == "turn_m":
                            turn_m(e[1])
                        elif e[0] == "check":
                            check(u)
                        elif e[0] == "turn_o":
                            turn_o(e[1])
                for k in range(KD + 1):
                    project(st.n - 1, k)

        clear(nc, sems)


def feed_forward(nc, w, identf, sign, x2D, out):
    NTA, NGA = B * NT, B * NG
    D2, D4 = D // 2, D // 4
    HN = 6
    with ExitStack() as ctx:
        sb = lambda n, s, d: ctx.enter_context(nc.sbuf_tensor(n, s, d))
        ps = lambda n, s, d: ctx.enter_context(nc.psum_tensor(n, s, d))
        sems = []

        def sem(n):
            sems.append(ctx.enter_context(nc.semaphore(n)))
            return sems[-1]

        x2 = sb("x2", [P, NTA, D], FP32)
        hn = sb("hn", [P, HN, D], FP32)
        stats = sb("fstats", [P, NTA, 6], FP32)
        mv = sb("fmv", [P, NTA, 2], FP32)
        sd = sb("fsd", [P, NTA], FP32)
        rstd = sb("frstd", [P, NTA], FP32)
        eps = sb("feps", [P, 1], FP32)
        hT = sb("hT", [P, KD, B * S], FP32)
        h1 = sb("h1", [P, 2, KD, GW], FP32)
        h2 = sb("h2", [P, 2, GW], FP32)
        h3 = sb("h3", [D4, 2, GW], FP32)
        th = sb("th", [P, 2, GW], FP32)
        tw = sb("tw", [P, 2, 2, GW], FP32)
        w1 = sb("w1", [P, KD, D], FP32)
        w2 = sb("w2", [P, KD, D2], FP32)
        w3 = sb("w3", [P, D4], FP32)
        w4 = sb("w4", [D4, P], FP32)
        g1 = sb("g1", [P, KD, D2], FP32)
        g2 = sb("g2", [P, D4], FP32)
        g3 = sb("g3", [D4, P], FP32)
        g3c = sb("g3c", [D4, 1], FP32)
        w4c = sb("w4c", [D4, 1], FP32)
        b1 = sb("b1", [P, KD], FP32)
        b2 = sb("b2", [P, 1], FP32)
        b3 = sb("b3", [D4, 1], FP32)
        b4 = sb("b4", [P, 1], FP32)
        c1 = sb("c1", [P, 1], FP32)
        c2 = sb("c2", [D4, 1], FP32)
        c3 = sb("c3", [P, 1], FP32)
        ar = sb("ar", [P, 1], FP32)
        half = sb("half", [P, 2], FP32)
        mean = sb("mean", [P, B, KD], FP32)
        gh1 = sb("gh1", [P, B], FP32)
        gh2 = sb("gh2", [D4, B], FP32)
        gt = sb("gt", [P, B], FP32)
        base = sb("base", [P, B], FP32)
        slope = sb("slope", [P, 1], FP32)
        pW = [ps(f"pW{k}", [P, 512], FP32) for k in range(8)]
        spare = (pW[3], pW[5], pW[7])
        x2_in = [sem(f"x2_in{g}") for g in range(NGA)]
        w_in, eps_set, stats_done, mv_done, sd_done, rstd_done = (sem(n) for n in ("fw_in", "feps_set", "fstats_done", "fmv_done", "fsd_done", "frstd_done"))
        hn_done, h_turned, hT_done, half_done, mean_done = (sem(n) for n in ("hn_done", "h_turned", "hT_done", "half_done", "mean_done"))
        gz1, gz2, gz3, ga1, ga2, ga3, coef = (sem(n) for n in ("gz1", "gz2", "gz3", "ga1", "ga2", "ga3", "coef"))
        z1, z2, z3, z4, a1, a2, a3, a4 = (sem(n) for n in ("z1", "z2", "z3", "z4", "a1", "a2", "a3", "a4"))
        c_done, tw_done, h_new, y_turned, y_done, y_out = (sem(n) for n in ("c_done", "tw_done", "h_new", "y_turned", "y_done", "y_out"))
        NC = CYCLES * NGA
        turned_at = {0: range(NG), 2: range(NG, NG + NG // 2), 3: range(NG + NG // 2, NGA)}

        with nc.Block() as block:

            @block.sync
            def _(sp):
                x2v = x2D.rearrange("(t p) d -> p t d", p=P)

                def load_x2(b):
                    for g in range(b * NG, (b + 1) * NG):
                        sp.dma_start(x2[:, g * GT:(g + 1) * GT, :], x2v[:, g * GT:(g + 1) * GT, :]).then_inc(x2_in[g], 16)

                load_x2(0)
                col = lambda a: a.rearrange("(p o) -> p o", o=1)
                kp = lambda a: a.rearrange("(k p) n -> p k n", p=P)
                loads = [(g1[:], kp(w["g1"])), (g2[:], w["g2"]), (g3c[:], w["g3"]), (c1[:], col(w["c1"])),
                         (c2[:], col(w["c2"])), (c3[:], w["c3"].partition_broadcast(P)), (ar[:], w["ar"].partition_broadcast(P)),
                         (b4[:], w["b4"].partition_broadcast(P)), (w1[:], kp(w["w1"])), (w2[:], kp(w["w2"])), (w3[:], w["w3"]),
                         (w4c[:], w["w4"]), (b1[:, 0:1], col(w["b1"][0:P])), (b1[:, 1:2], col(w["b1"][P:D])), (b2[:], col(w["b2"])), (b3[:], col(w["b3"]))]
                for dst, src in loads:
                    sp.dma_start(dst, src).then_inc(w_in, 16)
                for b in range(1, B):
                    load_x2(b)
                ob = out.rearrange("(t p) d -> p t d", p=P)
                for g in range(NGA):
                    sp.wait_ge(y_done, GT * (g + 1))
                    sp.dma_start(ob[:, g * GT:(g + 1) * GT, :], x2[:, g * GT:(g + 1) * GT, :]).then_inc(y_out, 16)
                sp.wait_ge(y_out, 16 * NGA)

            NW = 16

            @block.vector
            def _(dve):
                dve.memset(eps[:], EPS).then_inc(eps_set, 1)

                def spreads(b):
                    tiles = range(b * NT, (b + 1) * NT)
                    for i in tiles:
                        if i % GT == 0:
                            dve.wait_ge(x2_in[i // GT], 16)
                        dve.bn_stats(out=stats[:, i, :], in_=x2[:, i, :]).then_inc(stats_done, 1)
                    for i in tiles:
                        dve.wait_ge(stats_done, i + 1)
                        dve.bn_aggr(out=mv[:, i, :], in_=stats[:, i, :]).then_inc(mv_done, 1)
                    dve.wait_ge(sd_done, b + 1)
                    dve.reciprocal(rstd[:, b * NT:(b + 1) * NT], sd[:, b * NT:(b + 1) * NT]).then_inc(rstd_done, 1)
                    dve.wait_ge(rstd_done, b + 1)

                def normalise(b):
                    for i in range(b * NT, (b + 1) * NT):
                        if i >= HN:
                            dve.wait_ge(h_turned, i - HN + 1)
                        dve.tensor_scalar(hn[:, i % HN, :], x2[:, i, :], mv[:, i, 0:1], rstd[:, i:i + 1], ALU.subtract, ALU.mult).then_inc(hn_done, 1)

                def average(b):
                    dve.wait_ge(hT_done, (b + 1) * NT)
                    dve.tensor_reduce(mean[:, b, :], hT[:, :, b * S:(b + 1) * S], AX.X, ALU.add).then_inc(mean_done, 1)

                spreads(0)
                normalise(0)
                dve.wait_ge(w_in, 16 * NW)
                dve.tensor_scalar(half[:, 0:1], b4[:], 0.5, None, ALU.mult).then_inc(half_done, 1)
                dve.tensor_scalar(half[:, 1:2], c3[:], 0.5, None, ALU.mult).then_inc(half_done, 1)
                dve.tensor_copy(w4[:], w4c[:, 0:1].to_broadcast([D4, P])).then_inc(half_done, 1)
                dve.tensor_copy(g3[:], g3c[:, 0:1].to_broadcast([D4, P])).then_inc(half_done, 1)
                dve.tensor_scalar(slope[:], ar[:], sign[:, 0:1], 0.3, ALU.mult, ALU.mult).then_inc(half_done, 1)
                for b in range(1, B):
                    average(b - 1)
                    spreads(b)
                    normalise(b)
                average(B - 1)
                dve.wait_ge(half_done, 5)

                def coupling(b):
                    dve.wait_ge(ga3, b + 1)
                    dve.tensor_scalar(gt[:, b:b + 1], gt[:, b:b + 1], ar[:, 0:1], 0.7, ALU.mult, ALU.mult).then_inc(coef, 1)
                    dve.wait_ge(coef, 2 * b + 1)
                    dve.tensor_scalar(base[:, b:b + 1], gt[:, b:b + 1], 0.1, sign[:, 0:1], ALU.add, ALU.mult).then_inc(coef, 1)
                    dve.wait_ge(coef, 2 * b + 2)

                def outputs(g):
                    for i in range(g * GT, (g + 1) * GT):
                        dve.wait_ge(y_turned, i + 1)
                        dve.tensor_tensor(x2[:, i, :], spare[i % 3][:, 0:D], x2[:, i, :], ALU.add).then_inc(y_done, 1)

                for n in range(NC):
                    g = n % NGA
                    k = n % 2
                    cols = slice(g * GW, (g + 1) * GW)
                    if n < NGA and n % NG == 0:
                        coupling(n // NG)
                    dve.wait_ge(a4, n + 1)
                    dve.tensor_scalar(th[:, k, :], th[:, k, :], slope[:, 0:1], base[:, g // NG:g // NG + 1], ALU.mult, ALU.add).then_inc(c_done, 1)
                    dve.wait_ge(c_done, n + 1)
                    if n >= NGA:
                        dve.wait_ge(h_new, 2 * (n - NGA + 1))
                    if n >= 2:
                        dve.wait_ge(h_new, 2 * (n - 1))
                    dve.tensor_tensor(tw[:, k, 0, :], th[:, k, :], hT[:, 1, cols], ALU.mult).then_inc(tw_done, 1)
                    dve.tensor_tensor(tw[:, k, 1, :], th[:, k, :], hT[:, 0, cols], ALU.mult).then_inc(tw_done, 1)
                    dve.wait_ge(tw_done, 2 * (n + 1))
                    dve.tensor_tensor(hT[:, 0, cols], hT[:, 0, cols], tw[:, k, 0, :], ALU.add).then_inc(h_new, 1)
                    dve.tensor_tensor(hT[:, 1, cols], hT[:, 1, cols], tw[:, k, 1, :], ALU.subtract).then_inc(h_new, 1)
                    if n > NC - NGA:
                        outputs(g - 1)
                outputs(NGA - 1)

            @block.scalar
            def _(act):
                act.wait_ge(eps_set, 1)

                def deviations(b):
                    act.wait_ge(mv_done, (b + 1) * NT)
                    act.activation(sd[:, b * NT:(b + 1) * NT], mv[:, b * NT:(b + 1) * NT, 1], ACT.Sqrt, bias=eps[:, 0:1]).then_inc(sd_done, 1)

                def take_turned(g):
                    for i in range(g * GT, (g + 1) * GT):
                        act.wait_ge(h_turned, i + 1)
                        act.activation(hT[:, :, i * P:(i + 1) * P], spare[i % 3][:, 0:D].rearrange("p (k q) -> p k q", q=P), ACT.Copy).then_inc(hT_done, 1)

                def global_net(b):
                    act.wait_ge(gz1, b + 1)
                    act.activation(gh1[:, b:b + 1], pW[7][:, 0:1], ACT.Gelu, bias=c1[:, 0:1], scale=1.0 / S).then_inc(ga1, 1)
                    act.wait_ge(gz2, b + 1)
                    act.activation(gh2[:, b:b + 1], pW[7][0:D4, 1:2], ACT.Gelu, bias=c2[:, 0:1]).then_inc(ga2, 1)
                    act.wait_ge(gz3, b + 1)
                    act.activation(gt[:, b:b + 1], pW[7][:, 2:3], ACT.Tanh, bias=half[:, 1:2], scale=0.5).then_inc(ga3, 1)

                for m in range(NC + 3):
                    for g in turned_at.get(m, ()):
                        if g % NG == 0:
                            deviations(g // NG)
                        take_turned(g)
                    if m == 0:
                        act.wait_ge(w_in, 16 * NW)
                        act.wait_ge(half_done, 5)
                    if m < NC:
                        n, k = m, m % 2
                        for q in range(KD):
                            act.wait_ge(z1, 2 * n + q + 1)
                            if n >= 2:
                                act.wait_ge(z2, n - 1)
                            act.activation(h1[:, k, q, :], pW[q][:], ACT.Gelu, bias=b1[:, q:q + 1]).then_inc(a1, 1)
                    if m in (1, NG):
                        global_net(m // NG)
                    if 1 <= m <= NC:
                        n = m - 1
                        k = n % 2
                        act.wait_ge(z2, n + 1)
                        if n >= 2:
                            act.wait_ge(z3, n - 1)
                        act.activation(h2[:, k, :], pW[2][:], ACT.Gelu, bias=b2[:, 0:1]).then_inc(a2, 1)
                    if 2 <= m <= NC + 1:
                        n = m - 2
                        k = n % 2
                        act.wait_ge(z3, n + 1)
                        if n >= 2:
                            act.wait_ge(z4, n - 1)
                        act.activation(h3[:, k, :], pW[4][0:D4, :], ACT.Gelu, bias=b3[:, 0:1]).then_inc(a3, 1)
                    if m >= 3:
                        n = m - 3
                        k = n % 2
                        act.wait_ge(z4, n + 1)
                        if n >= 2:
                            act.wait_ge(tw_done, 2 * (n - 1))
                        act.activation(th[:, k, :], pW[6][:], ACT.Tanh, bias=half[:, 0:1], scale=0.5).then_inc(a4, 1)

            @block.tensor
            def _(pe):
                def turn(g):
                    for i in range(g * GT, (g + 1) * GT):
                        pe.wait_ge(hn_done, i + 1)
                        if i >= 3:
                            pe.wait_ge(hT_done, i - 2)
                        for k in range(KD):
                            mm = pe.transpose(spare[i % 3][:, k * P:(k + 1) * P], hn[:, i % HN, k * P:(k + 1) * P], identf[:])
                        mm.then_inc(h_turned, 1)

                def turn_back(g):
                    pe.wait_ge(h_new, 2 * (NC - NGA + g + 1))
                    for i in range(g * GT, (g + 1) * GT):
                        if i >= 3:
                            pe.wait_ge(y_done, i - 2)
                        for k in range(KD):
                            mm = pe.transpose(spare[i % 3][:, k * P:(k + 1) * P], hT[:, k, i * P:(i + 1) * P], identf[:])
                        mm.then_inc(y_turned, 1)

                def global_net(b):
                    pe.wait_ge(mean_done, b + 1)
                    pe.wait_ge(hT_done, (b + 1) * NT)
                    for k in range(KD):
                        mm = pe.matmul(pW[7][:, 0:1], g1[:, k, :], mean[:, b, k:k + 1], start=(k == 0), stop=(k == KD - 1))
                    mm.then_inc(gz1, 1)
                    pe.wait_ge(ga1, b + 1)
                    pe.matmul(pW[7][0:D4, 1:2], g2[:], gh1[:, b:b + 1], start=True, stop=True).then_inc(gz2, 1)
                    pe.wait_ge(ga2, b + 1)
                    pe.matmul(pW[7][:, 2:3], g3[:], gh2[:, b:b + 1], start=True, stop=True).then_inc(gz3, 1)

                for m in range(NC + 5):
                    for g in turned_at.get(m, ()):
                        turn(g)
                    if m == 0:
                        pe.wait_ge(w_in, 16 * NW)
                        pe.wait_ge(half_done, 5)
                    if m < NC:
                        n = m
                        cols = slice((n % NGA) * GW, (n % NGA + 1) * GW)
                        if n >= NGA:
                            pe.wait_ge(h_new, 2 * (n - NGA + 1))
                        else:
                            pe.wait_ge(hT_done, GT * (n + 1))
                        for q in range(KD):
                            if n >= 1:
                                pe.wait_ge(a1, 2 * (n - 1) + q + 1)
                            for k in range(KD):
                                mm = pe.matmul(pW[q][:], w1[:, k, q * P:(q + 1) * P], hT[:, k, cols], start=(k == 0), stop=(k == KD - 1))
                            mm.then_inc(z1, 1)
                    if m in (1, NG):
                        global_net(m // NG)
                    if 1 <= m <= NC:
                        n = m - 1
                        pe.wait_ge(a1, 2 * (n + 1))
                        if n >= 1:
                            pe.wait_ge(a2, n)
                        for k in range(KD):
                            mm = pe.matmul(pW[2][:], w2[:, k, :], h1[:, n % 2, k, :], start=(k == 0), stop=(k == KD - 1))
                        mm.then_inc(z2, 1)
                    if 2 <= m <= NC + 1:
                        n = m - 2
                        pe.wait_ge(a2, n + 1)
                        if n >= 1:
                            pe.wait_ge(a3, n)
                        pe.matmul(pW[4][0:D4, :], w3[:], h2[:, n % 2, :], start=True, stop=True).then_inc(z3, 1)
                    if 3 <= m <= NC + 2:
                        n = m - 3
                        pe.wait_ge(a3, n + 1)
                        if n >= 1:
                            pe.wait_ge(a4, n)
                        pe.matmul(pW[6][:], w4[:], h3[:, n % 2, :], start=True, stop=True).then_inc(z4, 1)
                    if m >= NC - NGA + 5:
                        turn_back(m - 5 - (NC - NGA))

        clear(nc, sems)


def build(nc, x, w, tabs, ranks, out):
    with ExitStack() as ctx:
        sb = lambda n, s, d: ctx.enter_context(nc.sbuf_tensor(n, s, d))
        identf = sb("identf", [P, P], FP32)
        sign = sb("sign", [P, 1], FP32)
        x2D = nc.dram_tensor("x2_scratch", (B * S, D), FP32, kind="Internal").ap()
        attend_all(nc, x, w, tabs, ranks, x2D, identf, sign)
        feed_forward(nc, w, identf, sign, x2D, out)


def attend_all(nc, x, w, tabs, ranks, x2D, identf, sign):
    with ExitStack() as ctx:
        sb = lambda n, s, d: ctx.enter_context(nc.sbuf_tensor(n, s, d))
        K99 = sb("K99", [KM, H, S], BF16)
        V = sb("V", [P, NT, VP], FP32)
        kiT = sb("kiT", [P, S], FP32)
        wi = sb("wi", [P, NT, HI], FP32)
        identb = sb("identb", [P, P], BF16)
        hide = sb("hide", [P, P], BF16)
        woT = sb("woT", [P, KD, D], FP32)
        tables = sb("tables", [P, P + NT + RANKS + NT], FP32)
        qkD = [nc.dram_tensor(f"qk{c}_parts", (H * PARTS * DK, S), BF16, kind="Internal").ap() for c in range(2)]
        qiD = nc.dram_tensor("qi_scratch", (P, 2, S), FP32, kind="Internal").ap()
        zeroed = ctx.enter_context(nc.semaphore("zeroed"))
        const_done = ctx.enter_context(nc.semaphore("const_done"))
        ones_set = ctx.enter_context(nc.semaphore("ones_set"))
        wo_in = ctx.enter_context(nc.semaphore("wo_in"))
        with nc.sbuf_tensor("ones", [PARTS, S], BF16) as ones, nc.Block() as block:

            @block.sync
            def _(sp):
                sp.dma_start(woT[:], w["oT"].rearrange("(k p) n -> p k n", p=P)).then_inc(wo_in, 16)
                sp.dma_start(tables[:], ranks).then_inc(wo_in, 16)
                sp.wait_ge(ones_set, 2)
                for h in range(H):
                    sp.dma_start(K99[KR:KM, h, :], ones[:]).then_inc(wo_in, 16)
                sp.wait_ge(wo_in, 16 * (2 + H))

            @block.gpsimd
            def _(pool):
                pool.memset(identf[:], 0.0).then_inc(zeroed, 1)
                pool.memset(identb[:], 0.0).then_inc(zeroed, 1)
                pool.memset(sign[:], 1.0).then_inc(zeroed, 1)
                pool.memset(hide[:], 0.0).then_inc(zeroed, 1)
                pool.wait_ge(zeroed, 4)
                for m, one in ((identf, 1.0), (identb, 1.0), (hide, HIDE)):
                    pool.affine_select(out=m[:], in_=m[:], compare_op=ALU.not_equal, fill=one, base=0,
                                       pattern=[[-1, P]], channel_multiplier=1).then_inc(const_done, 1)
                pool.affine_select(out=sign[:], in_=sign[:], compare_op=ALU.is_gt, fill=-1.0, base=D // 4,
                                   pattern=[[0, 1]], channel_multiplier=-1).then_inc(const_done, 1)
                pool.wait_ge(const_done, 4)

            @block.vector
            def _(dve):
                dve.memset(V[:], 1.0).then_inc(ones_set, 1)
                dve.memset(ones[:], 1.0).then_inc(ones_set, 1)
                dve.wait_ge(ones_set, 2)

        clear(nc, [zeroed, const_done, ones_set, wo_in])
        keep = (K99, V, kiT, wi)
        with nc.Fori(0, B) as b:
            prepare(nc, b, x, w, tabs, (identf, identb), keep, (qkD, qiD))
            attention(nc, b, x, (identf, identb, hide, woT, tables), keep, (qkD, qiD, x2D))


_TURNED = {'L0_attn_w_qkv': 'qkvT', 'L0_attn_w_o': 'oT', 'L0_attn_w_qi': 'qiT', 'L0_attn_w_ki': 'kiT', 'L0_attn_w_wi': 'wiT'}
_PLAIN = {'L0_ffn_cn_w1': 'w1', 'L0_ffn_cn_b1': 'b1', 'L0_ffn_cn_w2': 'w2', 'L0_ffn_cn_b2': 'b2', 'L0_ffn_cn_w3': 'w3',
          'L0_ffn_cn_b3': 'b3', 'L0_ffn_cn_w4': 'w4', 'L0_ffn_cn_b4': 'b4', 'L0_ffn_gc_w1': 'g1', 'L0_ffn_gc_b1': 'c1',
          'L0_ffn_gc_w2': 'g2', 'L0_ffn_gc_b2': 'c2', 'L0_ffn_gc_w3': 'g3', 'L0_ffn_gc_b3': 'c3', 'L0_ffn_adaptive_range': 'ar'}


def kernel(**inputs):
    import numpy as _np
    import concourse.bacc as _bacc
    from concourse import mybir as _mybir
    from concourse.bass_utils import run_bass_kernel_spmd as _run

    nc = _bacc.Bacc("TRN2", target_bir_lowering=False, num_devices=1)
    arrays = {}

    def tensor(name, a):
        a = _np.ascontiguousarray(a)
        arrays[name] = a
        return nc.dram_tensor(name, a.shape, _mybir.dt.from_np(a.dtype), kind="ExternalInput").ap()

    xs = _np.asarray(inputs['L0_attn_x'])
    x = tensor("x_dram", xs.reshape(B * S, D))
    w = {k: tensor(f"{k}_dram", _np.asarray(inputs[n]).T) for n, k in _TURNED.items()}
    w.update({k: tensor(f"{k}_dram", _np.asarray(inputs[n])) for n, k in _PLAIN.items()})
    tabs = [tensor(f"table{k}_dram", t) for k, t in enumerate(rope_tables())]
    out = nc.dram_tensor("out_dram", (B * S, D), _mybir.dt.float32, kind="ExternalOutput").ap()
    ranks = tensor("ranks_dram", rank_tables())
    build(nc, x, w, tabs, ranks, out)
    r = _run(nc, [arrays], core_ids=[0])
    return r.results[0]["out_dram"].reshape(xs.shape)
```
